# Optimizing a Trainium2 kernel written in Bass

```python
import numpy as np
import jax
import jax.numpy as jnp

def _softmax(x, axis=-1):
    return jax.nn.softmax(x, axis=axis)

def _gelu(x):
    return jax.nn.gelu(x, approximate=True)

def _silu(x):
    return jax.nn.silu(x)

def _sigmoid(x):
    return jax.nn.sigmoid(x)

def _layernorm(x, axis=-1, eps=1e-05):
    m = jnp.mean(x, axis=axis, keepdims=True)
    v = jnp.var(x, axis=axis, keepdims=True)
    return (x - m) / jnp.sqrt(v + eps)

def _scatter_add(tgt, idx, src, axis=0):
    return tgt.at[idx].add(src)

def _segment_sum(src, seg, n):
    return jax.ops.segment_sum(src, seg, n)
kernel_name = 'mk_hybrid_d1_jaxref_r8_5fe3d6'

def setup_inputs(seed: int=0):
    np.random.seed(seed)
    _w = jnp.asarray

    def _L0_attn_a_setup():
        import jax, jax.numpy as jnp
        import numpy as np
        import math
        DIM = 256
        N_HEADS = 16
        N_KV_HEADS = 8
        HEAD_DIM = DIM // N_HEADS
        N_REP = N_HEADS // N_KV_HEADS
        BLOCK = 128
        TOPK = 8
        NEG_INF = -10000.0
        SEQ = 512
        BS = 1

        def _rope_tables(seq_len, head_dim, base=10000.0):
            inv_freq = 1.0 / base ** (jnp.arange(0, head_dim, 2, dtype=jnp.float32) / head_dim)
            ang = jnp.arange(seq_len, dtype=jnp.float32)[:, None] * inv_freq[None, :]
            return (jnp.cos(ang), jnp.sin(ang))

        def _apply_rope(t, cos, sin):
            t1 = t[..., 0::2]
            t2 = t[..., 1::2]
            c = cos[None, :, None, :]
            s = sin[None, :, None, :]
            out_even = t1 * c - t2 * s
            out_odd = t1 * s + t2 * c
            out = jnp.stack([out_even, out_odd], axis=-1)
            return out.reshape(t.shape)
        key = jax.random.key(seed)
        ks = jax.random.split(key, 5)
        scale = 1.0 / math.sqrt(DIM)
        x = jax.random.normal(ks[0], (BS, SEQ, DIM), dtype=jnp.float32)
        wq = jax.random.normal(ks[1], (DIM, N_HEADS * HEAD_DIM), dtype=jnp.float32) * scale
        wk = jax.random.normal(ks[2], (DIM, N_KV_HEADS * HEAD_DIM), dtype=jnp.float32) * scale
        wv = jax.random.normal(ks[3], (DIM, N_KV_HEADS * HEAD_DIM), dtype=jnp.float32) * scale
        wo = jax.random.normal(ks[4], (DIM, DIM), dtype=jnp.float32) * scale
        return {'x': x, 'wq': wq, 'wk': wk, 'wv': wv, 'wo': wo}
    _L0_attn_a_in = _L0_attn_a_setup()

    def _L0_attn_b_setup():
        import jax, jax.numpy as jnp
        import numpy as np
        D_MODEL = 256
        D_INNER = 256
        D_XB = 128
        D_STATE = 128
        NHEADS = D_INNER // D_STATE
        NKV = D_XB // D_STATE
        NREP = NHEADS // NKV
        D_CONV = 4
        CHUNK = 128
        INTER = 1024
        EPS = 1e-05
        BATCH, SEQ = (2, 256)

        def _rmsnorm(x, w, eps=EPS):
            v = jnp.mean(x * x, axis=-1, keepdims=True)
            return x * jax.lax.rsqrt(v + eps) * w

        def _segsum(x):
            T = x.shape[-1]
            cs = jnp.cumsum(x, axis=-1)
            seg = cs[..., :, None] - cs[..., None, :]
            mask = jnp.tril(jnp.ones((T, T), bool))
            return jnp.where(mask, seg, -jnp.inf)

        def _ssd(X, dA, Bm, Cm, chunk):
            b, l, h, p = X.shape
            c = l // chunk
            X = X.reshape(b, c, chunk, h, p)
            Bm = Bm.reshape(b, c, chunk, h, -1)
            Cm = Cm.reshape(b, c, chunk, h, -1)
            dA = dA.reshape(b, c, chunk, h).transpose(0, 3, 1, 2)
            dA_cs = jnp.cumsum(dA, axis=-1)
            L = jnp.exp(_segsum(dA))
            Y_diag = jnp.einsum('bclhn,bcshn,bhcls,bcshp->bclhp', Cm, Bm, L, X)
            decay_states = jnp.exp(dA_cs[..., -1:] - dA_cs)
            states = jnp.einsum('bcshn,bhcs,bcshp->bchpn', Bm, decay_states, X)
            states = jnp.concatenate([jnp.zeros_like(states[:, :1]), states], axis=1)
            chunk_decay = jnp.exp(_segsum(jnp.pad(dA_cs[..., -1], ((0, 0), (0, 0), (1, 0)))))
            new_states = jnp.einsum('bhzc,bchpn->bzhpn', chunk_decay, states)
            prev_states = new_states[:, :-1]
            Y_off = jnp.einsum('bclhn,bchpn,bhcl->bclhp', Cm, prev_states, jnp.exp(dA_cs))
            return (Y_diag + Y_off).reshape(b, l, h, p)
        key = jax.random.key(seed)
        ks = jax.random.split(key, 8)
        conv_dim = 2 * D_XB + D_INNER
        proj_dim = 2 * D_INNER + 2 * D_XB + NHEADS
        g = lambda k, shape, sc: jax.random.normal(k, shape, jnp.float32) * sc
        return {'hidden_states': jax.random.normal(ks[0], (BATCH, SEQ, D_MODEL), jnp.float32), 'ln1_w': jnp.ones((D_MODEL,), jnp.float32), 'W_in': g(ks[1], (D_MODEL, proj_dim), 0.02), 'conv_w': g(ks[2], (D_CONV, conv_dim), 0.2), 'conv_b': jnp.zeros((conv_dim,), jnp.float32), 'dt_bias': jnp.log(jnp.expm1(jnp.linspace(0.001, 0.1, NHEADS))).astype(jnp.float32), 'A_log': jnp.log(jnp.linspace(1.0, 16.0, NHEADS)).astype(jnp.float32), 'D': jnp.ones((NHEADS,), jnp.float32), 'norm_w': jnp.ones((D_INNER,), jnp.float32), 'W_out': g(ks[3], (D_INNER, D_MODEL), 0.02), 'ln2_w': jnp.ones((D_MODEL,), jnp.float32), 'w1': g(ks[4], (D_MODEL, INTER), 0.02), 'w3': g(ks[5], (D_MODEL, INTER), 0.02), 'w2': g(ks[6], (INTER, D_MODEL), 0.02)}
    _L0_attn_b_in = _L0_attn_b_setup()

    def _L0_ffn_setup():
        import jax, jax.numpy as jnp
        import numpy as np
        B, S, D = (4, 256, 256)
        E = 8
        H = 352
        CAP_F = 1.0

        def _moe(x, Wg, W1, W3, W2, sw1, sw3, sw2):
            b, sl, d = x.shape
            T = b * sl
            C = int(CAP_F * T / E)
            xt = x.reshape(T, d)
            probs = jax.nn.softmax(xt @ Wg, axis=-1)
            eidx = jnp.argmax(probs, axis=-1)
            gate = jnp.take_along_axis(probs, eidx[:, None], 1)[:, 0]
            oh = jax.nn.one_hot(eidx, E, dtype=jnp.int32)
            pos = (jnp.cumsum(oh, axis=0) * oh).sum(-1) - 1
            keep = pos < C
            flat = jnp.where(keep, eidx * C + pos, E * C)
            xd = jnp.zeros((E * C, d), x.dtype).at[flat].set(xt, mode='drop')
            xd = xd.reshape(E, C, d)
            h = jax.nn.silu(jnp.einsum('ecd,edh->ech', xd, W1)) * jnp.einsum('ecd,edh->ech', xd, W3)
            oe = jnp.einsum('ech,ehd->ecd', h, W2).reshape(E * C, d)
            out = jnp.take(oe, jnp.minimum(flat, E * C - 1), axis=0)
            out = out * (gate * keep.astype(x.dtype))[:, None]
            shared = jax.nn.silu(xt @ sw1) * (xt @ sw3) @ sw2
            return (out + shared).reshape(b, sl, d)
        key = jax.random.key(seed)
        ks = jax.random.split(key, 8)
        s = lambda fan: 1.0 / np.sqrt(fan)
        return {'x': jax.random.normal(ks[0], (B, S, D), jnp.float32), 'Wg': jax.random.normal(ks[1], (D, E), jnp.float32) * s(D), 'W1': jax.random.normal(ks[2], (E, D, H), jnp.float32) * s(D), 'W3': jax.random.normal(ks[3], (E, D, H), jnp.float32) * s(D), 'W2': jax.random.normal(ks[4], (E, H, D), jnp.float32) * s(H), 'sw1': jax.random.normal(ks[5], (D, H), jnp.float32) * s(D), 'sw3': jax.random.normal(ks[6], (D, H), jnp.float32) * s(D), 'sw2': jax.random.normal(ks[7], (H, D), jnp.float32) * s(H)}
    _L0_ffn_in = _L0_ffn_setup()
    _d = {'L0_attn_a_x': _L0_attn_a_in['x'], 'L0_attn_a_wq': _L0_attn_a_in['wq'], 'L0_attn_a_wk': _L0_attn_a_in['wk'], 'L0_attn_a_wv': _L0_attn_a_in['wv'], 'L0_attn_a_wo': _L0_attn_a_in['wo'], 'L0_attn_b_ln1_w': _L0_attn_b_in['ln1_w'], 'L0_attn_b_W_in': _L0_attn_b_in['W_in'], 'L0_attn_b_conv_w': _L0_attn_b_in['conv_w'], 'L0_attn_b_conv_b': _L0_attn_b_in['conv_b'], 'L0_attn_b_dt_bias': _L0_attn_b_in['dt_bias'], 'L0_attn_b_A_log': _L0_attn_b_in['A_log'], 'L0_attn_b_D': _L0_attn_b_in['D'], 'L0_attn_b_norm_w': _L0_attn_b_in['norm_w'], 'L0_attn_b_W_out': _L0_attn_b_in['W_out'], 'L0_attn_b_ln2_w': _L0_attn_b_in['ln2_w'], 'L0_attn_b_w1': _L0_attn_b_in['w1'], 'L0_attn_b_w3': _L0_attn_b_in['w3'], 'L0_attn_b_w2': _L0_attn_b_in['w2'], 'L0_ffn_Wg': _L0_ffn_in['Wg'], 'L0_ffn_W1': _L0_ffn_in['W1'], 'L0_ffn_W3': _L0_ffn_in['W3'], 'L0_ffn_W2': _L0_ffn_in['W2'], 'L0_ffn_sw1': _L0_ffn_in['sw1'], 'L0_ffn_sw3': _L0_ffn_in['sw3'], 'L0_ffn_sw2': _L0_ffn_in['sw2']}
    _x0 = _d['L0_attn_a_x']
    _d['L0_attn_a_x'] = jax.random.normal(jax.random.fold_in(jax.random.key(seed), 1), (4, 512, 256), dtype=_x0.dtype)
    del _x0
    return _d

def reference(L0_attn_a_x, L0_attn_a_wq, L0_attn_a_wk, L0_attn_a_wv, L0_attn_a_wo, L0_attn_b_ln1_w, L0_attn_b_W_in, L0_attn_b_conv_w, L0_attn_b_conv_b, L0_attn_b_dt_bias, L0_attn_b_A_log, L0_attn_b_D, L0_attn_b_norm_w, L0_attn_b_W_out, L0_attn_b_ln2_w, L0_attn_b_w1, L0_attn_b_w3, L0_attn_b_w2, L0_ffn_Wg, L0_ffn_W1, L0_ffn_W3, L0_ffn_W2, L0_ffn_sw1, L0_ffn_sw3, L0_ffn_sw2):

    def _L0_attn_a_ref(x, wq, wk, wv, wo):
        import jax, jax.numpy as jnp
        import numpy as np
        import math
        DIM = 256
        N_HEADS = 16
        N_KV_HEADS = 8
        HEAD_DIM = DIM // N_HEADS
        N_REP = N_HEADS // N_KV_HEADS
        BLOCK = 128
        TOPK = 8
        NEG_INF = -10000.0
        SEQ = 512
        BS = 1

        def _rope_tables(seq_len, head_dim, base=10000.0):
            inv_freq = 1.0 / base ** (jnp.arange(0, head_dim, 2, dtype=jnp.float32) / head_dim)
            ang = jnp.arange(seq_len, dtype=jnp.float32)[:, None] * inv_freq[None, :]
            return (jnp.cos(ang), jnp.sin(ang))

        def _apply_rope(t, cos, sin):
            t1 = t[..., 0::2]
            t2 = t[..., 1::2]
            c = cos[None, :, None, :]
            s = sin[None, :, None, :]
            out_even = t1 * c - t2 * s
            out_odd = t1 * s + t2 * c
            out = jnp.stack([out_even, out_odd], axis=-1)
            return out.reshape(t.shape)
        bs, S, _ = x.shape
        inv_sqrt_d = 1.0 / math.sqrt(HEAD_DIM)
        q = (x @ wq).reshape(bs, S, N_HEADS, HEAD_DIM)
        k = (x @ wk).reshape(bs, S, N_KV_HEADS, HEAD_DIM)
        v = (x @ wv).reshape(bs, S, N_KV_HEADS, HEAD_DIM)
        cos, sin = _rope_tables(S, HEAD_DIM)
        q = _apply_rope(q, cos, sin)
        k = _apply_rope(k, cos, sin)
        q = jnp.transpose(q, (0, 2, 1, 3))
        k = jnp.transpose(k, (0, 2, 1, 3))
        v = jnp.transpose(v, (0, 2, 1, 3))
        k_e = jnp.repeat(k, N_REP, axis=1)
        v_e = jnp.repeat(v, N_REP, axis=1)
        num_blocks = S // BLOCK
        k_blocks = k_e.reshape(bs, N_HEADS, num_blocks, BLOCK, HEAD_DIM)
        block_means = k_blocks.mean(axis=3)
        gating = jnp.einsum('bhsd,bhnd->bhsn', q, block_means) * inv_sqrt_d
        q_block_idx = jnp.arange(S) // BLOCK
        future_block = q_block_idx[:, None] < jnp.arange(num_blocks)[None, :]
        gating = jnp.where(future_block[None, None], NEG_INF, gating)
        curr_k = min(TOPK, num_blocks)
        _, sel_idx = jax.lax.top_k(gating, curr_k)
        selected = jnp.sum(jax.nn.one_hot(sel_idx, num_blocks, dtype=jnp.float32), axis=-2) > 0
        token_keep = jnp.repeat(selected, BLOCK, axis=-1)[..., :S]
        token_mask = jnp.where(token_keep, 0.0, NEG_INF)
        scores = jnp.einsum('bhsd,bhtd->bhst', q, k_e) * inv_sqrt_d
        causal = jnp.triu(jnp.ones((S, S), dtype=jnp.float32), k=1)
        final_mask = jnp.maximum(token_mask, causal[None, None] * NEG_INF)
        scores = scores + final_mask
        probs = jax.nn.softmax(scores.astype(jnp.float32), axis=-1).astype(scores.dtype)
        out = jnp.einsum('bhst,bhtd->bhsd', probs, v_e)
        out = jnp.transpose(out, (0, 2, 1, 3)).reshape(bs, S, N_HEADS * HEAD_DIM)
        return out @ wo

    def _L0_attn_b_ref(hidden_states, ln1_w, W_in, conv_w, conv_b, dt_bias, A_log, D, norm_w, W_out, ln2_w, w1, w3, w2):
        import jax, jax.numpy as jnp
        import numpy as np
        D_MODEL = 256
        D_INNER = 256
        D_XB = 128
        D_STATE = 128
        NHEADS = D_INNER // D_STATE
        NKV = D_XB // D_STATE
        NREP = NHEADS // NKV
        D_CONV = 4
        CHUNK = 128
        INTER = 1024
        EPS = 1e-05
        BATCH, SEQ = (2, 256)

        def _rmsnorm(x, w, eps=EPS):
            v = jnp.mean(x * x, axis=-1, keepdims=True)
            return x * jax.lax.rsqrt(v + eps) * w

        def _segsum(x):
            T = x.shape[-1]
            cs = jnp.cumsum(x, axis=-1)
            seg = cs[..., :, None] - cs[..., None, :]
            mask = jnp.tril(jnp.ones((T, T), bool))
            return jnp.where(mask, seg, -jnp.inf)

        def _ssd(X, dA, Bm, Cm, chunk):
            b, l, h, p = X.shape
            c = l // chunk
            X = X.reshape(b, c, chunk, h, p)
            Bm = Bm.reshape(b, c, chunk, h, -1)
            Cm = Cm.reshape(b, c, chunk, h, -1)
            dA = dA.reshape(b, c, chunk, h).transpose(0, 3, 1, 2)
            dA_cs = jnp.cumsum(dA, axis=-1)
            L = jnp.exp(_segsum(dA))
            Y_diag = jnp.einsum('bclhn,bcshn,bhcls,bcshp->bclhp', Cm, Bm, L, X)
            decay_states = jnp.exp(dA_cs[..., -1:] - dA_cs)
            states = jnp.einsum('bcshn,bhcs,bcshp->bchpn', Bm, decay_states, X)
            states = jnp.concatenate([jnp.zeros_like(states[:, :1]), states], axis=1)
            chunk_decay = jnp.exp(_segsum(jnp.pad(dA_cs[..., -1], ((0, 0), (0, 0), (1, 0)))))
            new_states = jnp.einsum('bhzc,bchpn->bzhpn', chunk_decay, states)
            prev_states = new_states[:, :-1]
            Y_off = jnp.einsum('bclhn,bchpn,bhcl->bclhp', Cm, prev_states, jnp.exp(dA_cs))
            return (Y_diag + Y_off).reshape(b, l, h, p)
        b, l, _ = hidden_states.shape
        res = hidden_states
        h = _rmsnorm(hidden_states, ln1_w)
        zxbcdt = h @ W_in
        splits = np.cumsum([D_INNER, D_XB, D_XB, D_INNER]).tolist()
        z, xv, Bv, Cv, dt = jnp.split(zxbcdt, splits, axis=-1)
        xBC = jnp.concatenate([xv, Bv, Cv], axis=-1)
        xp = jnp.pad(xBC, ((0, 0), (D_CONV - 1, 0), (0, 0)))
        conv = sum((xp[:, k:k + l, :] * conv_w[k] for k in range(D_CONV))) + conv_b
        xBC = jax.nn.silu(conv)
        xv, Bv, Cv = jnp.split(xBC, [D_XB, 2 * D_XB], axis=-1)
        xh = jnp.repeat(xv.reshape(b, l, NKV, D_STATE), NREP, axis=2)
        Bh = jnp.repeat(Bv.reshape(b, l, NKV, D_STATE), NREP, axis=2)
        Ch = Cv.reshape(b, l, NHEADS, D_STATE)
        dt = jax.nn.softplus(dt + dt_bias)
        a = -jnp.exp(A_log)
        dA = dt * a
        X = xh * dt[..., None]
        y = _ssd(X, dA, Bh, Ch, CHUNK)
        y = y + D[None, None, :, None] * xh
        y = y.reshape(b, l, D_INNER)
        y = _rmsnorm(y * jax.nn.silu(z), norm_w)
        h = y @ W_out
        h = res + h
        res2 = h
        h = _rmsnorm(h, ln2_w)
        h = jax.nn.silu(h @ w1) * (h @ w3) @ w2
        return res2 + h

    def _L0_ffn_ref(x, Wg, W1, W3, W2, sw1, sw3, sw2):
        import jax, jax.numpy as jnp
        import numpy as np
        B, S, D = (4, 256, 256)
        E = 8
        H = 352
        CAP_F = 1.0

        def _moe(x, Wg, W1, W3, W2, sw1, sw3, sw2):
            b, sl, d = x.shape
            T = b * sl
            C = int(CAP_F * T / E)
            xt = x.reshape(T, d)
            probs = jax.nn.softmax(xt @ Wg, axis=-1)
            eidx = jnp.argmax(probs, axis=-1)
            gate = jnp.take_along_axis(probs, eidx[:, None], 1)[:, 0]
            oh = jax.nn.one_hot(eidx, E, dtype=jnp.int32)
            pos = (jnp.cumsum(oh, axis=0) * oh).sum(-1) - 1
            keep = pos < C
            flat = jnp.where(keep, eidx * C + pos, E * C)
            xd = jnp.zeros((E * C, d), x.dtype).at[flat].set(xt, mode='drop')
            xd = xd.reshape(E, C, d)
            h = jax.nn.silu(jnp.einsum('ecd,edh->ech', xd, W1)) * jnp.einsum('ecd,edh->ech', xd, W3)
            oe = jnp.einsum('ech,ehd->ecd', h, W2).reshape(E * C, d)
            out = jnp.take(oe, jnp.minimum(flat, E * C - 1), axis=0)
            out = out * (gate * keep.astype(x.dtype))[:, None]
            shared = jax.nn.silu(xt @ sw1) * (xt @ sw3) @ sw2
            return (out + shared).reshape(b, sl, d)
        return _moe(x, Wg, W1, W3, W2, sw1, sw3, sw2)
    x = L0_attn_a_x
    x = x + _L0_attn_a_ref(_layernorm(x, axis=-1), L0_attn_a_wq, L0_attn_a_wk, L0_attn_a_wv, L0_attn_a_wo)
    x = x + _L0_ffn_ref(_layernorm(x, axis=-1), L0_ffn_Wg, L0_ffn_W1, L0_ffn_W3, L0_ffn_W2, L0_ffn_sw1, L0_ffn_sw3, L0_ffn_sw2)
    x = x + _L0_attn_b_ref(_layernorm(x, axis=-1), L0_attn_b_ln1_w, L0_attn_b_W_in, L0_attn_b_conv_w, L0_attn_b_conv_b, L0_attn_b_dt_bias, L0_attn_b_A_log, L0_attn_b_D, L0_attn_b_norm_w, L0_attn_b_W_out, L0_attn_b_ln2_w, L0_attn_b_w1, L0_attn_b_w3, L0_attn_b_w2)
    x = x + _L0_ffn_ref(_layernorm(x, axis=-1), L0_ffn_Wg, L0_ffn_W1, L0_ffn_W3, L0_ffn_W2, L0_ffn_sw1, L0_ffn_sw3, L0_ffn_sw2)
    return x

_drawn_inputs = setup_inputs


def setup_inputs(seed=0):
    import zlib

    import numpy as np

    out = dict(_drawn_inputs(seed))
    spreads = {'L0_attn_b_ln1_w': (1.0, 0.2),
     'L0_attn_b_conv_b': (0.0, 0.1),
     'L0_attn_b_D': (1.0, 0.6),
     'L0_attn_b_norm_w': (1.0, 0.2),
     'L0_attn_b_ln2_w': (1.0, 0.6)}
    factors = {'L0_attn_b_dt_bias': 8.0,
     'L0_attn_b_A_log': 8.0,
     'L0_attn_b_w1': 3.159,
     'L0_attn_b_w3': 3.029,
     'L0_attn_b_w2': 3.043}
    for name, (base, spread) in spreads.items():
        noise = np.random.default_rng([zlib.crc32(name.encode()), seed]).standard_normal(out[name].shape)
        drawn = base * np.exp(spread * noise) if base else spread * noise
        out[name] = jnp.asarray(drawn.astype(out[name].dtype))
    for name, factor in factors.items():
        out[name] = (out[name] * factor).astype(out[name].dtype)
    return out
```

```python
from contextlib import ExitStack

import numpy as np

import concourse.bass as bass
from concourse import mybir

F32 = mybir.dt.float32
F32R = mybir.dt.float32r
U32 = mybir.dt.uint32
ALU = mybir.AluOpType
ACT = mybir.ActivationFunctionType
AX_X = mybir.AxisListType.X

P = 128
B, S, D = 4, 512, 256
KD = D // P
TB = S // P
TILES = B * TB
NH, NKV, HD = 16, 8, 16
QC, KC = NH * HD, NKV * HD
SLOTS = 4
PACKS = NH // 2
E, H, C = 8, 352, 256
HT = [P, P, H - 2 * P]
U = C // P
UNITS = TILES // U
XB, DI, INTER = 128, 256, 1024
PROJ = 2 * DI + 2 * XB + 2
IT = INTER // P
EPS = 1e-5


class Ring:

    def __init__(self, size, owners, steps=None):
        self.size, self.owners, self.steps = size, owners, steps or {}
        self.total = {o: owners.count(o) * self.steps.get(o, 1) for o in set(owners)}

    def count(self, use, owner):
        return self.owners[:use + 1].count(owner) * self.steps.get(owner, 1)

    def wait_free(self, eng, sems, it, use):
        last = use - self.size
        if last >= 0:
            o = self.owners[last]
            eng.wait_ge(sems[o], self.total[o] * it + self.count(last, o))
        else:
            o = self.owners[last]
            eng.wait_ge(sems[o], self.total[o] * it)


def product(pe, out, a, b, first, last):
    pe.matmul(out, a[0], b[0], start=first, stop=False)
    pe.matmul(out, a[0], b[1], start=False, stop=False)
    return pe.matmul(out, a[1], b[0], start=False, stop=last)


class Memory:

    def __init__(self, nc, ctx, stage, banks=None):
        self.nc, self.ctx, self.stage, self.banks, self.used = nc, ctx, stage, banks, 0
        self.sems = []

    def sb(self, name, shape, dt=F32):
        return self.ctx.enter_context(self.nc.sbuf_tensor(f"{self.stage}_{name}", shape, dt))

    def pair(self, name, shape):
        return self.sb(name + "_hi", shape, F32R), self.sb(name + "_lo", shape, F32R)

    def psum(self, shape):
        n = int(np.prod(shape[1:])) // S
        v = self.banks[:, self.used:self.used + n, :]
        self.used += n
        assert self.used <= 8
        if len(shape) == 4:
            return v.rearrange("p b n -> p (b n)").rearrange("p (x y z) -> p x y z", x=shape[1], y=shape[2])
        return v if len(shape) == 3 else v[:, 0, :]

    def sem(self, name, keep=False):
        h = self.nc.alloc_semaphore(f"{self.stage}_{name}")
        if not keep:
            self.sems.append(h)
        return h

    def close(self):
        self.nc.clear_and_free_semaphores(self.sems)
        self.nc.all_engine_barrier()


class RowStats:

    def __init__(self, m, name, n):
        self.n = n
        self.stats = m.sb(name + "_stats", [P, n, 6])
        self.tmp = m.sb(name + "_tmp", [P, 5, n])
        self.mean = m.sb(name + "_mean", [P, n])
        self.ve = m.sb(name + "_ve", [P, n])
        self.done = m.sem(name + "_done")
        self.steps = n + 7

    def run(self, dve, it, rows):
        n, s, done, base = self.n, self.stats, self.done, self.steps * it
        tot, dif, m2, q, m2e = (self.tmp[:, i, :] for i in range(5))
        for t in range(n):
            dve.bn_stats(s[:, t, :], rows(t)).then_inc(done, 1)
        dve.wait_ge(done, base + n)
        dve.tensor_tensor(tot, s[:, :, 1], s[:, :, 4], ALU.add).then_inc(done, 1)
        dve.tensor_tensor(dif, s[:, :, 1], s[:, :, 4], ALU.subtract).then_inc(done, 1)
        dve.tensor_tensor(m2, s[:, :, 2], s[:, :, 5], ALU.add).then_inc(done, 1)
        dve.wait_ge(done, base + n + 3)
        dve.tensor_scalar(self.mean[:, :], tot, 0.5, None, ALU.mult).then_inc(done, 1)
        dve.scalar_tensor_tensor(q, dif, 0.25, dif, ALU.mult, ALU.mult).then_inc(done, 1)
        dve.tensor_scalar(m2e, m2, 1.0 / D, EPS, ALU.mult, ALU.add).then_inc(done, 1)
        dve.wait_ge(done, base + n + 6)
        dve.tensor_tensor(self.ve[:, :], q, m2e, ALU.add).then_inc(done, 1)


def attention_stage(nc, x_dram, wqkv, wo, rope, X, ident, banks):
    with ExitStack() as ctx:
        m = Memory(nc, ctx, "attn", banks)
        sb, sem = m.sb, m.sem
        w_in = sb("w_in", [P, KD, 2 * D])
        w_h, w_l = m.pair("wqkv", [P, KD, 2 * D])
        wo_in = sb("wo_in", [P, KD, D])
        wo_h, wo_l = m.pair("wo", [P, KD, D])
        cs = sb("rope", [P, TB, 2, HD])
        xb = sb("xb", [P, TB, D])
        ln = RowStats(m, "ln", TB)
        rstd = sb("rstd", [P, TB])
        nhalf = sb("nhalf", [P, TB])
        xn = sb("xn", [P, TB, D])
        xt_h, xt_l = m.pair("xt", [P, KD, S])
        rc = sb("rc", [P, 2, 24, HD])
        rs = sb("rs", [P, 2, 24, HD])
        qk = sb("qk", [P, 2, 24, HD])
        st = sb("st", [P, TB, 24, SLOTS, HD])
        v = sb("v", [P, TB, NKV, 32])
        qp = sb("qp", [P, PACKS, S], F32R)
        kz = sb("kz", [P, NKV, S], F32R)
        nm = sb("nm", [P, TB, NH])
        pt = sb("pt", [P, 2, 4, S])
        ot = sb("ot", [P, 2, S])
        rec = sb("rec", [P, 2, TB, 4])
        ao = sb("ao", [P, TB, D])
        at_h, at_l = m.pair("at", [P, KD, S])

        ps_ring = m.psum([P, 2, 2, S])
        ps_sc = m.psum([P, 2, S])
        ps_pv = m.psum([P, S])
        ps_m = m.psum([P, S])

        w_loaded, wo_loaded, c_loaded, x_loaded = sem("w_loaded"), sem("wo_loaded"), sem("c_loaded"), sem("x_loaded")
        set_up, w_act, w_split = sem("set_up"), sem("w_act"), sem("w_split")
        kz_zeroed, nhalf_set = sem("kz_zeroed"), sem("nhalf_set")
        rstd_ready, xn_ready = sem("rstd_ready"), sem("xn_ready")
        filled = sem("filled")
        emptied = {"dve": sem("emptied_dve"), "act": sem("emptied_act")}
        xt_hi = sem("xt_hi")
        v_copied, rotated, qk_ready, rot_free = sem("v_copied"), sem("rotated"), sem("qk_ready"), sem("rot_free")
        emptied["rot"] = rotated
        st_hi, st_ready = sem("st_hi"), sem("st_ready")
        st_copied = sem("st_copied")
        aux0, aux1 = sem("aux0"), sem("aux1")
        aux_zeroed = sem("aux_zeroed")
        m_filled = sem("m_filled")
        m_emptied = {"dve": sem("m_emptied_dve"), "act": sem("m_emptied_act")}
        at_hi = sem("at_hi")
        sc_filled, exp_done, pv_done, ot_copied, rec_ready = (
            sem("sc_filled"), sem("exp_done"), sem("pv_done"), sem("ot_copied"), sem("rec_ready"))

        names = ["xt0", "xt1", "qkv0", "qkv1", "k0", "k1", "q0", "q1", "q2", "q3"]
        ring = Ring(2, ["dve", "dve", "rot", "rot", "act", "dve", "act", "dve", "act", "dve"] + ["dve"] * 32,
                    {"rot": 4})
        use_of = {n: i for i, n in enumerate(names)}
        MAX0 = len(names)
        USES = len(ring.owners)
        RD, RA = ring.total["dve"], ring.total["act"]
        m_uses = ["retr0a", "retr0b"]
        for g in range(1, 4):
            m_uses += [f"retr{g}a", f"retr{g}b", f"ot{g - 1}"]
        m_uses += ["ot3", "at0", "at1", "wo0", "wo1"]
        misc = Ring(1, ["act" if n.startswith("retr") else "dve" for n in m_uses])
        m_of = {n: i for i, n in enumerate(m_uses)}
        MU = len(m_uses)

        def misc_filled(b, name):
            return MU * b + m_of[name] + 1

        def ring_filled(b, use):
            return USES * b + use + 1

        with nc.Block() as block:

            @block.sync
            def _(sp):
                sp.dma_start(w_in[:, :, :], wqkv.rearrange("(k p) n -> p k n", p=P)).then_inc(w_loaded, 16)
                sp.dma_start(cs[:, :, :, :], rope.rearrange("(t p) a n -> p t a n", p=P)).then_inc(c_loaded, 16)
                sp.dma_start(wo_in[:, :, :], wo.rearrange("(k p) n -> p k n", p=P)).then_inc(wo_loaded, 16)
                for b in range(B):
                    if b > 0:
                        sp.wait_ge(x_loaded, 16 * b)
                    sp.dma_start(X[:, TB * b:TB * (b + 1), :],
                                 x_dram[b].rearrange("(t p) d -> p t d", p=P)).then_inc(x_loaded, 16)
                sp.wait_ge(x_loaded, 16 * B)

            @block.gpsimd
            def _(pool):
                pool.memset(nhalf[:, :], -0.5).then_inc(nhalf_set, 1)
                pool.wait_ge(nhalf_set, 1)
                with pool.Fori(0, B) as b:
                    pool.wait_ge(ln.done, ln.steps * (b + 1))
                    pool.wait_ge(xn_ready, TB * b)
                    pool.tensor_tensor(rstd[:, :], ln.ve[:, :], nhalf[:, :], ALU.pow).then_inc(rstd_ready, 1)
                    for t in range(TB):
                        pool.wait_ge(rotated, 2 * (TB * b + t) + 2)
                        if t >= 2:
                            pool.wait_ge(st_ready, 2 * (TB * b + t - 1))
                        else:
                            pool.wait_ge(st_ready, 2 * TB * b)
                        pool.tensor_tensor(qk[:, t % 2, :, 0:8], rc[:, t % 2, :, 0:8], rs[:, t % 2, :, 8:16],
                                           ALU.subtract).then_inc(qk_ready, 1)
                        pool.tensor_tensor(qk[:, t % 2, :, 8:16], rs[:, t % 2, :, 0:8], rc[:, t % 2, :, 8:16],
                                           ALU.add).then_inc(qk_ready, 1)
                        pool.wait_ge(st_hi, TB * b + t + 1)
                        pool.tensor_tensor(st[:, t, 0:NH, 1, :], qk[:, t % 2, 0:NH, :], st[:, t, 0:NH, 0, :],
                                           ALU.subtract).then_inc(st_ready, 1)
                        pool.tensor_tensor(st[:, t, NH:24, 2, :], qk[:, t % 2, NH:24, :], st[:, t, NH:24, 0, :],
                                           ALU.subtract).then_inc(st_ready, 1)

            @block.scalar
            def _(act):
                act.wait_ge(w_loaded, 16)
                act.activation(w_h[:, :, :], w_in[:, :, :], ACT.Copy).then_inc(w_act, 1)
                act.wait_ge(wo_loaded, 16)
                act.activation(wo_h[:, :, :], wo_in[:, :, :], ACT.Copy).then_inc(w_act, 1)
                act.wait_ge(kz_zeroed, 1)
                act.wait_ge(set_up, 5)
                with act.Fori(0, B) as b:
                    for k in range(KD):
                        act.wait_ge(filled, ring_filled(b, k))
                        act.activation(xt_h[:, k, :], ps_ring[:, k % 2, 0, :], ACT.Copy).then_inc(xt_hi, 1)
                    for i in range(2):
                        act.wait_ge(filled, ring_filled(b, use_of[f"qkv{i}"]))
                        act.wait_ge(pv_done, 16 * b)
                        act.activation(v[:, 2 * i:2 * i + 2, :, 0:HD],
                                       ps_ring[:, i % 2, :, QC + KC:].rearrange("p t (j d) -> p t j d", d=HD),
                                       ACT.Copy).then_inc(v_copied, 1)
                    for t in range(TB):
                        act.wait_ge(st_hi, TB * b + t + 1)
                        act.activation(st[:, t, 0:NH, 2, :], st[:, t, 0:NH, 0, :], ACT.Copy).then_inc(st_copied, 1)
                        act.activation(st[:, t, NH:24, 1, :], st[:, t, NH:24, 0, :], ACT.Copy).then_inc(st_copied, 1)
                    for name in ("k0", "q0", "q2"):
                        u = use_of[name]
                        act.wait_ge(filled, ring_filled(b, u))
                        if name == "k0":
                            act.activation(kz[0:64, 0:4:2, :], ps_ring[0:64, u % 2, :, :], ACT.Copy)
                            act.activation(kz[64:P, 1:4:2, :], ps_ring[64:P, u % 2, :, :],
                                           ACT.Copy).then_inc(emptied["act"], 1)
                        else:
                            n = 2 * int(name[1])
                            act.activation(qp[:, n:n + 2, :], ps_ring[:, u % 2, :, :],
                                           ACT.Copy).then_inc(emptied["act"], 1)

                    def requeries(g):
                        for r in range(2):
                            act.wait_ge(m_filled, misc_filled(b, f"retr{g}{'ab'[r]}"))
                            act.activation(qp[:, 2 * g + r, :], ps_m[:, :], ACT.Copy).then_inc(m_emptied["act"], 1)

                    requeries(0)
                    for s in range(16):
                        g, kt = s // 4, s % 4
                        if kt == 3 and g < 3:
                            pass
                        for a in range(4):
                            act.wait_ge(sc_filled, 64 * b + 4 * s + a + 1)
                            if a == 0:
                                act.wait_ge(pv_done, 16 * b + max(s - 1, 0))
                            act.activation(pt[:, s % 2, a, :], ps_sc[:, a % 2, :], ACT.Exp,
                                           scale=HD ** -0.5).then_inc(exp_done, 1)
                        if kt == 3 and g < 3:
                            requeries(g + 1)
                        if kt == 0 and g > 0:
                            copy_out(act, b, g - 1, ot, ps_pv, pv_done, ot_copied, m_filled, MU, misc, m_of)
                    copy_out(act, b, 3, ot, ps_pv, pv_done, ot_copied, m_filled, MU, misc, m_of)
                    for k in range(KD):
                        act.wait_ge(m_filled, misc_filled(b, f"at{k}"))
                        act.activation(at_h[:, k, :], ps_m[:, :], ACT.Copy).then_inc(at_hi, 1)

            @block.vector
            def _(dve):
                dve.memset(v[:, :, :, HD:32], 0.0).then_inc(set_up, 1)
                dve.memset(st[:, :, :, 3, :], 0.0).then_inc(set_up, 1)
                dve.memset(kz[64:P, 0:NKV:2, :].bitcast(F32), 0.0)
                dve.memset(kz[0:64, 1:NKV:2, :].bitcast(F32), 0.0).then_inc(kz_zeroed, 1)
                dve.wait_ge(set_up, 2)
                dve.memset(v[:, :, :, HD:HD + 1], 1.0).then_inc(set_up, 1)
                dve.memset(st[:, :, NH:24, 3, 0:2], 1.0).then_inc(set_up, 1)
                dve.wait_ge(w_act, 1)
                dve.tensor_tensor(w_l[:, :, :], w_in[:, :, :], w_h[:, :, :].bitcast(F32),
                                  ALU.subtract).then_inc(w_split, 1)
                dve.wait_ge(w_act, 2)
                dve.tensor_tensor(wo_l[:, :, :], wo_in[:, :, :], wo_h[:, :, :].bitcast(F32),
                                  ALU.subtract).then_inc(w_split, 1)
                dve.wait_ge(c_loaded, 16)
                dve.memset(rec[:, :, :, :], 0.0).then_inc(set_up, 1)
                dve.wait_ge(set_up, 5)
                with dve.Fori(0, B) as b:
                    dve.wait_ge(x_loaded, 16 * (b + 1))
                    dve.tensor_copy(xb[:, :, :], X[:, bass.ts(b, TB), :]).then_inc(aux_zeroed, 1)
                    dve.memset(st[:, :, 0:NH, 3, 0:2], 0.0).then_inc(aux_zeroed, 1)
                    dve.wait_ge(aux_zeroed, 2 * b + 1)
                    ln.run(dve, b, lambda t: xb[:, t, :])
                    dve.wait_ge(rstd_ready, b + 1)
                    for t in range(TB):
                        dve.tensor_scalar(xn[:, t, :], xb[:, t, :], ln.mean[:, t:t + 1], rstd[:, t:t + 1],
                                          ALU.subtract, ALU.mult).then_inc(xn_ready, 1)
                    for k in range(KD):
                        dve.wait_ge(xt_hi, KD * b + k + 1)
                        dve.tensor_tensor(xt_l[:, k, :], ps_ring[:, k % 2, 0, :], xt_h[:, k, :].bitcast(F32),
                                          ALU.subtract).then_inc(emptied["dve"], 1)

                    def high(t):
                        dve.wait_ge(qk_ready, 2 * (TB * b + t) + 2)
                        dve.tensor_copy(st[:, t, :, 0, :].bitcast(F32R), qk[:, t % 2, :, :]).then_inc(st_hi, 1)

                    for t in range(TB):
                        i = t // 2
                        if t % 2 == 0:
                            dve.wait_ge(filled, ring_filled(b, use_of[f"qkv{i}"]))
                            dve.wait_ge(v_copied, 2 * b + i + 1)
                        if t >= 2:
                            dve.wait_ge(qk_ready, 2 * (TB * b + t - 1))
                        else:
                            dve.wait_ge(qk_ready, 2 * TB * b)
                        src = ps_ring[:, i % 2, t % 2, 0:QC + KC].rearrange("p (h d) -> p h d", d=HD)
                        dve.tensor_tensor(rc[:, t % 2, :, :], src, cs[:, t, 0:1, :].to_broadcast([P, 24, HD]),
                                          ALU.mult).then_inc(rotated, 1)
                        dve.tensor_tensor(rs[:, t % 2, :, :], src, cs[:, t, 1:2, :].to_broadcast([P, 24, HD]),
                                          ALU.mult).then_inc(rotated, 1)
                        if t >= 1:
                            high(t - 1)
                    high(TB - 1)
                    for name in ("k1", "q1", "q3"):
                        u = use_of[name]
                        dve.wait_ge(filled, ring_filled(b, u))
                        if name == "k1":
                            dve.tensor_copy(kz[0:64, 4:8:2, :], ps_ring[0:64, u % 2, :, :])
                            dve.tensor_copy(kz[64:P, 5:8:2, :], ps_ring[64:P, u % 2, :, :]).then_inc(emptied["dve"], 1)
                        else:
                            n = 2 * int(name[1])
                            dve.tensor_copy(qp[:, n:n + 2, :], ps_ring[:, u % 2, :, :]).then_inc(emptied["dve"], 1)

                    def maxima(g, lo, hi):
                        for n in range(lo, hi):
                            use = MAX0 + 8 * g + n
                            i, qt = 4 * g + n // 2, 2 * (n % 2)
                            dve.wait_ge(filled, ring_filled(b, use))
                            if g == 0 and n == 0:
                                dve.wait_ge(aux1, 4 * b)
                            dve.tensor_reduce(nm[:, qt:qt + 2, i], ps_ring[:, use % 2, :, :], AX_X, ALU.max,
                                              negate=True).then_inc(emptied["dve"], 1)

                    def spare_rows(g):
                        h = slice(4 * g, 4 * g + 4)
                        dve.wait_ge(emptied["dve"], RD * b + ring.count(MAX0 + 8 * g + 7, "dve"))
                        dve.tensor_copy(st[:, :, h, 3, 0].bitcast(F32R), nm[:, :, h]).then_inc(aux0, 1)
                        dve.wait_ge(aux0, 4 * b + g + 1)
                        dve.tensor_tensor(st[:, :, h, 3, 1], nm[:, :, h], st[:, :, h, 3, 0],
                                          ALU.subtract).then_inc(aux1, 1)

                    def normalize(g):
                        dve.wait_ge(m_filled, misc_filled(b, f"ot{g}"))
                        o = ps_m[:, :].rearrange("p (t a c) -> p t a c", t=TB, c=32)
                        dve.reciprocal(rec[:, g % 2, :, :], o[:, :, :, HD]).then_inc(rec_ready, 1)
                        dve.wait_ge(rec_ready, 4 * b + g + 1)
                        for t in range(TB):
                            ins = dve.tensor_tensor(
                                ao[:, t, 64 * g:64 * g + 64].rearrange("p (a d) -> p a d", d=HD), o[:, t, :, 0:HD],
                                rec[:, g % 2, t, :].unsqueeze(2).to_broadcast([P, 4, HD]), ALU.mult)
                        ins.then_inc(m_emptied["dve"], 1)

                    maxima(0, 0, 8)
                    spare_rows(0)
                    for g in range(4):
                        if g < 3:
                            maxima(g + 1, 0, 6)
                        if g > 0:
                            normalize(g - 1)
                        if g < 3:
                            maxima(g + 1, 6, 8)
                            spare_rows(g + 1)
                    normalize(3)
                    for k in range(KD):
                        dve.wait_ge(at_hi, KD * b + k + 1)
                        dve.tensor_tensor(at_l[:, k, :], ps_m[:, :], at_h[:, k, :].bitcast(F32),
                                          ALU.subtract).then_inc(m_emptied["dve"], 1)
                    for i in range(2):
                        dve.wait_ge(m_filled, misc_filled(b, f"wo{i}"))
                        dve.tensor_tensor(X[:, bass.ds(TB * b + 2 * i, 2), :],
                                          ps_m[:, :].rearrange("p (t d) -> p t d", t=2),
                                          xb[:, 2 * i:2 * i + 2, :], ALU.add).then_inc(m_emptied["dve"], 1)
                    dve.wait_ge(m_emptied["dve"], misc.total["dve"] * (b + 1))

            @block.tensor
            def _(pe):
                pe.wait_ge(w_split, 2)
                pe.wait_ge(set_up, 5)
                with pe.Fori(0, B) as b:

                    def begin(use):
                        ring.wait_free(pe, emptied, b, use)
                        return ps_ring[:, use % 2, :, :]

                    def transposes(out, cols):
                        for t in range(TB):
                            ins = pe.transpose(out[:, P * t:P * (t + 1)], cols(t), ident[:, :])
                        return ins

                    pe.wait_ge(xn_ready, TB * (b + 1))
                    for k in range(KD):
                        o = begin(k)
                        transposes(o[:, 0, :], lambda t: xn[:, t, P * k:P * (k + 1)]).then_inc(filled, 1)
                    for i in range(2):
                        o = begin(use_of[f"qkv{i}"])
                        if i == 0:
                            pe.wait_ge(xt_hi, KD * (b + 1))
                            pe.wait_ge(emptied["dve"], RD * b + KD)
                        for t in range(2):
                            at = P * (2 * i + t)
                            for k in range(KD):
                                ins = product(pe, o[:, t, :], (xt_h[:, k, at:at + P], xt_l[:, k, at:at + P]),
                                              (w_h[:, k, :], w_l[:, k, :]), k == 0, k == KD - 1)
                        ins.then_inc(filled, 1)
                    for name in names[4:]:
                        u = use_of[name]
                        o = begin(u)
                        if name in ("k0", "k1"):
                            pe.wait_ge(v_copied, 2 * b + int(name[1]) + 1)
                        if name == "k0":
                            pe.wait_ge(st_ready, 2 * TB * (b + 1))
                            pe.wait_ge(st_copied, 2 * TB * (b + 1))
                            pe.wait_ge(aux_zeroed, 2 * b + 2)
                        for r in range(2):
                            h = (NH if name[0] == "k" else 0) + 4 * int(name[1]) + 2 * r
                            ins = transposes(o[:, r, :],
                                             lambda t: st[:, t, h:h + 2, :, :].rearrange("p h s d -> p (h s d)"))
                        ins.then_inc(filled, 1)
                    pe.wait_ge(emptied["act"], RA * (b + 1))
                    pe.wait_ge(emptied["dve"], RD * b + ring.count(MAX0 - 1, "dve"))

                    def score_rows(g, lo, hi):
                        for n in range(lo, hi):
                            use = MAX0 + 8 * g + n
                            i, qt = 4 * g + n // 2, 2 * (n % 2)
                            pack, j = i // 2, 2 * g + i % 2
                            o = begin(use)
                            for q in range(2):
                                at = P * (qt + q)
                                ins = pe.matmul(o[:, q, :], qp[:, pack, at:at + P], kz[:, j, :], start=True, stop=True)
                            ins.then_inc(filled, 1)

                    def requeries(g):
                        pe.wait_ge(aux1, 4 * b + g + 1)
                        for r in range(2):
                            misc.wait_free(pe, m_emptied, b, m_of[f"retr{g}{'ab'[r]}"])
                            h = 4 * g + 2 * r
                            transposes(ps_m[:, :], lambda t: st[:, t, h:h + 2, :, :].rearrange(
                                "p h s d -> p (h s d)")).then_inc(m_filled, 1)

                    def scores(s):
                        g, kt = s // 4, s % 4
                        if kt == 0:
                            pe.wait_ge(m_emptied["act"], misc.total["act"] * b + 2 * g + 2)
                        for a in range(4):
                            half, r = a // 2, a % 2
                            pe.wait_ge(exp_done, 64 * b + max(4 * s + a - 1, 0))
                            pe.matmul(ps_sc[:, a % 2, :], kz[:, 2 * g + half, P * kt:P * (kt + 1)],
                                      qp[:, 2 * g + r, :], start=True, stop=True).then_inc(sc_filled, 1)

                    def values(s):
                        g, kt = s // 4, s % 4
                        if kt == 0:
                            pe.wait_ge(ot_copied, 4 * b + g)
                        pe.wait_ge(exp_done, 64 * b + 4 * s + 4)
                        for a in range(4):
                            ins = pe.matmul(ps_pv[32 * a:32 * a + 32, :], v[:, kt, 2 * g + a // 2, :],
                                            pt[:, s % 2, a, :], start=(kt == 0), stop=(kt == 3))
                        ins.then_inc(pv_done, 1)

                    def outputs(g):
                        pe.wait_ge(ot_copied, 4 * b + g + 1)
                        misc.wait_free(pe, m_emptied, b, m_of[f"ot{g}"])
                        transposes(ps_m[:, :], lambda t: ot[:, g % 2, P * t:P * (t + 1)]).then_inc(m_filled, 1)

                    score_rows(0, 0, 8)
                    requeries(0)
                    for s in range(16):
                        g, kt = s // 4, s % 4
                        if g < 3 and kt < 3:
                            score_rows(g + 1, 3 * kt, min(3 * kt + 3, 8))
                        scores(s)
                        if s > 0:
                            values(s - 1)
                        if kt == 1 and g > 0:
                            outputs(g - 1)
                        if kt == 3 and g < 3:
                            requeries(g + 1)
                    values(15)
                    outputs(3)
                    pe.wait_ge(m_emptied["dve"], misc.total["dve"] * b + 4)
                    for k in range(KD):
                        misc.wait_free(pe, m_emptied, b, m_of[f"at{k}"])
                        transposes(ps_m[:, :], lambda t: ao[:, t, P * k:P * (k + 1)]).then_inc(m_filled, 1)
                    for i in range(2):
                        misc.wait_free(pe, m_emptied, b, m_of[f"wo{i}"])
                        for t in range(2):
                            at = P * (2 * i + t)
                            for k in range(KD):
                                ins = product(pe, ps_m[:, D * t:D * (t + 1)],
                                              (at_h[:, k, at:at + P], at_l[:, k, at:at + P]),
                                              (wo_h[:, k, :], wo_l[:, k, :]), k == 0, k == KD - 1)
                        ins.then_inc(m_filled, 1)

        m.close()


def copy_out(act, b, g, ot, ps_pv, pv_done, ot_copied, m_filled, MU, misc, m_of):
    act.wait_ge(pv_done, 16 * b + 4 * g + 4)
    if g >= 2:
        act.wait_ge(m_filled, MU * b + m_of[f"ot{g - 2}"] + 1)
    act.activation(ot[:, g % 2, :], ps_pv[:, :], ACT.Copy).then_inc(ot_copied, 1)


def experts_stage(nc, stage, w13, w2a, w2b, wg, X, ident, consts, xd, oe, banks):
    upper, ones, rank, first_slot = consts
    NW = 2 * KD * H
    with ExitStack() as ctx:
        m = Memory(nc, ctx, stage, banks)
        sb, sem = m.sb, m.sem
        s13_in, s2_in = sb("s13_in", [P, KD, 2, H]), sb("s2_in", [P, 3, D])
        s13, s2 = m.pair("s13", [P, KD, 2, H]), m.pair("s2", [P, 3, D])
        e13_in, e2_in = sb("e13_in", [P, 2, KD, 2, H]), sb("e2_in", [P, 2, 3, D])
        e13, e2 = m.pair("e13", [P, 2, KD, 2, H]), m.pair("e2", [P, 2, 3, D])
        wg_in, wgs = sb("wg_in", [P, KD, E]), m.pair("wg", [P, KD, E])
        ln = RowStats(m, "ln", TB)
        nhalf, rstd = sb("nhalf", [P, TB]), sb("rstd", [P, TB])
        xb = sb("xb", [P, TB, D])
        xn = sb("xn", [P, TB, D])
        xs = sb("xs", [P, TB, D])
        xt_h, xt_l = m.pair("xt", [P, KD, S])
        sil, hid = sb("sil", [P, 3, C]), sb("hid", [P, 3, C])
        h_h, h_l = m.pair("h", [P, 3, C])
        lg, ex, eq, sc, oh = (sb(n, [P, TB, E]) for n in ("lg", "ex", "eq", "sc", "oh"))
        pos, val = sb("pos", [P, TB, E]), sb("val", [P, TB, E])
        mx, sm, em, ms, rsm, gate, px, slot, keep, off, sls, slg = (
            sb(n, [P, TB]) for n in ("mx", "sm", "em", "ms", "rsm", "gate", "px", "slot", "keep", "off", "sls", "slg"))
        base = sb("base", [P, E])
        to_slot = sb("to_slot", [P, TB], U32)
        from_slot = sb("from_slot", [P, TILES], U32)
        weight = sb("weight", [P, TILES])
        xe = sb("xe", [P, 2, U, D])
        xet_h, xet_l = m.pair("xet", [P, KD, C])
        eo = sb("eo", [P, 2, U, D])
        got = sb("got", [P, 4, D])

        ps_t = m.psum([P, 2, S])
        ps_up = m.psum([P, 3, 2, C])
        ps_down = m.psum([P, U, S])
        ps_r = m.psum([P, S])

        s_loaded, g_loaded = sem("s_loaded"), sem("g_loaded")
        e_loaded = [sem("e_loaded0"), sem("e_loaded1")]
        xe_loaded = [sem("xe_loaded0"), sem("xe_loaded1")]
        set_up = sem("set_up")
        s_high, s_low = sem("s_high"), sem("s_low")
        e_high, e_low = sem("e_high"), sem("e_low")
        xb_copied, rstd_ready, xn_ready, xs_copied = (
            sem("xb_copied"), sem("rstd_ready"), sem("xn_ready"), sem("xs_copied"))
        t_filled, xt_high, xt_low = sem("t_filled"), sem("xt_high"), sem("xt_low")
        up_done, sil_done, hid_done, h_high, h_low = (
            sem("up_done"), sem("sil_done"), sem("hid_done"), sem("h_high"), sem("h_low"))
        down_done, added = sem("down_done"), sem("added")
        logits_done, ex_done, counted = sem("logits_done"), sem("ex_done"), sem("counted")
        route = sem("route")
        scattered = sem("scattered", keep=True)
        eo_stored = [sem("eo_stored0"), sem("eo_stored1")]
        gathered = [sem(f"gathered{i}", keep=True) for i in range(4)]
        combined = sem("combined")
        ROUTE = 24

        def load_weights(q, dst13, dst2, e, done):
            q.dma_start(dst13.rearrange("p k a h -> p (k a h)"), w13[e]).then_inc(done, 16)
            q.dma_start(dst2[:, 0:2, :].rearrange("p i d -> p (i d)"), w2a[e]).then_inc(done, 16)
            q.dma_start(dst2[0:HT[2], 2, :], w2b[e]).then_inc(done, 16)

        def high_parts(eng, hi13, hi2, in13, in2, done):
            copy = (lambda o, i: eng.activation(o, i, ACT.Copy))
            copy(hi13, in13)
            copy(hi2[:, 0:2, :], in2[:, 0:2, :])
            copy(hi2[0:HT[2], 2, :], in2[0:HT[2], 2, :]).then_inc(done, 1)

        def low_parts(eng, lo13, lo2, hi13, hi2, in13, in2, done):
            sub = (lambda o, i, h: eng.tensor_tensor(o, i, h.bitcast(F32), ALU.subtract))
            sub(lo13, in13, hi13)
            sub(lo2[:, 0:2, :], in2[:, 0:2, :], hi2[:, 0:2, :])
            sub(lo2[0:HT[2], 2, :], in2[0:HT[2], 2, :], hi2[0:HT[2], 2, :]).then_inc(done, 1)

        def up(pe, n, i, xt, w, off_t):
            rows = slice(P * i, P * i + HT[i])
            if i == 0:
                pe.wait_ge(hid_done, 3 * n)
            for a in range(2):
                for k in range(KD):
                    ins = product(pe, ps_up[0:HT[i], i, a, :], (w[0][:, k, a, rows], w[1][:, k, a, rows]),
                                  (xt[0][:, k, off_t:off_t + C], xt[1][:, k, off_t:off_t + C]), k == 0, k == KD - 1)
            ins.then_inc(up_done, 1)

        def down(pe, n, i, w):
            if i == 0:
                pe.wait_ge(added, n)
            pe.wait_ge(h_low, 3 * n + i + 1)
            for t in range(U):
                ins = product(pe, ps_down[:, t, 0:D],
                              (h_h[0:HT[i], i, P * t:P * (t + 1)], h_l[0:HT[i], i, P * t:P * (t + 1)]),
                              (w[0][0:HT[i], i, :], w[1][0:HT[i], i, :]), i == 0, i == 2)
            if i == 2:
                ins.then_inc(down_done, 1)

        def silu(act, n, i):
            act.wait_ge(up_done, 3 * n + i + 1)
            act.activation(sil[0:HT[i], i, :], ps_up[0:HT[i], i, 0, :], ACT.Silu).then_inc(sil_done, 1)

        def hidden_high(act, n, i):
            act.wait_ge(hid_done, 3 * n + i + 1)
            act.activation(h_h[0:HT[i], i, :], hid[0:HT[i], i, :], ACT.Copy).then_inc(h_high, 1)

        def hidden(dve, n, i):
            dve.wait_ge(sil_done, 3 * n + i + 1)
            dve.tensor_tensor(hid[0:HT[i], i, :], sil[0:HT[i], i, :], ps_up[0:HT[i], i, 1, :],
                              ALU.mult).then_inc(hid_done, 1)

        def hidden_low(eng, n, i):
            eng.wait_ge(h_high, 3 * n + i + 1)
            eng.tensor_tensor(h_l[0:HT[i], i, :], hid[0:HT[i], i, :], h_h[0:HT[i], i, :].bitcast(F32),
                              ALU.subtract).then_inc(h_low, 1)

        def rows(eng, body):
            with eng.Fori(0, B - 1) as b:
                body(b, False)
            body(B - 1, True)

        def experts(eng, body):
            with eng.Fori(0, E // 2 - 1) as v:
                body(2 * v, 0, False)
                body(2 * v + 1, 1, False)
            body(E - 2, 0, False)
            body(E - 1, 1, True)

        N0 = UNITS

        with nc.Block() as block:

            @block.sync
            def _(sp):
                load_weights(sp, s13_in[:, :, :, :], s2_in, E, s_loaded)
                sp.dma_start(wg_in[:, :, :], wg.rearrange("(k p) e -> p k e", p=P)).then_inc(g_loaded, 16)
                load_weights(sp, e13_in[:, 0], e2_in[:, 0], 0, e_loaded[0])
                load_weights(sp, e13_in[:, 1], e2_in[:, 1], 1, e_loaded[1])

                def load_rows(e, w):
                    sp.dma_start(xe[:, w, :, :], xd[bass.ds(C * e, C), :].rearrange("(t p) d -> p t d", p=P)
                                 ).then_inc(xe_loaded[w], 16)

                sp.wait_ge(scattered, 64 * B)
                load_rows(0, 0)
                load_rows(1, 1)

                def body(e, w, last):
                    sp.wait_ge(added, N0 + e + 1)
                    sp.dma_start(oe[bass.ds(C * e, C), :].rearrange("(t p) d -> p t d", p=P),
                                 eo[:, w, :, :]).then_inc(eo_stored[w], 16)

                def loads(e, w):
                    sp.wait_ge(t_filled, 2 * B + e + 1)
                    load_rows(e + 2, w)
                    sp.wait_ge(e_low, e + 1)
                    load_weights(sp, e13_in[:, w], e2_in[:, w], e + 2, e_loaded[w])

                with sp.Fori(0, E // 2 - 1) as v:
                    for w in range(2):
                        loads(2 * v + w, w)
                        body(2 * v + w, w, False)
                body(E - 2, 0, False)
                body(E - 1, 1, True)
                for w in range(2):
                    sp.wait_ge(eo_stored[w], 16 * E // 2)

            @block.gpsimd
            def _(pool):
                pool.memset(nhalf[:, :], -0.5).then_inc(set_up, 1)
                pool.wait_ge(set_up, 1)

                def power(b):
                    pool.wait_ge(ln.done, ln.steps * (b + 1))
                    pool.tensor_tensor(rstd[:, :], ln.ve[:, :], nhalf[:, :], ALU.pow).then_inc(rstd_ready, 1)

                power(0)
                pool.wait_ge(e_high, 1)
                low_parts(pool, e13[1][:, 0], e2[1][:, 0], e13[0][:, 0], e2[0][:, 0], e13_in[:, 0], e2_in[:, 0], e_low)

                def row(b, last):
                    for i in range(3):
                        hidden_low(pool, 2 * b, i)
                    pool.wait_ge(route, ROUTE * b + 22)
                    pool.wait_ge(xs_copied, b + 1)
                    if not last:
                        pool.wait_ge(xn_ready, TB * (b + 1))
                        power(b + 1)
                    for t in range(TB):
                        pool.indirect_dma_start(
                            xd, bass.IndirectOffsetOnAxis(ap=to_slot[:, t:t + 1], axis=0), xs[:, t, :], None,
                            bounds_check=E * C - 1, oob_is_err=False).then_inc(scattered, 16)
                    for i in range(3):
                        hidden_low(pool, 2 * b + 1, i)

                rows(pool, row)

                def expert(e, w, last):
                    if not last:
                        pool.wait_ge(e_high, e + 2)
                        pool.wait_ge(down_done, N0 + e)
                        low_parts(pool, e13[1][:, 1 - w], e2[1][:, 1 - w], e13[0][:, 1 - w], e2[0][:, 1 - w],
                                  e13_in[:, 1 - w], e2_in[:, 1 - w], e_low)

                experts(pool, expert)
                for w in range(2):
                    pool.wait_ge(eo_stored[w], 16 * E // 2)
                for t in range(TILES):
                    if t >= 4:
                        pool.wait_ge(combined, t - 3)
                    pool.indirect_dma_start(
                        got[:, t % 4, :], None, oe, bass.IndirectOffsetOnAxis(ap=from_slot[:, t:t + 1], axis=0),
                        bounds_check=E * C - 1, oob_is_err=False).then_inc(gathered[t % 4], 16)

            @block.scalar
            def _(act):
                act.wait_ge(s_loaded, 48)
                high_parts(act, s13[0][:, :, :, :], s2[0], s13_in[:, :, :, :], s2_in, s_high)
                act.wait_ge(g_loaded, 16)
                act.activation(wgs[0][:, :, :], wg_in[:, :, :], ACT.Copy).then_inc(s_high, 1)

                def transposed(b):
                    for k in range(KD):
                        act.wait_ge(t_filled, 2 * b + k + 1)
                        act.activation(xt_h[:, k, :], ps_t[:, k, :], ACT.Copy).then_inc(xt_high, 1)

                def stage_rows(b):
                    act.wait_ge(scattered, 64 * b)
                    act.activation(xs[:, :, :], xn[:, :, :], ACT.Copy).then_inc(xs_copied, 1)

                transposed(0)
                stage_rows(0)
                act.wait_ge(e_loaded[0], 48)
                high_parts(act, e13[0][:, 0], e2[0][:, 0], e13_in[:, 0], e2_in[:, 0], e_high)

                def row(b, last):
                    n = 2 * b
                    silu(act, n, 0)
                    silu(act, n, 1)
                    hidden_high(act, n, 0)
                    silu(act, n, 2)
                    hidden_high(act, n, 1)
                    hidden_high(act, n, 2)
                    act.wait_ge(route, ROUTE * b + 2)
                    act.activation(ex[:, :, :], lg[:, :, :], ACT.Exp).then_inc(ex_done, 1)
                    n = 2 * b + 1
                    silu(act, n, 0)
                    silu(act, n, 1)
                    hidden_high(act, n, 0)
                    silu(act, n, 2)
                    hidden_high(act, n, 1)
                    hidden_high(act, n, 2)
                    if not last:
                        transposed(b + 1)
                        stage_rows(b + 1)

                rows(act, row)

                def expert_rows(e):
                    act.wait_ge(t_filled, 2 * B + e + 1)
                    act.activation(xet_h[:, :, :].rearrange("p k c -> p (k c)"), ps_t[:, 0, :],
                                   ACT.Copy).then_inc(xt_high, 1)

                expert_rows(0)

                def expert(e, w, last):
                    n = N0 + e
                    silu(act, n, 0)
                    silu(act, n, 1)
                    hidden_high(act, n, 0)
                    silu(act, n, 2)
                    hidden_high(act, n, 1)
                    hidden_high(act, n, 2)
                    if not last:
                        expert_rows(e + 1)
                        act.wait_ge(e_loaded[1 - w], 24 * (e - w) + 48 * (1 + w))
                        act.wait_ge(down_done, N0 + e)
                        high_parts(act, e13[0][:, 1 - w], e2[0][:, 1 - w], e13_in[:, 1 - w], e2_in[:, 1 - w], e_high)

                experts(act, expert)

            @block.vector
            def _(dve):
                dve.memset(base[:, :], 0.0).then_inc(set_up, 1)
                dve.wait_ge(set_up, 2)

                def normalize(b):
                    dve.tensor_copy(xb[:, :, :], X[:, bass.ds(TB * b, TB), :]).then_inc(xb_copied, 1)
                    dve.wait_ge(xb_copied, b + 1)
                    ln.run(dve, b, lambda t: xb[:, t, :])
                    dve.wait_ge(rstd_ready, b + 1)
                    dve.wait_ge(xs_copied, b)
                    for t in range(TB):
                        dve.tensor_scalar(xn[:, t, :], xb[:, t, :], ln.mean[:, t:t + 1], rstd[:, t:t + 1],
                                          ALU.subtract, ALU.mult).then_inc(xn_ready, 1)

                def transposed(b):
                    for k in range(KD):
                        dve.wait_ge(xt_high, KD * b + k + 1)
                        dve.tensor_tensor(xt_l[:, k, :], ps_t[:, k, :], xt_h[:, k, :].bitcast(F32),
                                          ALU.subtract).then_inc(xt_low, 1)

                normalize(0)
                dve.wait_ge(s_high, 1)
                low_parts(dve, s13[1][:, :, :, :], s2[1], s13[0][:, :, :, :], s2[0], s13_in[:, :, :, :], s2_in, s_low)
                dve.wait_ge(s_high, 2)
                dve.tensor_tensor(wgs[1][:, :, :], wg_in[:, :, :], wgs[0][:, :, :].bitcast(F32),
                                  ALU.subtract).then_inc(s_low, 1)
                transposed(0)

                def wide(a):
                    return a[:, :].unsqueeze(2).to_broadcast([P, TB, E])

                def row(b, last):
                    at = ROUTE * b
                    steps = [0]

                    def step(ins):
                        ins.then_inc(route, 1)
                        steps[0] += 1
                        dve.wait_ge(route, at + steps[0])

                    def add_down(n, half):
                        dve.wait_ge(down_done, n + 1)
                        dve.tensor_tensor(X[:, bass.ds(TB * b + U * half, U), :],
                                          ps_down[:, :, 0:D], X[:, bass.ds(TB * b + U * half, U), :],
                                          ALU.add).then_inc(added, 1)

                    bank = ps_r[:, 0:3 * TB * E].rearrange("p (a t e) -> p a t e", a=3, e=E)
                    hidden(dve, 2 * b, 0)
                    dve.wait_ge(logits_done, b + 1)
                    step(dve.tensor_reduce(mx[:, :], bank[:, 0], AX_X, ALU.max))
                    step(dve.tensor_tensor(lg[:, :, :], bank[:, 0], wide(mx), ALU.subtract))
                    hidden(dve, 2 * b, 1)
                    hidden(dve, 2 * b, 2)
                    dve.wait_ge(ex_done, b + 1)
                    step(dve.tensor_reduce(em[:, :], ex[:, :, :], AX_X, ALU.max))
                    step(dve.tensor_tensor(eq[:, :, :], ex[:, :, :], wide(em), ALU.is_ge))
                    step(dve.tensor_tensor(sc[:, :, :], eq[:, :, :], rank, ALU.mult))
                    step(dve.tensor_reduce(ms[:, :], sc[:, :, :], AX_X, ALU.max))
                    step(dve.tensor_tensor(oh[:, :, :], sc[:, :, :], wide(ms), ALU.is_equal))
                    step(dve.tensor_reduce(sm[:, :], ex[:, :, :], AX_X, ALU.add))
                    step(dve.reciprocal(rsm[:, :], sm[:, :]))
                    step(dve.tensor_tensor(gate[:, :], em[:, :], rsm[:, :], ALU.mult))
                    add_down(2 * b, 0)
                    hidden(dve, 2 * b + 1, 0)
                    dve.wait_ge(counted, b + 1)
                    for t in range(TB):
                        dve.tensor_tensor(pos[:, t, :], bank[:, 1, t, :], base[:, :], ALU.add)
                        step(dve.tensor_tensor(base[:, :], bank[:, 2, t, :], base[:, :], ALU.add))
                    step(dve.tensor_tensor(val[:, :, :], pos[:, :, :], first_slot, ALU.add))
                    step(dve.tensor_tensor(pos[:, :, :], pos[:, :, :], oh[:, :, :], ALU.mult))
                    step(dve.tensor_tensor(val[:, :, :], val[:, :, :], oh[:, :, :], ALU.mult))
                    dve.tensor_reduce(px[:, :], pos[:, :, :], AX_X, ALU.add)
                    step(dve.tensor_reduce(slot[:, :], val[:, :, :], AX_X, ALU.add))
                    step(dve.tensor_scalar(keep[:, :], px[:, :], float(C), None, ALU.is_le))
                    step(dve.tensor_scalar(off[:, :], keep[:, :], -2.0 * E * C, 2.0 * E * C, ALU.mult, ALU.add))
                    step(dve.tensor_tensor(sls[:, :], slot[:, :], off[:, :], ALU.add))
                    step(dve.tensor_copy(to_slot[:, :], sls[:, :]))
                    step(dve.tensor_scalar(from_slot[:, bass.ds(TB * b, TB)], sls[:, :], float(E * C - 1), None,
                                           ALU.min))
                    step(dve.tensor_tensor(weight[:, bass.ds(TB * b, TB)], gate[:, :], keep[:, :], ALU.mult))
                    assert steps[0] == ROUTE
                    if not last:
                        normalize(b + 1)
                    hidden(dve, 2 * b + 1, 1)
                    hidden(dve, 2 * b + 1, 2)
                    if not last:
                        transposed(b + 1)
                    add_down(2 * b + 1, 1)

                rows(dve, row)

                def expert_rows(e):
                    dve.wait_ge(xt_high, KD * B + e + 1)
                    dve.tensor_tensor(xet_l[:, :, :].rearrange("p k c -> p (k c)"), ps_t[:, 0, :],
                                      xet_h[:, :, :].bitcast(F32).rearrange("p k c -> p (k c)"),
                                      ALU.subtract).then_inc(xt_low, 1)

                expert_rows(0)

                def expert(e, w, last):
                    n = N0 + e
                    hidden(dve, n, 0)
                    hidden(dve, n, 1)
                    hidden_low(dve, n, 0)
                    hidden(dve, n, 2)
                    hidden_low(dve, n, 1)
                    hidden_low(dve, n, 2)
                    if not last:
                        expert_rows(e + 1)
                    dve.wait_ge(down_done, n + 1)
                    dve.wait_ge(eo_stored[w], 8 * (e - w))
                    dve.tensor_copy(eo[:, w, :, :], ps_down[:, :, 0:D]).then_inc(added, 1)

                experts(dve, expert)
                for t in range(TILES):
                    dve.wait_ge(gathered[t % 4], 16 * (t // 4 + 1))
                    dve.scalar_tensor_tensor(X[:, t, :], got[:, t % 4, :], weight[:, t:t + 1], X[:, t, :],
                                             ALU.mult, ALU.add).then_inc(combined, 1)

            @block.tensor
            def _(pe):
                shared_w13, shared_w2 = s13, s2
                xt = (xt_h, xt_l)

                def transposes(b):
                    pe.wait_ge(xn_ready, TB * (b + 1))
                    for k in range(KD):
                        for t in range(TB):
                            ins = pe.transpose(ps_t[:, k, P * t:P * (t + 1)], xn[:, t, P * k:P * (k + 1)], ident[:, :])
                        ins.then_inc(t_filled, 1)

                transposes(0)
                pe.wait_ge(s_low, 2)

                def row(b, last):
                    n = 2 * b
                    pe.wait_ge(xt_low, KD * (b + 1))
                    up(pe, n, 0, xt, shared_w13, 0)
                    pe.wait_ge(route, ROUTE * b)
                    for t in range(TB):
                        for k in range(KD):
                            at = P * t
                            ins = product(pe, ps_r[:, E * t:E * (t + 1)], (xt_h[:, k, at:at + P], xt_l[:, k, at:at + P]),
                                          (wgs[0][:, k, :], wgs[1][:, k, :]), k == 0, k == KD - 1)
                    ins.then_inc(logits_done, 1)
                    up(pe, n, 1, xt, shared_w13, 0)
                    up(pe, n, 2, xt, shared_w13, 0)
                    for i in range(3):
                        down(pe, n, i, shared_w2)
                    n = 2 * b + 1
                    up(pe, n, 0, xt, shared_w13, C)
                    pe.wait_ge(route, ROUTE * b + 7)
                    one_hot = oh[:, :, :].rearrange("p t e -> p (t e)")
                    pe.matmul(ps_r[:, TB * E:2 * TB * E], upper, one_hot, start=True, stop=True)
                    pe.matmul(ps_r[:, 2 * TB * E:3 * TB * E], ones, one_hot, start=True, stop=True).then_inc(counted, 1)
                    up(pe, n, 1, xt, shared_w13, C)
                    up(pe, n, 2, xt, shared_w13, C)
                    if not last:
                        transposes(b + 1)
                    for i in range(3):
                        down(pe, n, i, shared_w2)

                rows(pe, row)

                def expert_rows(e, w):
                    pe.wait_ge(xe_loaded[w], 8 * (e - w) + 16)
                    for k in range(KD):
                        for t in range(U):
                            at = C * k + P * t
                            ins = pe.transpose(ps_t[:, 0, at:at + P], xe[:, w, t, P * k:P * (k + 1)], ident[:, :])
                    ins.then_inc(t_filled, 1)

                expert_rows(0, 0)

                def expert(e, w, last):
                    n = N0 + e
                    w13p = (e13[0][:, w], e13[1][:, w])
                    w2p = (e2[0][:, w], e2[1][:, w])
                    pe.wait_ge(e_low, e + 1)
                    pe.wait_ge(xt_low, KD * B + e + 1)
                    for i in range(3):
                        up(pe, n, i, (xet_h, xet_l), w13p, 0)
                    if not last:
                        expert_rows(e + 1, 1 - w)
                    for i in range(3):
                        down(pe, n, i, w2p)

                experts(pe, expert)
        m.close()


def state_space_stage(nc, a, X, ident, consts, banks):
    upper, ones = consts[0], consts[1]
    NF = 4
    with ExitStack() as ctx:
        m = Memory(nc, ctx, "ssm", banks)
        sb, sem = m.sb, m.sem
        stage_in = sb("stage_in", [P, 2 * INTER])
        win_in = sb("win_in", [P, KD, PROJ])
        wout_in = sb("wout_in", [P, KD, D])
        win, wout = m.pair("win", [P, KD, PROJ]), m.pair("wout", [P, KD, D])
        w1, w3, w2 = m.pair("w1", [P, KD, INTER]), m.pair("w3", [P, KD, INTER]), m.pair("w2", [P, IT, D])
        norms = sb("norms", [P, 3, KD])
        conv_w = sb("conv_w", [P, NF, 4])
        conv_b = sb("conv_b", [P, NF])
        heads = sb("heads", [P, 3, 2])
        neg_a = sb("neg_a", [P, 2])
        cap = sb("cap", [P, P])
        nhalf = sb("nhalf", [P, TB])
        xb, xh, hn = sb("xb", [P, TB, D]), sb("xh", [P, TB, D]), sb("hn", [P, TB, D])
        ln = RowStats(m, "ln", TB)
        rstd, rstd2, var, v2, r1, rr = (sb(n, [P, TB]) for n in ("rstd", "rstd2", "var", "v2", "r1", "rr"))
        ht_h, ht_l = m.pair("ht", [P, KD, S])
        cv = sb("cv", [P, NF, S + 4])
        ca = sb("ca", [P, 2, S])
        xc = sb("xc", [P, NF, S])
        sz = sb("sz", [P, TB, D])
        small = [sb(f"dt{i}", [P, TB, 2]) for i in range(16)]
        (xdt, adt, udt, wdt, ddt, zdt, dden, rden, qdt, lnw, tdt, t2, mdt, sdt, dt, dA) = small
        ecs, etot, csum, dif, dec0, dec = (sb(n, [P, TB, 2]) for n in ("ecs", "etot", "csum", "dif", "dec0", "dec"))
        xtm, btm = sb("xtm", [P, TB, P]), sb("btm", [P, TB, P])
        dd, ee, mm = sb("dd", [P, 2, P]), sb("ee", [P, 2, P]), sb("mm", [P, 2, P])
        xd, t0 = sb("xd", [P, 2, P]), sb("t0", [P, 2, P])
        state = sb("state", [P, 2, 2, P])
        y1, y2 = sb("y1", [P, 2, P]), sb("y2", [P, 2, P])
        yg = sb("yg", [P, TB, D])
        sq = sb("sq", [P, D])
        ss, ms, rq = sb("ss", [P, TB]), sb("ms", [P, TB]), sb("rq", [P, TB])
        sil, hid = sb("sil", [P, 3, C]), sb("hid", [P, 3, C])
        h_h, h_l = m.pair("h", [P, IT, C])

        ps = m.psum([P, 8, S])
        bank_t = (5, 6)
        bank_small = 7

        loads = sem("loads")
        staged = [sem(f"staged{i}") for i in range(3)]
        scaled, w_high, w_low, set_up, nhalf_set = sem("scaled"), sem("w_high"), sem("w_low"), sem("set_up"), sem("nhalf_set")
        nega = sem("nega")
        xb_copied, rstd_ready, r1_ready = sem("xb_copied"), sem("rstd_ready"), sem("r1_ready")
        pre, hn_ready = sem("pre"), sem("hn_ready")
        t_filled, t_high, t_low = sem("t_filled"), sem("t_high"), sem("t_low")
        feat, feat_out, z_filled, z_out = sem("feat"), sem("feat_out"), sem("z_filled"), sem("z_out")
        conv, conv_out, softplus = sem("conv"), sem("conv_out"), sem("softplus")
        dts, dt_act, sums, dt_filled = sem("dts"), sem("dt_act"), sem("sums"), sem("dt_filled")
        tm_filled, tm_out = sem("tm_filled"), sem("tm_out")
        g_done, row_done, dd_done, ee_done, mm_done, xd_done = (
            sem("g_done"), sem("row_done"), sem("dd_done"), sem("ee_done"), sem("mm_done"), sem("xd_done"))
        y_done, s_done, st_done, ys, yg_done, sq_done = (
            sem("y_done"), sem("s_done"), sem("st_done"), sem("ys"), sem("yg_done"), sem("sq_done"))
        norm_v, rq_ready = sem("norm_v"), sem("rq_ready")
        o_done, h2_done, r2_done = sem("o_done"), sem("h2_done"), sem("r2_done")
        up_done, sil_done, hid_done, h_high, h_low = (
            sem("up_done"), sem("sil_done"), sem("hid_done"), sem("h_high"), sem("h_low"))
        down_done, added = sem("down_done"), sem("added")

        def square(act, b, c):
            act.wait_ge(yg_done, TB * b + c + 1)
            act.wait_ge(sq_done, 2 * TB * b + c)
            act.activation(sq[:, :], yg[:, c, :], ACT.Square, accum_out=ss[:, c:c + 1]).then_inc(sq_done, 1)

        def t_banks(k):
            return ps[:, bank_t[k], :]

        with nc.Block() as block:

            @block.sync
            def _(sp):
                def load(dst, src):
                    sp.dma_start(dst, src).then_inc(loads, 16)
                load(win_in[:, :, :], a["win"].rearrange("(k p) n -> p k n", p=P))
                load(wout_in[:, :, :], a["wout"].rearrange("(k p) n -> p k n", p=P))
                load(norms[:, :, :], a["norms"])
                load(conv_w[:, :, :], a["conv_w"])
                load(conv_b[:, :], a["conv_b"])
                load(heads[:, :, :].rearrange("p a h -> p (a h)"),
                     a["heads"].rearrange("(o n) -> o n", o=1).to_broadcast([P, 6]))
                load(cap[:, :], a["cap"])
                for i, n in enumerate(("w1", "w3", "w2")):
                    if i > 0:
                        sp.wait_ge(w_low, 2 + i)
                    sp.dma_start(stage_in[:, :].rearrange("p (k n) -> p k n", k=IT if n == "w2" else KD),
                                 a[n].rearrange("(k p) n -> p k n", p=P)).then_inc(staged[i], 16)

            @block.gpsimd
            def _(pool):
                pool.memset(nhalf[:, :], -0.5).then_inc(nhalf_set, 1)
                pool.wait_ge(nhalf_set, 1)
                with pool.Fori(0, B) as b:
                    pool.wait_ge(ln.done, ln.steps * (b + 1))
                    pool.tensor_tensor(rstd[:, :], ln.ve[:, :], nhalf[:, :], ALU.pow).then_inc(rstd_ready, 1)
                    pool.wait_ge(pre, 6 * b + 4)
                    pool.tensor_tensor(r1[:, :], v2[:, :], nhalf[:, :], ALU.pow).then_inc(r1_ready, 1)
                    for i in range(2):
                        pool.wait_ge(norm_v, 2 * b + i + 1)
                        pool.tensor_tensor(rq[:, :], ms[:, :], nhalf[:, :], ALU.pow).then_inc(rq_ready, 1)
                    pool.wait_ge(h2_done, 2 * (b + 1))
                    pool.tensor_tensor(xb[:, :, :], xb[:, :, :], xh[:, :, :], ALU.add).then_inc(r2_done, 1)

            @block.scalar
            def _(act):
                act.wait_ge(loads, 16 * 7)
                act.activation(neg_a[:, :], heads[:, 1, :], ACT.Exp).then_inc(nega, 1)
                for i, (w, src) in enumerate(((win, win_in), (wout, wout_in), (w1, stage_in), (w3, stage_in),
                                              (w2, stage_in))):
                    k = IT if w is w2 else KD
                    v = src[:, :].rearrange("p (k n) -> p k n", k=k) if src is stage_in else src[:, :, :]
                    if w is w2:
                        act.wait_ge(staged[2], 16)
                    else:
                        act.wait_ge(scaled, i + 1)
                    act.activation(w[0][:, :, :], v, ACT.Copy).then_inc(w_high, 1)
                act.wait_ge(set_up, 2)
                with act.Fori(0, B) as b:

                    def high(n):
                        for k in range(KD):
                            act.wait_ge(t_filled, 6 * b + 2 * n + k + 1)
                            act.activation(ht_h[:, k, :], t_banks(k), ACT.Copy).then_inc(t_high, 1)

                    high(0)
                    for f in range(NF):
                        act.wait_ge(feat, NF * b + f + 1)
                        act.activation(cv[:, f, 3:3 + S], ps[:, f, :], ACT.Copy).then_inc(feat_out, 1)
                    act.wait_ge(dts, 11 * b + 2)
                    act.activation(udt[:, :, :], adt[:, :, :], ACT.Exp, scale=-1.0).then_inc(dt_act, 1)
                    act.wait_ge(dts, 11 * b + 3)
                    act.activation(lnw[:, :, :], wdt[:, :, :], ACT.Ln).then_inc(dt_act, 1)
                    act.wait_ge(sums, 2 * b + 2)
                    act.activation(ecs[:, :, :], ps[:, bank_small, 8:16].rearrange("p (t h) -> p t h", h=2), ACT.Exp)
                    act.activation(etot[:, :, :], ps[:, bank_small, 16:24].rearrange("p (t h) -> p t h", h=2),
                                   ACT.Exp).then_inc(dt_act, 1)
                    act.wait_ge(dts, 11 * b + 10)
                    act.activation(dec0[:, :, :], dif[:, :, :], ACT.Exp).then_inc(dt_act, 1)
                    for i in range(2):
                        act.wait_ge(z_filled, 2 * b + i + 1)
                        act.activation(sz[:, 2 * i:2 * i + 2, :].rearrange("p t d -> p (t d)"), t_banks(i),
                                       ACT.Silu).then_inc(z_out, 1)
                    for f in range(NF):
                        act.wait_ge(conv, 4 * (NF * b + f + 1))
                        act.activation(xc[:, f, :], ca[:, f % 2, :], ACT.Silu, bias=conv_b[:, f:f + 1]).then_inc(conv_out, 1)
                    for i, o in enumerate((xtm, btm)):
                        act.wait_ge(tm_filled, 2 * b + i + 1)
                        act.activation(o[:, :, :].rearrange("p t n -> p (t n)"), t_banks(i), ACT.Copy).then_inc(tm_out, 1)
                    for c in range(TB):
                        act.wait_ge(dd_done, 2 * (TB * b + c) + 2)
                        act.activation(ee[:, :, :], dd[:, :, :], ACT.Exp).then_inc(ee_done, 1)
                        if c > 0:
                            square(act, b, c - 1)
                    square(act, b, TB - 1)
                    high(1)
                    for t in range(TB):
                        act.wait_ge(h2_done, 2 * b + t // 2 + 1)
                        act.wait_ge(sq_done, 2 * TB * b + TB + t)
                        act.activation(sq[:, :], xh[:, t, :], ACT.Square, accum_out=ss[:, t:t + 1]).then_inc(sq_done, 1)
                    high(2)
                    for u in range(2):
                        n = IT * 2 * b + IT * u
                        for i in range(IT + 1):
                            if i < IT:
                                act.wait_ge(up_done, n + i + 1)
                                act.activation(sil[:, i % 3, :], ps[:, i % 3, 0:C], ACT.Silu).then_inc(sil_done, 1)
                            if i > 0:
                                act.wait_ge(hid_done, n + i)
                                act.activation(h_h[:, i - 1, :], hid[:, (i - 1) % 3, :], ACT.Copy).then_inc(h_high, 1)

            @block.vector
            def _(dve):
                dve.memset(cv[:, :, 0:3], 0.0).then_inc(set_up, 1)
                dve.wait_ge(nega, 1)
                dve.tensor_scalar(neg_a[:, :], neg_a[:, :], -1.0, None, ALU.mult).then_inc(set_up, 1)
                dve.wait_ge(set_up, 2)
                for i, (w, src) in enumerate(((win, win_in), (wout, wout_in), (w1, stage_in), (w3, stage_in),
                                              (w2, stage_in))):
                    k = IT if w is w2 else KD
                    v = src[:, :].rearrange("p (k n) -> p k n", k=k) if src is stage_in else src[:, :, :]
                    if w is not w2:
                        if i >= 2:
                            dve.wait_ge(staged[i - 2], 16)
                        norm = (0, 1, 2, 2)[i]
                        for j in range(KD):
                            ins = dve.tensor_scalar(v[:, j, :], v[:, j, :], norms[:, norm, j:j + 1], None, ALU.mult)
                        ins.then_inc(scaled, 1)
                        dve.wait_ge(scaled, i + 1)
                    dve.wait_ge(w_high, i + 1)
                    dve.tensor_tensor(w[1][:, :, :], v, w[0][:, :, :].bitcast(F32), ALU.subtract).then_inc(w_low, 1)
                with dve.Fori(0, B) as b:
                    dve.wait_ge(r2_done, b)
                    dve.tensor_copy(xb[:, :, :], X[:, bass.ds(TB * b, TB), :]).then_inc(xb_copied, 1)
                    dve.wait_ge(xb_copied, b + 1)
                    ln.run(dve, b, lambda t: xb[:, t, :])
                    at = 6 * b
                    dve.wait_ge(rstd_ready, b + 1)
                    dve.wait_ge(ln.done, ln.steps * (b + 1))
                    dve.tensor_scalar(var[:, :], ln.ve[:, :], -EPS, None, ALU.add).then_inc(pre, 1)
                    dve.tensor_tensor(rstd2[:, :], rstd[:, :], rstd[:, :], ALU.mult).then_inc(pre, 1)
                    dve.wait_ge(pre, at + 2)
                    dve.tensor_tensor(v2[:, :], var[:, :], rstd2[:, :], ALU.mult).then_inc(pre, 1)
                    dve.wait_ge(pre, at + 3)
                    dve.tensor_scalar(v2[:, :], v2[:, :], EPS, None, ALU.add).then_inc(pre, 1)
                    for t in range(TB):
                        ins = dve.tensor_scalar(xh[:, t, :], xb[:, t, :], ln.mean[:, t:t + 1], rstd[:, t:t + 1],
                                                ALU.subtract, ALU.mult)
                    ins.then_inc(pre, 1)
                    dve.wait_ge(r1_ready, b + 1)
                    dve.tensor_tensor(rr[:, :], rstd[:, :], r1[:, :], ALU.mult).then_inc(pre, 1)
                    dve.wait_ge(pre, at + 6)
                    for t in range(TB):
                        ins = dve.tensor_scalar(hn[:, t, :], xb[:, t, :], ln.mean[:, t:t + 1], rr[:, t:t + 1],
                                                ALU.subtract, ALU.mult)
                    ins.then_inc(hn_ready, 1)

                    def low(n):
                        for k in range(KD):
                            dve.wait_ge(t_high, 6 * b + 2 * n + k + 1)
                            dve.tensor_tensor(ht_l[:, k, :], t_banks(k), ht_h[:, k, :].bitcast(F32),
                                              ALU.subtract).then_inc(t_low, 1)

                    low(0)
                    d0 = 11 * b
                    dve.wait_ge(dt_filled, b + 1)
                    raw = ps[:, bank_small, 0:8].rearrange("p (t h) -> p t h", h=2)
                    wide = (lambda v: v.unsqueeze(1).to_broadcast([P, TB, 2]))
                    dve.tensor_tensor(xdt[:, :, :], raw, wide(heads[:, 0, :]), ALU.add).then_inc(dts, 1)
                    dve.wait_ge(dts, d0 + 1)
                    dve.tensor_scalar(mdt[:, :, :], xdt[:, :, :], 0.0, None, ALU.max)
                    dve.scalar_tensor_tensor(adt[:, :, :], xdt[:, :, :], -1.0, xdt[:, :, :], ALU.mult, ALU.max
                                             ).then_inc(dts, 1)
                    dve.wait_ge(dt_act, 4 * b + 1)
                    dve.tensor_scalar(wdt[:, :, :], udt[:, :, :], 1.0, None, ALU.add).then_inc(dts, 1)
                    dve.wait_ge(dts, d0 + 3)
                    dve.tensor_scalar(ddt[:, :, :], wdt[:, :, :], -1.0, None, ALU.add).then_inc(dts, 1)
                    dve.wait_ge(dts, d0 + 4)
                    dve.tensor_scalar(zdt[:, :, :], ddt[:, :, :], 0.0, None, ALU.is_equal).then_inc(dts, 1)
                    dve.wait_ge(dts, d0 + 5)
                    dve.tensor_tensor(t2[:, :, :], zdt[:, :, :], udt[:, :, :], ALU.mult)
                    dve.tensor_tensor(dden[:, :, :], zdt[:, :, :], ddt[:, :, :], ALU.add).then_inc(dts, 1)
                    dve.wait_ge(dts, d0 + 6)
                    dve.reciprocal(rden[:, :, :], dden[:, :, :]).then_inc(dts, 1)
                    dve.wait_ge(dts, d0 + 7)
                    dve.tensor_tensor(qdt[:, :, :], udt[:, :, :], rden[:, :, :], ALU.mult).then_inc(softplus, 1)
                    dve.wait_ge(softplus, 4 * b + 1)
                    dve.wait_ge(dt_act, 4 * b + 2)
                    dve.tensor_tensor(tdt[:, :, :], qdt[:, :, :], lnw[:, :, :], ALU.mult).then_inc(softplus, 1)
                    dve.wait_ge(softplus, 4 * b + 2)
                    dve.tensor_tensor(sdt[:, :, :], tdt[:, :, :], t2[:, :, :], ALU.add).then_inc(softplus, 1)
                    dve.wait_ge(softplus, 4 * b + 3)
                    dve.tensor_tensor(dt[:, :, :], sdt[:, :, :], mdt[:, :, :], ALU.add).then_inc(softplus, 1)
                    dve.wait_ge(softplus, 4 * b + 4)
                    dve.tensor_tensor(dA[:, :, :], dt[:, :, :], wide(neg_a[:, :]), ALU.mult).then_inc(dts, 1)
                    for f in range(NF):
                        dve.wait_ge(feat_out, NF * b + f + 1)
                        n = 4 * (NF * b + f)
                        if f >= 2:
                            dve.wait_ge(conv_out, NF * b + f - 1)
                        else:
                            dve.wait_ge(conv_out, NF * b)
                        dve.tensor_scalar(ca[:, f % 2, :], cv[:, f, 0:S], conv_w[:, f, 0:1], None,
                                          ALU.mult).then_inc(conv, 1)
                        for j in range(1, 4):
                            dve.wait_ge(conv, n + j)
                            dve.scalar_tensor_tensor(ca[:, f % 2, :], cv[:, f, j:j + S], conv_w[:, f, j:j + 1],
                                                     ca[:, f % 2, :], ALU.mult, ALU.add).then_inc(conv, 1)
                        if f == 1:
                            dve.wait_ge(dt_act, 4 * b + 3)
                            dve.tensor_copy(csum[:, :, :], ps[:, bank_small, 8:16].rearrange("p (t h) -> p t h", h=2)
                                            ).then_inc(dts, 1)
                            dve.wait_ge(dts, d0 + 9)
                            dve.tensor_tensor(dif[:, :, :], ps[:, bank_small, 16:24].rearrange("p (t h) -> p t h", h=2),
                                              csum[:, :, :], ALU.subtract).then_inc(dts, 1)
                    dve.wait_ge(dt_act, 4 * b + 4)
                    dve.tensor_tensor(dec[:, :, :], dec0[:, :, :], dt[:, :, :], ALU.mult).then_inc(dts, 1)
                    dve.wait_ge(dts, d0 + 11)
                    dve.wait_ge(tm_out, 2 * b + 2)
                    for c in range(TB):
                        q = TB * b + c
                        dve.wait_ge(row_done, q + 1)
                        for h in range(2):
                            dve.scalar_tensor_tensor(dd[:, h, :], ps[:, bank_small, P * h:P * (h + 1)],
                                                     csum[:, c, h:h + 1], cap[:, :], ALU.subtract, ALU.min
                                                     ).then_inc(dd_done, 1)
                        dve.wait_ge(y_done, q)
                        for h in range(2):
                            dve.tensor_scalar(xd[:, h, :], xtm[:, c, :], dec[:, c, h:h + 1], None, ALU.mult)
                            ins = dve.tensor_scalar(t0[:, h, :], xtm[:, c, :], heads[:, 2, h:h + 1], None, ALU.mult)
                        ins.then_inc(xd_done, 1)
                        dve.wait_ge(ee_done, q + 1)
                        dve.wait_ge(g_done, q + 1)
                        for h in range(2):
                            ins = dve.scalar_tensor_tensor(mm[:, h, :], ps[:, c % 2, P * h:P * (h + 1)],
                                                           dt[:, c, h:h + 1], ee[:, h, :], ALU.mult, ALU.mult)
                        ins.then_inc(mm_done, 1)
                        if c < TB - 1:
                            dve.wait_ge(s_done, 3 * b + c + 1)
                            new, old = state[:, (c + 1) % 2], state[:, c % 2]
                            for h in range(2):
                                src = ps[:, 4, P * h:P * (h + 1)]
                                if c == 0:
                                    ins = dve.tensor_copy(new[:, h, :], src)
                                else:
                                    ins = dve.scalar_tensor_tensor(new[:, h, :], old[:, h, :], etot[:, c, h:h + 1], src,
                                                                   ALU.mult, ALU.add)
                            ins.then_inc(st_done, 1)
                        dve.wait_ge(y_done, q + 1)
                        dve.wait_ge(xd_done, q + 1)
                        yd = ps[:, 2 + c % 2, 0:2 * P]
                        flat = (lambda v: v[:, :, :].rearrange("p h n -> p (h n)"))
                        if c > 0:
                            for h in range(2):
                                ins = dve.scalar_tensor_tensor(y1[:, h, :], ps[:, 2 + c % 2, P * (2 + h):P * (3 + h)],
                                                               ecs[:, c, h:h + 1], t0[:, h, :], ALU.mult, ALU.add)
                            ins.then_inc(ys, 1)
                            dve.wait_ge(ys, 7 * b + 2 * c)
                            dve.tensor_tensor(flat(y2), yd, flat(y1), ALU.add).then_inc(ys, 1)
                            dve.wait_ge(ys, 7 * b + 2 * c + 1)
                        else:
                            dve.tensor_tensor(flat(y2), yd, flat(t0), ALU.add).then_inc(ys, 1)
                            dve.wait_ge(ys, 7 * b + 1)
                        dve.tensor_tensor(yg[:, c, :], flat(y2), sz[:, c, :], ALU.mult).then_inc(yg_done, 1)

                    def norm(i, src, dst):
                        dve.wait_ge(sq_done, 2 * TB * b + TB * (i + 1))
                        dve.tensor_scalar(ms[:, :], ss[:, :], 1.0 / D, EPS, ALU.mult, ALU.add).then_inc(norm_v, 1)
                        dve.wait_ge(rq_ready, 2 * b + i + 1)
                        for t in range(TB):
                            ins = dve.tensor_scalar(dst[:, t, :], src[:, t, :], rq[:, t:t + 1], None, ALU.mult)
                        ins.then_inc(hn_ready, 1)

                    norm(0, yg, hn)
                    low(1)
                    for i in range(2):
                        dve.wait_ge(o_done, 2 * b + i + 1)
                        v = xh[:, 2 * i:2 * i + 2, :].rearrange("p t d -> p (t d)")
                        dve.tensor_tensor(v, ps[:, i, :], v, ALU.add).then_inc(h2_done, 1)
                    norm(1, xh, hn)
                    low(2)
                    for u in range(2):
                        n = IT * 2 * b + IT * u
                        for i in range(IT + 1):
                            if i < IT:
                                dve.wait_ge(sil_done, n + i + 1)
                                if i >= 3:
                                    dve.wait_ge(h_low, n + i - 2)
                                dve.tensor_tensor(hid[:, i % 3, :], sil[:, i % 3, :], ps[:, i % 3, C:2 * C],
                                                  ALU.mult).then_inc(hid_done, 1)
                            if i > 0:
                                dve.wait_ge(h_high, n + i)
                                dve.tensor_tensor(h_l[:, i - 1, :], hid[:, (i - 1) % 3, :],
                                                  h_h[:, i - 1, :].bitcast(F32), ALU.subtract).then_inc(h_low, 1)
                        dve.wait_ge(down_done, 2 * b + u + 1)
                        dve.wait_ge(r2_done, b + 1)
                        dve.tensor_tensor(X[:, bass.ds(TB * b + U * u, U), :], ps[:, 3:5, 0:D], xb[:, U * u:U * u + U, :],
                                          ALU.add).then_inc(added, 1)
                    dve.wait_ge(added, 2 * (b + 1))

            @block.tensor
            def _(pe):
                pe.wait_ge(w_low, 5)
                pe.wait_ge(set_up, 2)
                with pe.Fori(0, B) as b:

                    def transposes(n, before):
                        pe.wait_ge(hn_ready, 3 * b + n + 1)
                        before()
                        for k in range(KD):
                            for t in range(TB):
                                ins = pe.transpose(t_banks(k)[:, P * t:P * (t + 1)], hn[:, t, P * k:P * (k + 1)],
                                                   ident[:, :])
                            ins.then_inc(t_filled, 1)
                        pe.wait_ge(t_low, 6 * b + 2 * (n + 1))

                    transposes(0, lambda: pe.wait_ge(added, 2 * b))
                    rows = (lambda k, at: (ht_h[:, k, at:at + P], ht_l[:, k, at:at + P]))
                    cols = (lambda w, k, lo, hi: (w[0][:, k, lo:hi], w[1][:, k, lo:hi]))
                    for t in range(TB):
                        for k in range(KD):
                            ins = product(pe, ps[:, bank_small, 2 * t:2 * t + 2], rows(k, P * t),
                                          cols(win, k, PROJ - 2, PROJ), k == 0, k == KD - 1)
                    ins.then_inc(dt_filled, 1)
                    for f in range(NF):
                        for k in range(KD):
                            at = D + P * f
                            ins = product(pe, ps[:, f, :], cols(win, k, at, at + P),
                                          (ht_h[:, k, :], ht_l[:, k, :]), k == 0, k == KD - 1)
                        ins.then_inc(feat, 1)
                    for i in range(2):
                        for t in range(2):
                            for k in range(KD):
                                ins = product(pe, t_banks(i)[:, D * t:D * (t + 1)], rows(k, P * (2 * i + t)),
                                              cols(win, k, 0, D), k == 0, k == KD - 1)
                        ins.then_inc(z_filled, 1)
                    pe.wait_ge(dts, 11 * b + 8)
                    flat = dA[:, :, :].rearrange("p t h -> p (t h)")
                    pe.matmul(ps[:, bank_small, 8:16], upper, flat, start=True, stop=True).then_inc(sums, 1)
                    pe.matmul(ps[:, bank_small, 16:24], ones, flat, start=True, stop=True).then_inc(sums, 1)
                    for i in range(2):
                        pe.wait_ge(z_out, 2 * b + i + 1)
                        pe.wait_ge(conv_out, NF * b + i + 1)
                        for t in range(TB):
                            ins = pe.transpose(t_banks(i)[:, P * t:P * (t + 1)], xc[:, i, P * t:P * (t + 1)], ident[:, :])
                        ins.then_inc(tm_filled, 1)
                    pe.wait_ge(conv_out, NF * (b + 1))
                    pe.wait_ge(feat_out, NF * (b + 1))
                    pe.wait_ge(dts, 11 * b + 10)
                    for c in range(TB):
                        q = TB * b + c
                        ch = slice(P * c, P * (c + 1))
                        pe.wait_ge(dd_done, 2 * q)
                        for h in range(2):
                            ins = pe.matmul(ps[:, bank_small, P * h:P * (h + 1)],
                                            dA[:, c, h:h + 1].to_broadcast([P, P]), upper, start=True, stop=True)
                        ins.then_inc(row_done, 1)
                        if c >= 2:
                            pe.wait_ge(mm_done, q - 1)
                        pe.matmul(ps[:, c % 2, 0:2 * P], xc[:, 1, ch], xc[:, 2:4, ch], start=True,
                                  stop=True).then_inc(g_done, 1)
                        if c >= 2:
                            pe.wait_ge(yg_done, q - 1)
                        if c > 0:
                            pe.wait_ge(st_done, 3 * b + c)
                            for h in range(2):
                                pe.matmul(ps[:, 2 + c % 2, P * (2 + h):P * (3 + h)], xc[:, 2 + h, ch],
                                          state[:, c % 2, h, :], start=True, stop=True)
                        if c < TB - 1:
                            pe.wait_ge(xd_done, q + 1)
                            pe.wait_ge(tm_out, 2 * (b + 1))
                            pe.matmul(ps[:, 4, 0:2 * P], btm[:, c, :], xd[:, :, :], start=True, stop=True).then_inc(s_done, 1)
                        pe.wait_ge(mm_done, q + 1)
                        for h in range(2):
                            ins = pe.matmul(ps[:, 2 + c % 2, P * h:P * (h + 1)], mm[:, h, :], xtm[:, c, :], start=True,
                                            stop=True)
                        ins.then_inc(y_done, 1)
                    transposes(1, lambda: None)
                    pe.wait_ge(mm_done, TB * (b + 1))
                    for i in range(2):
                        for t in range(2):
                            for k in range(KD):
                                ins = product(pe, ps[:, i, D * t:D * (t + 1)], rows(k, P * (2 * i + t)),
                                              cols(wout, k, 0, D), k == 0, k == KD - 1)
                        ins.then_inc(o_done, 1)
                    transposes(2, lambda: None)
                    for u in range(2):
                        n = IT * 2 * b + IT * u
                        for i in range(IT + 2):
                            if i < IT:
                                pe.wait_ge(hid_done, n + max(i - 2, 0))
                                for j, w in enumerate((w1, w3)):
                                    for k in range(KD):
                                        ins = product(pe, ps[:, i % 3, C * j:C * (j + 1)], cols(w, k, P * i, P * (i + 1)),
                                                      (ht_h[:, k, C * u:C * (u + 1)], ht_l[:, k, C * u:C * (u + 1)]),
                                                      k == 0, k == KD - 1)
                                ins.then_inc(up_done, 1)
                            if i >= 2:
                                d = i - 2
                                if d == 0:
                                    pe.wait_ge(added, 2 * b + u)
                                pe.wait_ge(h_low, n + d + 1)
                                for t in range(U):
                                    ins = product(pe, ps[:, 3 + t, 0:D],
                                                  (h_h[:, d, P * t:P * (t + 1)], h_l[:, d, P * t:P * (t + 1)]),
                                                  (w2[0][:, d, :], w2[1][:, d, :]), d == 0, d == IT - 1)
                        ins.then_inc(down_done, 1)
        m.close()


def build(nc, a, out, stages=4):
    with ExitStack() as ctx:
        m = Memory(nc, ctx, "all")
        X = m.sb("x", [P, TILES, D])
        banks = ctx.enter_context(nc.psum_tensor("banks", [P, 8, S], F32))
        ident = m.sb("ident", [P, P])
        upper, ones = m.sb("upper", [P, P]), m.sb("ones", [P, P])
        rank, first_slot = m.sb("rank", [P, TB, E]), m.sb("first_slot", [P, TB, E])
        zero_rows = m.sb("zero_rows", [P, D])
        loaded, stored, zeroed, zero_set = m.sem("loaded"), m.sem("stored"), m.sem("zeroed"), m.sem("zero_set")
        xd = [nc.dram_tensor(f"dispatched{i}", (E * C, D), F32, kind="Internal").ap() for i in range(2)]
        oe = [nc.dram_tensor(f"expert_rows{i}", (E * C, D), F32, kind="Internal").ap() for i in range(2)]
        consts = (upper[:, :], ones[:, :], rank[:, :, :], first_slot[:, :, :])
        with nc.Block() as block:

            @block.sync
            def _(sp):
                sp.dma_start(ident[:, :], a["ident"]).then_inc(loaded, 16)
                sp.dma_start(upper[:, :], a["upper"]).then_inc(loaded, 16)
                sp.dma_start(ones[:, :], a["ones"]).then_inc(loaded, 16)
                sp.dma_start(rank[:, :, :], a["rank"]).then_inc(loaded, 16)
                sp.dma_start(first_slot[:, :, :], a["first_slot"]).then_inc(loaded, 16)
                sp.wait_ge(zero_set, 1)
                for i in range(2):
                    for r in range(E * C // P):
                        sp.dma_start(xd[i][P * r:P * (r + 1), :], zero_rows[:, :]).then_inc(zeroed, 16)
                sp.wait_ge(loaded, 16 * 5)
                sp.wait_ge(zeroed, 16 * 2 * (E * C // P))

            @block.vector
            def _(dve):
                dve.memset(zero_rows[:, :], 0.0).then_inc(zero_set, 1)

        if stages >= 1:
            attention_stage(nc, a["x"], a["wqkv"], a["wo"], a["rope"], X, ident, banks)
        if stages >= 2:
            experts_stage(nc, "moe1", a["w13"], a["w2a"], a["w2b"], a["wg"], X, ident, consts, xd[0], oe[0], banks)
        if stages >= 3:
            state_space_stage(nc, a, X, ident, consts, banks)
        if stages >= 4:
            experts_stage(nc, "moe2", a["w13"], a["w2a"], a["w2b"], a["wg"], X, ident, consts, xd[1], oe[1], banks)
        with nc.Block() as block:

            @block.sync
            def _(sp):
                sp.dma_start(out.rearrange("b (t p) d -> p (b t) d", p=P), X[:, :, :]).then_inc(stored, 16)
                sp.wait_ge(stored, 16)


def layout(inputs):
    g = {k.removeprefix("L0_"): np.asarray(v) for k, v in inputs.items()}
    arrays = {"x": g["attn_a_x"]}
    heads = [2 * (2 * m + half) + r for m in range(NKV // 2) for r in range(2) for half in range(2)]
    halves = [d for p in range(2) for d in range(p, HD, 2)]
    qcols = [HD * h + d for h in heads for d in halves]
    kcols = [HD * j + d for j in range(NKV) for d in halves]
    arrays["wqkv"] = np.concatenate([g["attn_a_wq"][:, qcols], g["attn_a_wk"][:, kcols], g["attn_a_wv"]], axis=1)
    arrays["wo"] = g["attn_a_wo"]
    f = np.float32
    inv = f(1.0) / (f(10000.0) ** (np.arange(0, HD, 2, dtype=f) / f(HD)))
    ang = np.arange(S, dtype=f)[:, None] * inv[None, :]
    arrays["rope"] = np.stack([np.tile(np.cos(ang), 2), np.tile(np.sin(ang), 2)], axis=1).astype(f)
    arrays["ident"] = np.eye(P, dtype=f)
    arrays["upper"] = np.triu(np.ones((P, P), f))
    arrays["ones"] = np.ones((P, P), f)
    arrays["rank"] = np.broadcast_to(np.arange(E, 0, -1, dtype=f), (P, TB, E))
    arrays["first_slot"] = np.broadcast_to(np.arange(E, dtype=f) * C - 1, (P, TB, E))
    w1 = np.concatenate([g["ffn_W1"], g["ffn_sw1"][None]]).reshape(E + 1, KD, P, H)
    w3 = np.concatenate([g["ffn_W3"], g["ffn_sw3"][None]]).reshape(E + 1, KD, P, H)
    w2 = np.concatenate([g["ffn_W2"], g["ffn_sw2"][None]])
    arrays["w13"] = np.stack([w1, w3], axis=3).transpose(0, 2, 1, 3, 4).reshape(E + 1, P, 2 * KD * H)
    arrays["w2a"] = w2[:, :2 * P].reshape(E + 1, 2, P, D).transpose(0, 2, 1, 3).reshape(E + 1, P, 2 * D)
    arrays["w2b"] = w2[:, 2 * P:]
    arrays["wg"] = g["ffn_Wg"]
    arrays["win"], arrays["wout"] = g["attn_b_W_in"], g["attn_b_W_out"]
    arrays["w1"], arrays["w3"], arrays["w2"] = g["attn_b_w1"], g["attn_b_w3"], g["attn_b_w2"]
    arrays["norms"] = np.stack([g["attn_b_ln1_w"], g["attn_b_norm_w"], g["attn_b_ln2_w"]]
                               ).reshape(3, KD, P).transpose(2, 0, 1)
    arrays["conv_w"] = g["attn_b_conv_w"].reshape(4, 4, P).transpose(2, 1, 0)
    arrays["conv_b"] = g["attn_b_conv_b"].reshape(4, P).T
    arrays["heads"] = np.concatenate([g["attn_b_dt_bias"], g["attn_b_A_log"], g["attn_b_D"]])
    arrays["cap"] = np.tril(np.full((P, P), -1e30, f), -1)
    return {k: np.ascontiguousarray(v) for k, v in arrays.items()}


def kernel(**inputs):
    import concourse.bacc as bacc
    from concourse.bass_utils import run_bass_kernel_spmd

    nc = bacc.Bacc("TRN2", target_bir_lowering=False, num_devices=1)
    arrays = layout(inputs)
    aps = {k: nc.dram_tensor(f"in_{k}", v.shape, mybir.dt.from_np(v.dtype), kind="ExternalInput").ap()
           for k, v in arrays.items()}
    out = nc.dram_tensor("out_x", (B, S, D), F32, kind="ExternalOutput").ap()
    build(nc, aps, out)
    r = run_bass_kernel_spmd(nc, [{f"in_{k}": v for k, v in arrays.items()}], core_ids=[0])
    return r.results[0]["out_x"]
```

```python
from contextlib import ExitStack

import numpy as np

import concourse.bass as bass
from concourse import mybir

F32 = mybir.dt.float32
F32R = mybir.dt.float32r
U32 = mybir.dt.uint32
ALU = mybir.AluOpType
ACT = mybir.ActivationFunctionType
AX_X = mybir.AxisListType.X

P = 128
B, S, D = 4, 512, 256
KD = D // P
TB = S // P
TILES = B * TB
NH, NKV, HD = 16, 8, 16
QC, KC = NH * HD, NKV * HD
SLOTS = 4
PACKS = NH // 2
E, H, C = 8, 352, 256
HT = [P, P, H - 2 * P]
U = C // P
UNITS = TILES // U
XB, DI, INTER = 128, 256, 1024
PROJ = 2 * DI + 2 * XB + 2
IT = INTER // P
EPS = 1e-5
AHEAD = 1


class Ring:

    def __init__(self, size, first, body, last, owner, steps=None):
        self.size, self.uses, self.owner = size, {"first": first, "body": body, "last": last}, owner
        self.steps = steps or {}
        assert len(first) % size == 0 and len(body) % size == 0

    def increments(self, names, owner):
        return sum(self.steps.get(owner, 1) for n in names if self.owner(n) == owner)

    def before(self, phase, owner):
        kind, it = phase
        if kind == "first":
            return 0
        return self.increments(self.uses["first"], owner) + self.increments(self.uses["body"], owner) * it

    def index(self, phase, name):
        return self.uses[phase[0]].index(name)

    def slot(self, phase, name):
        return self.index(phase, name) % self.size

    def filled(self, phase, name):
        kind, it = phase
        n = self.index(phase, name) + 1
        return n if kind == "first" else len(self.uses["first"]) + len(self.uses["body"]) * it + n

    def emptied(self, phase, name, owner):
        i = self.index(phase, name)
        return AHEAD + self.before(phase, owner) + self.increments(self.uses[phase[0]][:i + 1], owner)

    def wait_free(self, eng, sems, phase, name):
        i = self.index(phase, name)
        if i >= self.size:
            last = self.uses[phase[0]][i - self.size]
            o = self.owner(last)
            eng.wait_ge(sems[o], self.emptied(phase, last, o))
        elif phase[0] != "first":
            tails = [self.uses[k][len(self.uses[k]) - self.size + i:] for k in ("first", "body")]
            o = self.owner(tails[0][0])
            if o == self.owner(tails[1][0]):
                late = [self.increments(t[1:], o) for t in tails]
                assert late[0] == late[1]
                eng.wait_ge(sems[o], AHEAD + self.before(phase, o) - late[0])
            else:
                for o in (o, self.owner(tails[1][0])):
                    eng.wait_ge(sems[o], AHEAD + self.before(phase, o))


def product(pe, out, a, b, first, last):
    pe.matmul(out, a[0], b[0], start=first, stop=False)
    pe.matmul(out, a[0], b[1], start=False, stop=False)
    return pe.matmul(out, a[1], b[0], start=False, stop=last)


class Memory:

    def __init__(self, nc, ctx, stage, banks=None):
        self.nc, self.ctx, self.stage, self.banks, self.used = nc, ctx, stage, banks, 0
        self.sems, self.ahead = [], []

    def sb(self, name, shape, dt=F32):
        return self.ctx.enter_context(self.nc.sbuf_tensor(f"{self.stage}_{name}", shape, dt))

    def pair(self, name, shape):
        return self.sb(name + "_hi", shape, F32R), self.sb(name + "_lo", shape, F32R)

    def psum(self, shape):
        n = int(np.prod(shape[1:])) // S
        v = self.banks[:, self.used:self.used + n, :]
        self.used += n
        assert self.used <= 8
        if len(shape) == 4:
            return v.rearrange("p b n -> p (b n)").rearrange("p (x y z) -> p x y z", x=shape[1], y=shape[2])
        return v if len(shape) == 3 else v[:, 0, :]

    def sem(self, name, keep=False, ahead=False):
        h = self.nc.alloc_semaphore(f"{self.stage}_{name}")
        if ahead:
            self.ahead.append(h)
        if not keep:
            self.sems.append(h)
        return h

    def open(self):
        for h in self.ahead:
            self.nc.gpsimd.sem_inc(h, AHEAD)
        self.nc.all_engine_barrier()

    def close(self):
        self.nc.clear_and_free_semaphores(self.sems)
        self.nc.all_engine_barrier()


class RowStats:

    def __init__(self, m, name, n):
        self.n = n
        self.stats = m.sb(name + "_stats", [P, n, 6])
        self.tmp = m.sb(name + "_tmp", [P, 5, n])
        self.mean = m.sb(name + "_mean", [P, n])
        self.ve = m.sb(name + "_ve", [P, n])
        self.done = m.sem(name + "_done")
        self.steps = n + 7

    def run(self, dve, it, rows):
        n, s, done, base = self.n, self.stats, self.done, self.steps * it
        tot, dif, m2, q, m2e = (self.tmp[:, i, :] for i in range(5))
        for t in range(n):
            dve.bn_stats(s[:, t, :], rows(t)).then_inc(done, 1)
        dve.wait_ge(done, base + n)
        dve.tensor_tensor(tot, s[:, :, 1], s[:, :, 4], ALU.add).then_inc(done, 1)
        dve.tensor_tensor(dif, s[:, :, 1], s[:, :, 4], ALU.subtract).then_inc(done, 1)
        dve.tensor_tensor(m2, s[:, :, 2], s[:, :, 5], ALU.add).then_inc(done, 1)
        dve.wait_ge(done, base + n + 3)
        dve.tensor_scalar(self.mean[:, :], tot, 0.5, None, ALU.mult).then_inc(done, 1)
        dve.scalar_tensor_tensor(q, dif, 0.25, dif, ALU.mult, ALU.mult).then_inc(done, 1)
        dve.tensor_scalar(m2e, m2, 1.0 / D, EPS, ALU.mult, ALU.add).then_inc(done, 1)
        dve.wait_ge(done, base + n + 6)
        dve.tensor_tensor(self.ve[:, :], q, m2e, ALU.add).then_inc(done, 1)


def attention_stage(nc, x_dram, wqkv, wo, rope, X, ident, banks, xd, zero_rows, zeroed):
    with ExitStack() as ctx:
        m = Memory(nc, ctx, "attn", banks)
        sb, sem = m.sb, m.sem
        w_in = sb("w_in", [P, KD, 2 * D])
        w_h, w_l = m.pair("wqkv", [P, KD, 2 * D])
        wo_in = sb("wo_in", [P, KD, D])
        wo_h, wo_l = m.pair("wo", [P, KD, D])
        cs = sb("rope", [P, TB, 2, HD])
        xb = sb("xb", [P, TB, D])
        ln = RowStats(m, "ln", TB)
        rstd = sb("rstd", [P, TB])
        nhalf = sb("nhalf", [P, TB])
        xn = sb("xn", [P, TB, D])
        xt_h, xt_l = m.pair("xt", [P, KD, S])
        rc = sb("rc", [P, 2, 24, HD])
        rs = sb("rs", [P, 2, 24, HD])
        qk = sb("qk", [P, TB, 24, HD])
        st = sb("st", [P, TB, 24, SLOTS, HD])
        vn = sb("vn", [P, TB, NKV, HD])
        v = sb("v", [P, TB, NKV, 32])
        qp = sb("qp", [P, PACKS, S], F32R)
        kz = sb("kz", [P, NKV, S], F32R)
        nm = sb("nm", [P, TB, NH])
        pt = sb("pt", [P, 3, 4, S])
        ot = sb("ot", [P, 2, S])
        rec = sb("rec", [P, 2, TB, 4])
        ao = sb("ao", [P, TB, D])
        at_h, at_l = m.pair("at", [P, KD, S])

        ps_ring = m.psum([P, 2, 2, S])
        ps_sc = m.psum([P, 2, S])
        ps_pv = m.psum([P, S])
        ps_m = m.psum([P, S])

        w_loaded, wo_loaded, c_loaded, x_loaded = sem("w_loaded"), sem("wo_loaded"), sem("c_loaded"), sem("x_loaded")
        set_up, w_act, w_split = sem("set_up"), sem("w_act"), sem("w_split")
        kz_zeroed, nhalf_set = sem("kz_zeroed"), sem("nhalf_set")
        xb_copied, rstd_ready, xn_ready = sem("xb_copied"), sem("rstd_ready"), sem("xn_ready", ahead=True)
        filled = sem("filled")
        emptied = {"dve": sem("emptied_dve", ahead=True), "act": sem("emptied_act", ahead=True)}
        xt_hi = sem("xt_hi")
        v_copied, rotated, qk_ready = sem("v_copied"), sem("rotated", ahead=True), sem("qk_ready", ahead=True)
        v_moved = sem("v_moved")
        emptied["rot"] = rotated
        spare_zeroed = sem("spare_zeroed")
        k_hi, k_low, k_copied = sem("k_hi"), sem("k_low", ahead=True), sem("k_copied")
        q_hi, q_low, q_copied = sem("q_hi"), sem("q_low", ahead=True), sem("q_copied")
        aux0, aux1 = sem("aux0"), sem("aux1", ahead=True)
        m_filled = sem("m_filled")
        m_emptied = {"dve": sem("m_emptied_dve", ahead=True), "act": sem("m_emptied_act", ahead=True)}
        at_hi = sem("at_hi")
        sc_filled, exp_done, pv_done, ot_copied, rec_ready = (
            sem("sc_filled"), sem("exp_done", ahead=True), sem("pv_done", ahead=True), sem("ot_copied", ahead=True),
            sem("rec_ready"))

        STEPS, UNIT, LEAD = 16, 8, 10
        EARLY = {13: (0, 1), 14: (2, 3), 15: (4, 5)}
        LATE = ((6, 7), (8, 9))
        HEAD = 3
        END = {0: ("at0",), 1: ("at1",), 2: ("wo0", "wo1")}
        ENDS = [n for s in range(HEAD) for n in END[s]]
        units = [f"max{n}" for n in range(4 * UNIT)]
        NORM, SCALE, TURN, PROJECT, KEYS, PARTS = 3, 4, 5, (6, 8), (7, 9), 11
        PACKED = {10: ("k0",), 12: ("q0", "q1"), 13: ("q2",)}
        PACKED_LAST = ("k1", "q3")

        def step_units(s):
            return range(LEAD + 2 * s, min(LEAD + 2 * s + 2, 4 * UNIT))

        head = [units[n] for s in range(HEAD) for n in step_units(s)]
        first = ["xt0", "xt1", "qkv0", "qkv1", "k0", "q0", "k1", "q1", "q2", "q3"] + units[:LEAD] + head
        body, last = [], []
        for s in range(HEAD, STEPS):
            body += [units[n] for n in step_units(s)]
            last += [units[n] for n in step_units(s)]
            if s == TURN:
                body += ["xt0", "xt1"]
            if s in PROJECT:
                body += [f"qkv{PROJECT.index(s)}"]
            body += PACKED.get(s, ())
            body += [units[n] for n in EARLY.get(s, ())]
        body += list(PACKED_LAST) + [units[n] for ns in LATE for n in ns] + head
        OWNER = {"qkv0": "rot", "qkv1": "rot", "k0": "act", "q1": "act", "q3": "act"}
        ring = Ring(2, first, body, last, lambda n: OWNER.get(n, "dve"), {"rot": 4})
        last = []
        for g in range(4):
            if g > 0:
                last += [f"ot{g - 1}"]
            if g < 3:
                last += [f"retr{g + 1}a", f"retr{g + 1}b"]
        last += ["ot3"]
        misc = Ring(1, ["retr0a", "retr0b"], last + ["retr0a", "retr0b"] + ENDS, last + ENDS,
                    lambda n: "act" if n.startswith("retr") else "dve")

        def rows(eng, body):
            with eng.Fori(0, B - 1) as b:
                body(("body", b), b, False)
            body(("last", B - 1), B - 1, True)

        FIRST = ("first", 0)

        m.open()
        with nc.Block() as block:

            @block.sync
            def _(sp):
                for b in range(B):
                    if b > 0:
                        sp.wait_ge(x_loaded, 16 * b)
                    sp.dma_start(X[:, TB * b:TB * (b + 1), :],
                                 x_dram[b].rearrange("(t p) d -> p t d", p=P)).then_inc(x_loaded, 16)
                    if b == 0:
                        sp.dma_start(w_in[:, :, :], wqkv.rearrange("(k p) n -> p k n", p=P)).then_inc(w_loaded, 16)
                        sp.dma_start(cs[:, :, :, :], rope.rearrange("(t p) a n -> p t a n", p=P)).then_inc(c_loaded, 16)
                        sp.dma_start(wo_in[:, :, :], wo.rearrange("(k p) n -> p k n", p=P)).then_inc(wo_loaded, 16)
                for dst in xd:
                    sp.dma_start(dst.rearrange("(r p) d -> p r d", p=P),
                                 zero_rows[:, :].unsqueeze(1).to_broadcast([P, E * C // P, D])).then_inc(zeroed, 16)
                sp.wait_ge(x_loaded, 16 * B)

            @block.gpsimd
            def _(pool):
                pool.memset(nhalf[:, :], -0.5).then_inc(nhalf_set, 1)
                pool.wait_ge(nhalf_set, 1)

                def power(r):
                    pool.wait_ge(ln.done, ln.steps * (r + 1))
                    pool.wait_ge(xn_ready, AHEAD + TB * r)
                    pool.tensor_tensor(rstd[:, :], ln.ve[:, :], nhalf[:, :], ALU.pow).then_inc(rstd_ready, 1)

                def rotation_sums(r, i):
                    for t in (2 * i, 2 * i + 1):
                        pool.wait_ge(rotated, AHEAD + 2 * (TB * r + t) + 2)
                        pool.wait_ge(q_low, AHEAD + TB * r)
                        pool.tensor_tensor(qk[:, t, :, 0:8], rc[:, t % 2, :, 0:8], rs[:, t % 2, :, 8:16],
                                           ALU.subtract).then_inc(qk_ready, 1)
                        pool.tensor_tensor(qk[:, t, :, 8:16], rs[:, t % 2, :, 0:8], rc[:, t % 2, :, 8:16],
                                           ALU.add).then_inc(qk_ready, 1)

                def key_low_parts(r, i):
                    for t in (2 * i, 2 * i + 1):
                        pool.wait_ge(k_hi, TB * r + t + 1)
                        pool.tensor_tensor(st[:, t, NH:24, 2, :], qk[:, t, NH:24, :], st[:, t, NH:24, 0, :],
                                           ALU.subtract).then_inc(k_low, 1)

                def prepare(r):
                    power(r)
                    for i in range(2):
                        rotation_sums(r, i)
                        key_low_parts(r, i)

                prepare(0)
                with pool.Fori(0, B - 1) as b:
                    prepare(b + 1)

            @block.scalar
            def _(act):
                act.wait_ge(w_loaded, 16)
                act.activation(w_h[:, :, :], w_in[:, :, :], ACT.Copy).then_inc(w_act, 1)

                def turned(phase, r):
                    for k in range(KD):
                        act.wait_ge(filled, ring.filled(phase, f"xt{k}"))
                        act.activation(xt_h[:, k, :], ps_ring[:, ring.slot(phase, f"xt{k}"), 0, :],
                                       ACT.Copy).then_inc(xt_hi, 1)

                def values(phase, r, i):
                    act.wait_ge(filled, ring.filled(phase, f"qkv{i}"))
                    act.activation(vn[:, 2 * i:2 * i + 2, :, :],
                                   ps_ring[:, ring.slot(phase, f"qkv{i}"), :, QC + KC:].rearrange(
                                       "p t (j d) -> p t j d", d=HD), ACT.Copy).then_inc(v_copied, 1)

                def key_copies(r, i):
                    for t in (2 * i, 2 * i + 1):
                        act.wait_ge(k_hi, TB * r + t + 1)
                        act.activation(st[:, t, NH:24, 1, :], st[:, t, NH:24, 0, :], ACT.Copy).then_inc(k_copied, 1)

                def query_copies(r):
                    for t in range(TB):
                        act.wait_ge(q_hi, TB * r + t + 1)
                        act.activation(st[:, t, 0:NH, 2, :], st[:, t, 0:NH, 0, :], ACT.Copy).then_inc(q_copied, 1)

                def pack(phase, names):
                    for name in names:
                        if OWNER.get(name) == "act":
                            act.wait_ge(filled, ring.filled(phase, name))
                            src = ps_ring[:, ring.slot(phase, name), :, :]
                            if name == "k0":
                                act.activation(kz[0:64, 0:4:2, :], src[0:64], ACT.Copy)
                                act.activation(kz[64:P, 1:4:2, :], src[64:P], ACT.Copy).then_inc(emptied["act"], 1)
                            else:
                                n = 2 * int(name[1])
                                act.activation(qp[:, n:n + 2, :], src, ACT.Copy).then_inc(emptied["act"], 1)

                def move_values(r):
                    act.wait_ge(v_copied, 2 * (r + 1))
                    act.wait_ge(pv_done, AHEAD + STEPS * r)
                    act.activation(v[:, :, :, 0:HD], vn[:, :, :, :], ACT.Copy).then_inc(v_moved, 1)

                def requery(phase, g, j):
                    act.wait_ge(m_filled, misc.filled(phase, f"retr{g}{'ab'[j]}"))
                    act.activation(qp[:, 2 * g + j, :], ps_m[:, :], ACT.Copy).then_inc(m_emptied["act"], 1)

                def copy_out(phase, b, g):
                    act.wait_ge(pv_done, AHEAD + STEPS * b + 4 * g + 4)
                    if g >= 2:
                        act.wait_ge(m_filled, misc.filled(phase, f"ot{g - 2}"))
                    act.activation(ot[:, g % 2, :], ps_pv[:, :], ACT.Copy).then_inc(ot_copied, 1)

                act.wait_ge(kz_zeroed, 1)
                act.wait_ge(set_up, 5)
                def step(phase, b, s, prepare):
                    g, kt = s // 4, s % 4
                    for a in range(4):
                        act.wait_ge(sc_filled, 64 * b + 4 * s + a + 1)
                        if a == 0:
                            act.wait_ge(pv_done, AHEAD + STEPS * b + max(s - 2, 0))
                        act.activation(pt[:, s % 3, a, :], ps_sc[:, a % 2, :], ACT.Exp,
                                       scale=HD ** -0.5).then_inc(exp_done, 1)
                        if kt == 3 and g < 3 and a in (1, 2):
                            requery(phase, g + 1, a - 1)
                    if kt == 1 and g > 0:
                        copy_out(phase, b, g - 1)
                    if prepare:
                        if s == TURN:
                            turned(phase, b + 1)
                        if s in PROJECT:
                            values(phase, b + 1, PROJECT.index(s))
                        if s in KEYS:
                            key_copies(b + 1, KEYS.index(s))
                        if s == PARTS:
                            query_copies(b + 1)
                        pack(phase, PACKED.get(s, ()))

                def end(phase, b, name):
                    if name in ("at0", "at1"):
                        k = int(name[2])
                        act.wait_ge(m_filled, misc.filled(phase, name))
                        act.activation(at_h[:, k, :], ps_m[:, :], ACT.Copy).then_inc(at_hi, 1)

                turned(FIRST, 0)
                values(FIRST, 0, 0)
                values(FIRST, 0, 1)
                key_copies(0, 0)
                key_copies(0, 1)
                query_copies(0)
                pack(FIRST, ("k0", "q0", "k1", "q1", "q2", "q3"))
                move_values(0)
                requery(FIRST, 0, 0)
                requery(FIRST, 0, 1)
                for s in range(HEAD):
                    step(FIRST, 0, s, False)
                act.wait_ge(wo_loaded, 16)
                act.activation(wo_h[:, :, :], wo_in[:, :, :], ACT.Copy).then_inc(w_act, 1)

                def row(phase, b, last):
                    for s in range(HEAD, STEPS):
                        step(phase, b, s, not last)
                    if not last:
                        pack(phase, PACKED_LAST)
                    copy_out(phase, b, 3)
                    if not last:
                        move_values(b + 1)
                        requery(phase, 0, 0)
                        requery(phase, 0, 1)
                    for s in range(HEAD):
                        if not last:
                            step(phase, b + 1, s, False)
                        for name in END[s]:
                            end(phase, b, name)

                rows(act, row)

            @block.vector
            def _(dve):

                def statistics(r):
                    dve.wait_ge(x_loaded, 16 * (r + 1))
                    dve.tensor_copy(xb[:, :, :], X[:, bass.ds(TB * r, TB), :]).then_inc(xb_copied, 1)
                    dve.wait_ge(xb_copied, r + 1)
                    ln.run(dve, r, lambda t: xb[:, t, :])

                def scale_rows(r):
                    dve.wait_ge(rstd_ready, r + 1)
                    for t in range(TB):
                        dve.tensor_scalar(xn[:, t, :], xb[:, t, :], ln.mean[:, t:t + 1], rstd[:, t:t + 1],
                                          ALU.subtract, ALU.mult).then_inc(xn_ready, 1)

                def turned(phase, r):
                    for k in range(KD):
                        dve.wait_ge(xt_hi, KD * r + k + 1)
                        dve.tensor_tensor(xt_l[:, k, :], ps_ring[:, ring.slot(phase, f"xt{k}"), 0, :],
                                          xt_h[:, k, :].bitcast(F32), ALU.subtract).then_inc(emptied["dve"], 1)

                def rotate(phase, r, i):
                    name = f"qkv{i}"
                    dve.wait_ge(filled, ring.filled(phase, name))
                    dve.wait_ge(v_copied, 2 * r + i + 1)
                    for t in (2 * i, 2 * i + 1):
                        if t >= 2:
                            dve.wait_ge(qk_ready, AHEAD + 2 * (TB * r + t - 1))
                        else:
                            dve.wait_ge(qk_ready, AHEAD + 2 * TB * r)
                        src = ps_ring[:, ring.slot(phase, name), t % 2, 0:QC + KC].rearrange(
                            "p (h d) -> p h d", d=HD)
                        dve.tensor_tensor(rc[:, t % 2, :, :], src, cs[:, t, 0:1, :].to_broadcast([P, 24, HD]),
                                          ALU.mult).then_inc(rotated, 1)
                        dve.tensor_tensor(rs[:, t % 2, :, :], src, cs[:, t, 1:2, :].to_broadcast([P, 24, HD]),
                                          ALU.mult).then_inc(rotated, 1)

                def key_parts(r, i):
                    for t in (2 * i, 2 * i + 1):
                        dve.wait_ge(qk_ready, AHEAD + 2 * (TB * r + t) + 2)
                        dve.tensor_copy(st[:, t, NH:24, 0, :].bitcast(F32R), qk[:, t, NH:24, :]).then_inc(k_hi, 1)

                def query_parts(r):
                    dve.memset(st[:, :, 0:NH, 3, 0:2], 0.0).then_inc(spare_zeroed, 1)
                    for t in range(TB):
                        dve.tensor_copy(st[:, t, 0:NH, 0, :].bitcast(F32R), qk[:, t, 0:NH, :]).then_inc(q_hi, 1)
                    for t in range(TB):
                        dve.wait_ge(q_hi, TB * r + t + 1)
                        dve.tensor_tensor(st[:, t, 0:NH, 1, :], qk[:, t, 0:NH, :], st[:, t, 0:NH, 0, :],
                                          ALU.subtract).then_inc(q_low, 1)

                def pack(phase, names):
                    for name in names:
                        if name not in OWNER:
                            dve.wait_ge(filled, ring.filled(phase, name))
                            src = ps_ring[:, ring.slot(phase, name), :, :]
                            if name == "k1":
                                dve.tensor_copy(kz[0:64, 4:8:2, :], src[0:64])
                                dve.tensor_copy(kz[64:P, 5:8:2, :], src[64:P]).then_inc(emptied["dve"], 1)
                            else:
                                n = 2 * int(name[1])
                                dve.tensor_copy(qp[:, n:n + 2, :], src).then_inc(emptied["dve"], 1)

                def maxima(phase, r, ns):
                    for n in ns:
                        i, qt = n // 2, 2 * (n % 2)
                        dve.wait_ge(filled, ring.filled(phase, units[n]))
                        if n == 0:
                            dve.wait_ge(aux1, AHEAD + 4 * r)
                        dve.tensor_reduce(nm[:, qt:qt + 2, i], ps_ring[:, ring.slot(phase, units[n]), :, :],
                                          AX_X, ALU.max, negate=True).then_inc(emptied["dve"], 1)

                def spare_rows(phase, r, g):
                    h = slice(4 * g, 4 * g + 4)
                    dve.wait_ge(emptied["dve"], ring.emptied(phase, units[UNIT * g + UNIT - 1], "dve"))
                    dve.tensor_copy(st[:, :, h, 3, 0].bitcast(F32R), nm[:, :, h]).then_inc(aux0, 1)
                    dve.wait_ge(aux0, 4 * r + g + 1)
                    dve.tensor_tensor(st[:, :, h, 3, 1], nm[:, :, h], st[:, :, h, 3, 0],
                                      ALU.subtract).then_inc(aux1, 1)

                def first_maxima(phase, r, ns):
                    maxima(phase, r, ns)
                    if UNIT - 1 in ns:
                        spare_rows(phase, r, 0)

                statistics(0)
                dve.memset(v[:, :, :, HD:32], 0.0).then_inc(set_up, 1)
                dve.memset(st[:, :, :, 3, :], 0.0).then_inc(set_up, 1)
                scale_rows(0)
                dve.memset(kz[64:P, 0:NKV:2, :].bitcast(F32), 0.0)
                dve.memset(kz[0:64, 1:NKV:2, :].bitcast(F32), 0.0).then_inc(kz_zeroed, 1)
                dve.wait_ge(set_up, 2)
                dve.memset(v[:, :, :, HD:HD + 1], 1.0).then_inc(set_up, 1)
                dve.memset(st[:, :, NH:24, 3, 0:2], 1.0).then_inc(set_up, 1)
                dve.memset(rec[:, :, :, :], 0.0).then_inc(set_up, 1)
                dve.wait_ge(set_up, 5)
                dve.wait_ge(w_act, 1)
                dve.tensor_tensor(w_l[:, :, :], w_in[:, :, :], w_h[:, :, :].bitcast(F32),
                                  ALU.subtract).then_inc(w_split, 1)
                turned(FIRST, 0)
                dve.wait_ge(c_loaded, 16)
                rotate(FIRST, 0, 0)
                rotate(FIRST, 0, 1)
                key_parts(0, 0)
                key_parts(0, 1)
                query_parts(0)
                pack(FIRST, ("k0", "q0", "k1", "q1", "q2", "q3"))
                for n in range(LEAD):
                    first_maxima(FIRST, 0, (n,))

                def normalize(phase, b, g):
                    dve.wait_ge(m_filled, misc.filled(phase, f"ot{g}"))
                    o = ps_m[:, :].rearrange("p (t a c) -> p t a c", t=TB, c=32)
                    dve.reciprocal(rec[:, g % 2, :, :], o[:, :, :, HD]).then_inc(rec_ready, 1)
                    dve.wait_ge(rec_ready, 4 * b + g + 1)
                    for t in range(TB):
                        ins = dve.tensor_tensor(
                            ao[:, t, 64 * g:64 * g + 64].rearrange("p (a d) -> p a d", d=HD), o[:, t, :, 0:HD],
                            rec[:, g % 2, t, :].unsqueeze(2).to_broadcast([P, 4, HD]), ALU.mult)
                    ins.then_inc(m_emptied["dve"], 1)

                def step(phase, b, s, prepare):
                    g, kt = s // 4, s % 4
                    maxima(phase, b, step_units(s))
                    if kt == 2 and g < 3:
                        spare_rows(phase, b, g + 1)
                    if kt == 2 and g > 0:
                        normalize(phase, b, g - 1)
                    if prepare:
                        if s == NORM:
                            statistics(b + 1)
                        if s == SCALE:
                            scale_rows(b + 1)
                        if s == TURN:
                            turned(phase, b + 1)
                        if s in PROJECT:
                            rotate(phase, b + 1, PROJECT.index(s))
                        if s in KEYS:
                            key_parts(b + 1, KEYS.index(s))
                        if s == PARTS:
                            dve.wait_ge(m_filled, misc.filled(phase, "retr3b"))
                            query_parts(b + 1)
                        pack(phase, PACKED.get(s, ()))
                        first_maxima(phase, b + 1, EARLY.get(s, ()))

                def end(phase, b, name):
                    k = int(name[2])
                    if name in ("at0", "at1"):
                        dve.wait_ge(at_hi, KD * b + k + 1)
                        dve.tensor_tensor(at_l[:, k, :], ps_m[:, :], at_h[:, k, :].bitcast(F32),
                                          ALU.subtract).then_inc(m_emptied["dve"], 1)
                    else:
                        dve.wait_ge(m_filled, misc.filled(phase, name))
                        dve.tensor_tensor(X[:, bass.ds(TB * b + 2 * k, 2), :],
                                          ps_m[:, :].rearrange("p (t d) -> p t d", t=2),
                                          X[:, bass.ds(TB * b + 2 * k, 2), :], ALU.add).then_inc(m_emptied["dve"], 1)

                for s in range(HEAD):
                    step(FIRST, 0, s, False)
                dve.wait_ge(w_act, 2)
                dve.tensor_tensor(wo_l[:, :, :], wo_in[:, :, :], wo_h[:, :, :].bitcast(F32),
                                  ALU.subtract).then_inc(w_split, 1)

                def row(phase, b, last):
                    for s in range(HEAD, STEPS):
                        step(phase, b, s, not last)
                    if not last:
                        pack(phase, PACKED_LAST)
                        first_maxima(phase, b + 1, LATE[0])
                    normalize(phase, b, 3)
                    if not last:
                        first_maxima(phase, b + 1, LATE[1])
                    for s in range(HEAD):
                        if not last:
                            step(phase, b + 1, s, False)
                        for name in END[s]:
                            end(phase, b, name)

                rows(dve, row)

            @block.tensor
            def _(pe):

                def transposes(out, cols):
                    for t in range(TB):
                        ins = pe.transpose(out[:, P * t:P * (t + 1)], cols(t), ident[:, :])
                    return ins

                def begin(phase, name):
                    ring.wait_free(pe, emptied, phase, name)
                    return ps_ring[:, ring.slot(phase, name), :, :]

                def turn(phase, r):
                    pe.wait_ge(xn_ready, AHEAD + TB * (r + 1))
                    for k in range(KD):
                        o = begin(phase, f"xt{k}")
                        transposes(o[:, 0, :], lambda t: xn[:, t, P * k:P * (k + 1)]).then_inc(filled, 1)

                def project(phase, r, i):
                    o = begin(phase, f"qkv{i}")
                    if i == 0:
                        pe.wait_ge(xt_hi, KD * (r + 1))
                        pe.wait_ge(emptied["dve"], ring.emptied(phase, "xt1", "dve"))
                    for t in range(2):
                        at = P * (2 * i + t)
                        for k in range(KD):
                            ins = product(pe, o[:, t, :], (xt_h[:, k, at:at + P], xt_l[:, k, at:at + P]),
                                          (w_h[:, k, :], w_l[:, k, :]), k == 0, k == KD - 1)
                    ins.then_inc(filled, 1)

                def pack(phase, r, names):
                    for name in names:
                        o = begin(phase, name)
                        if name == "k0":
                            pe.wait_ge(k_low, AHEAD + TB * (r + 1))
                            pe.wait_ge(k_copied, TB * (r + 1))
                        if name == "q0":
                            pe.wait_ge(q_low, AHEAD + TB * (r + 1))
                            pe.wait_ge(q_copied, TB * (r + 1))
                            pe.wait_ge(spare_zeroed, r + 1)
                        for j in range(2):
                            h = (NH if name[0] == "k" else 0) + 4 * int(name[1]) + 2 * j
                            ins = transposes(o[:, j, :],
                                             lambda t: st[:, t, h:h + 2, :, :].rearrange("p h s d -> p (h s d)"))
                        ins.then_inc(filled, 1)

                def score_rows(phase, n):
                    if n == 0:
                        for o in ("act", "dve"):
                            pe.wait_ge(emptied[o], ring.emptied(phase, "q1", o))
                    i, qt = n // 2, 2 * (n % 2)
                    o = begin(phase, units[n])
                    for q in range(2):
                        at = P * (qt + q)
                        ins = pe.matmul(o[:, q, :], qp[:, i // 2, at:at + P], kz[:, 2 * (i // 4) + i % 2, :],
                                        start=True, stop=True)
                    ins.then_inc(filled, 1)

                def all_packed(phase):
                    for o in ("act", "dve"):
                        name = [n for n in ("k0", "q0", "q1", "q2", "k1", "q3") if OWNER.get(n, "dve") == o][-1]
                        pe.wait_ge(emptied[o], ring.emptied(phase, name, o))

                def requery(phase, r, g, j):
                    if j == 0:
                        pe.wait_ge(aux1, AHEAD + 4 * r + g + 1)
                    misc.wait_free(pe, m_emptied, phase, f"retr{g}{'ab'[j]}")
                    h = 4 * g + 2 * j
                    transposes(ps_m[:, :], lambda t: st[:, t, h:h + 2, :, :].rearrange(
                        "p h s d -> p (h s d)")).then_inc(m_filled, 1)

                pe.wait_ge(set_up, 5)
                turn(FIRST, 0)
                pe.wait_ge(w_split, 1)
                project(FIRST, 0, 0)
                project(FIRST, 0, 1)
                pack(FIRST, 0, ("k0", "q0", "k1", "q1", "q2", "q3"))
                for n in range(LEAD):
                    score_rows(FIRST, n)
                all_packed(FIRST)
                requery(FIRST, 0, 0, 0)
                requery(FIRST, 0, 0, 1)

                def scores(phase, b, s):
                    g, kt = s // 4, s % 4
                    ns = step_units(s)
                    for a in range(4):
                        if a in (1, 3) and a // 2 < len(ns):
                            score_rows(phase, ns[a // 2])
                        if a == 2 and s > 1:
                            values(b, s - 2)
                        if a > 1 and kt == 3 and g < 3:
                            requery(phase, b, g + 1, a - 2)
                        if kt == 0 and a == 0:
                            pe.wait_ge(m_emptied["act"], AHEAD + 8 * b + 2 * g + 2)
                        pe.wait_ge(exp_done, AHEAD + 64 * b + max(4 * s + a - 1, 0))
                        pe.matmul(ps_sc[:, a % 2, :], kz[:, 2 * g + a // 2, P * kt:P * (kt + 1)],
                                  qp[:, 2 * g + a % 2, :], start=True, stop=True).then_inc(sc_filled, 1)

                def values(b, s):
                    g, kt = s // 4, s % 4
                    if s == 0:
                        pe.wait_ge(v_moved, b + 1)
                    if kt == 0:
                        pe.wait_ge(ot_copied, AHEAD + 4 * b + g)
                    pe.wait_ge(exp_done, AHEAD + 64 * b + 4 * s + 4)
                    for a in range(4):
                        ins = pe.matmul(ps_pv[32 * a:32 * a + 32, :], v[:, kt, 2 * g + a // 2, :],
                                        pt[:, s % 3, a, :], start=(kt == 0), stop=(kt == 3))
                    ins.then_inc(pv_done, 1)

                def outputs(phase, b, g):
                    pe.wait_ge(ot_copied, AHEAD + 4 * b + g + 1)
                    misc.wait_free(pe, m_emptied, phase, f"ot{g}")
                    transposes(ps_m[:, :], lambda t: ot[:, g % 2, P * t:P * (t + 1)]).then_inc(m_filled, 1)

                def step(phase, b, s, prepare):
                    g, kt = s // 4, s % 4
                    scores(phase, b, s)
                    if kt == 2 and g > 0:
                        outputs(phase, b, g - 1)
                    if prepare:
                        if s == TURN:
                            turn(phase, b + 1)
                        if s in PROJECT:
                            project(phase, b + 1, PROJECT.index(s))
                        pack(phase, b + 1, PACKED.get(s, ()))
                        for n in EARLY.get(s, ()):
                            score_rows(phase, n)

                def end(phase, b, name):
                    k = int(name[2])
                    misc.wait_free(pe, m_emptied, phase, name)
                    if name in ("at0", "at1"):
                        if k == 0:
                            pe.wait_ge(m_emptied["dve"], AHEAD + 8 * b + 4)
                        transposes(ps_m[:, :], lambda t: ao[:, t, P * k:P * (k + 1)]).then_inc(m_filled, 1)
                    else:
                        pe.wait_ge(m_emptied["dve"], AHEAD + 8 * b + 6)
                        for t in range(2):
                            at = P * (2 * k + t)
                            for j in range(KD):
                                ins = product(pe, ps_m[:, D * t:D * (t + 1)],
                                              (at_h[:, j, at:at + P], at_l[:, j, at:at + P]),
                                              (wo_h[:, j, :], wo_l[:, j, :]), j == 0, j == KD - 1)
                        ins.then_inc(m_filled, 1)

                for s in range(HEAD):
                    step(FIRST, 0, s, False)
                pe.wait_ge(w_split, 2)

                def row(phase, b, last):
                    for s in range(HEAD, STEPS):
                        step(phase, b, s, not last)
                    values(b, STEPS - 2)
                    if not last:
                        pack(phase, b + 1, PACKED_LAST)
                    values(b, STEPS - 1)
                    if not last:
                        for n in LATE[0]:
                            score_rows(phase, n)
                    outputs(phase, b, 3)
                    if not last:
                        for n in LATE[1]:
                            score_rows(phase, n)
                        all_packed(phase)
                        requery(phase, b + 1, 0, 0)
                        requery(phase, b + 1, 0, 1)
                    for s in range(HEAD):
                        if not last:
                            step(phase, b + 1, s, False)
                        for name in END[s]:
                            end(phase, b, name)

                rows(pe, row)

        m.close()


def experts_stage(nc, stage, w13, w2a, w2b, wg, X, ident, consts, xd, oe, banks, zeroed, zeroings,
                  ahead=(), ahead_loaded=None):
    upper, ones, rank, first_slot = consts
    NW = 2 * KD * H
    with ExitStack() as ctx:
        m = Memory(nc, ctx, stage, banks)
        sb, sem = m.sb, m.sem
        s13_in, s2_in = sb("s13_in", [P, KD, 2, H]), sb("s2_in", [P, 3, D])
        s13, s2 = m.pair("s13", [P, KD, 2, H]), m.pair("s2", [P, 3, D])
        e13_in, e2_in = sb("e13_in", [P, 2, KD, 2, H]), sb("e2_in", [P, 2, 3, D])
        e13, e2 = m.pair("e13", [P, 2, KD, 2, H]), m.pair("e2", [P, 2, 3, D])
        wg_in, wgs = sb("wg_in", [P, KD, E]), m.pair("wg", [P, KD, E])
        ln = RowStats(m, "ln", TB)
        nhalf, rstd = sb("nhalf", [P, TB]), sb("rstd", [P, TB])
        xb = sb("xb", [P, TB, D])
        xn = sb("xn", [P, TB, D])
        xs = sb("xs", [P, TB, D])
        xt_h, xt_l = m.pair("xt", [P, KD, S])
        sil, hid = sb("sil", [P, 3, C]), sb("hid", [P, 3, C])
        h_h, h_l = m.pair("h", [P, 3, C])
        lg, ex, eq, sc, oh = (sb(n, [P, TB, E]) for n in ("lg", "ex", "eq", "sc", "oh"))
        pos, val = sb("pos", [P, TB, E]), sb("val", [P, TB, E])
        mx, sm, em, ms, rsm, gate, px, slot, keep, off, sls, slg = (
            sb(n, [P, TB]) for n in ("mx", "sm", "em", "ms", "rsm", "gate", "px", "slot", "keep", "off", "sls", "slg"))
        base = sb("base", [P, E])
        to_slot = sb("to_slot", [P, TB], U32)
        from_slot = sb("from_slot", [P, TILES], U32)
        weight = sb("weight", [P, TILES])
        xe = sb("xe", [P, 2, U, D])
        xet_h, xet_l = m.pair("xet", [P, KD, C])
        eo = sb("eo", [P, 2, U, D])
        got = sb("got", [P, 4, D])

        ps_t = m.psum([P, 2, S])
        ps_up = m.psum([P, 3, 2, C])
        ps_down = m.psum([P, U, S])
        ps_r = m.psum([P, S])

        s_loaded, g_loaded = sem("s_loaded"), sem("g_loaded")
        e_loaded = [sem("e_loaded0"), sem("e_loaded1")]
        xe_loaded = [sem("xe_loaded0"), sem("xe_loaded1")]
        set_up = sem("set_up")
        s_high, s_low = sem("s_high"), sem("s_low")
        e_high, e_low = sem("e_high"), sem("e_low")
        xb_copied, rstd_ready, xn_ready, xs_copied = (
            sem("xb_copied"), sem("rstd_ready"), sem("xn_ready"), sem("xs_copied"))
        t_filled, xt_high, xt_low = sem("t_filled"), sem("xt_high"), sem("xt_low")
        up_done, sil_done, hid_done, h_high, h_low = (
            sem("up_done"), sem("sil_done"), sem("hid_done", ahead=True), sem("h_high"), sem("h_low"))
        down_done, added = sem("down_done"), sem("added", ahead=True)
        logits_done, ex_done, counted = sem("logits_done"), sem("ex_done"), sem("counted")
        route = sem("route", ahead=True)
        scattered = sem("scattered", keep=True)
        eo_stored = [sem("eo_stored0", ahead=True), sem("eo_stored1", ahead=True)]
        gathered = [sem(f"gathered{i}", keep=True) for i in range(4)]
        combined, gate_ready = sem("combined"), sem("gate_ready")
        ROUTE = 23

        def load_weights(q, dst13, dst2, e, done):
            q.dma_start(dst13.rearrange("p k a h -> p (k a h)"), w13[e]).then_inc(done, 16)
            q.dma_start(dst2[:, 0:2, :].rearrange("p i d -> p (i d)"), w2a[e]).then_inc(done, 16)
            q.dma_start(dst2[0:HT[2], 2, :], w2b[e]).then_inc(done, 16)

        def high_parts(eng, hi13, hi2, in13, in2, done):
            copy = (lambda o, i: eng.activation(o, i, ACT.Copy))
            copy(hi13, in13)
            copy(hi2[:, 0:2, :], in2[:, 0:2, :])
            copy(hi2[0:HT[2], 2, :], in2[0:HT[2], 2, :]).then_inc(done, 1)

        def low_parts(eng, lo13, lo2, hi13, hi2, in13, in2, done):
            sub = (lambda o, i, h: eng.tensor_tensor(o, i, h.bitcast(F32), ALU.subtract))
            sub(lo13, in13, hi13)
            sub(lo2[:, 0:2, :], in2[:, 0:2, :], hi2[:, 0:2, :])
            sub(lo2[0:HT[2], 2, :], in2[0:HT[2], 2, :], hi2[0:HT[2], 2, :]).then_inc(done, 1)

        def up(pe, n, i, xt, w, off_t):
            rows = slice(P * i, P * i + HT[i])
            if i == 0:
                pe.wait_ge(hid_done, AHEAD + 3 * n)
            for a in range(2):
                for k in range(KD):
                    ins = product(pe, ps_up[0:HT[i], i, a, :], (w[0][:, k, a, rows], w[1][:, k, a, rows]),
                                  (xt[0][:, k, off_t:off_t + C], xt[1][:, k, off_t:off_t + C]), k == 0, k == KD - 1)
            ins.then_inc(up_done, 1)

        def down(pe, n, i, w):
            if i == 0:
                pe.wait_ge(added, AHEAD + n)
            pe.wait_ge(h_low, 3 * n + i + 1)
            for t in range(U):
                ins = product(pe, ps_down[:, t, 0:D],
                              (h_h[0:HT[i], i, P * t:P * (t + 1)], h_l[0:HT[i], i, P * t:P * (t + 1)]),
                              (w[0][0:HT[i], i, :], w[1][0:HT[i], i, :]), i == 0, i == 2)
            if i == 2:
                ins.then_inc(down_done, 1)

        def silu(act, n, i):
            act.wait_ge(up_done, 3 * n + i + 1)
            act.activation(sil[0:HT[i], i, :], ps_up[0:HT[i], i, 0, :], ACT.Silu).then_inc(sil_done, 1)

        def hidden_high(act, n, i):
            act.wait_ge(hid_done, AHEAD + 3 * n + i + 1)
            act.activation(h_h[0:HT[i], i, :], hid[0:HT[i], i, :], ACT.Copy).then_inc(h_high, 1)

        def hidden(dve, n, i):
            dve.wait_ge(sil_done, 3 * n + i + 1)
            dve.tensor_tensor(hid[0:HT[i], i, :], sil[0:HT[i], i, :], ps_up[0:HT[i], i, 1, :],
                              ALU.mult).then_inc(hid_done, 1)

        def hidden_low(eng, n, i):
            eng.wait_ge(h_high, 3 * n + i + 1)
            eng.tensor_tensor(h_l[0:HT[i], i, :], hid[0:HT[i], i, :], h_h[0:HT[i], i, :].bitcast(F32),
                              ALU.subtract).then_inc(h_low, 1)

        def rows(eng, body):
            body(0, False)
            with eng.Fori(1, B - 1) as b:
                body(b, False)
            body(B - 1, True)

        def experts(eng, body):
            with eng.Fori(0, E // 2 - 1) as v:
                body(2 * v, 0, False)
                body(2 * v + 1, 1, False)
            body(E - 2, 0, False)
            body(E - 1, 1, True)

        N0 = UNITS

        m.open()
        with nc.Block() as block:

            @block.sync
            def _(sp):
                load_weights(sp, s13_in[:, :, :, :], s2_in, E, s_loaded)
                sp.dma_start(wg_in[:, :, :], wg.rearrange("(k p) e -> p k e", p=P)).then_inc(g_loaded, 16)
                load_weights(sp, e13_in[:, 0], e2_in[:, 0], 0, e_loaded[0])
                load_weights(sp, e13_in[:, 1], e2_in[:, 1], 1, e_loaded[1])

                for dst, src in ahead:
                    sp.dma_start(dst, src.rearrange("(k p) n -> p k n", p=P)).then_inc(ahead_loaded, 16)

                def load_rows(e, w):
                    sp.dma_start(xe[:, w, :, :], xd[bass.ds(C * e, C), :].rearrange("(t p) d -> p t d", p=P)
                                 ).then_inc(xe_loaded[w], 16)

                sp.wait_ge(scattered, 64 * B)
                load_rows(0, 0)
                load_rows(1, 1)

                def body(e, w, last):
                    sp.wait_ge(added, AHEAD + N0 + e + 1)
                    sp.dma_start(oe[bass.ds(C * e, C), :].rearrange("(t p) d -> p t d", p=P),
                                 eo[:, w, :, :]).then_inc(eo_stored[w], 16)

                def loads(e, w):
                    sp.wait_ge(t_filled, 2 * B + e + 1)
                    load_rows(e + 2, w)
                    sp.wait_ge(e_low, e + 1)
                    load_weights(sp, e13_in[:, w], e2_in[:, w], e + 2, e_loaded[w])

                with sp.Fori(0, E // 2 - 1) as v:
                    for w in range(2):
                        loads(2 * v + w, w)
                        body(2 * v + w, w, False)
                body(E - 2, 0, False)
                body(E - 1, 1, True)
                for w in range(2):
                    sp.wait_ge(eo_stored[w], AHEAD + 16 * E // 2)

            @block.gpsimd
            def _(pool):
                pool.memset(nhalf[:, :], -0.5).then_inc(set_up, 1)
                pool.wait_ge(set_up, 1)

                def power(b):
                    pool.wait_ge(ln.done, ln.steps * (b + 1))
                    pool.tensor_tensor(rstd[:, :], ln.ve[:, :], nhalf[:, :], ALU.pow).then_inc(rstd_ready, 1)

                power(0)
                pool.wait_ge(zeroed, 16 * zeroings)
                pool.wait_ge(e_high, 1)
                low_parts(pool, e13[1][:, 0], e2[1][:, 0], e13[0][:, 0], e2[0][:, 0], e13_in[:, 0], e2_in[:, 0], e_low)

                def row(b, last):
                    for i in range(3):
                        hidden_low(pool, 2 * b, i)
                    if not last:
                        pool.wait_ge(xn_ready, TB * (b + 1))
                        power(b + 1)
                    for i in range(3):
                        hidden_low(pool, 2 * b + 1, i)
                    pool.wait_ge(xs_copied, b + 1)
                    pool.wait_ge(route, AHEAD + ROUTE * b + 21)
                    pool.tensor_tensor(gate[:, :], em[:, :], rsm[:, :], ALU.mult).then_inc(gate_ready, 1)
                    for t in range(TB):
                        pool.indirect_dma_start(
                            xd, bass.IndirectOffsetOnAxis(ap=to_slot[:, t:t + 1], axis=0), xs[:, t, :], None,
                            bounds_check=E * C - 1, oob_is_err=False).then_inc(scattered, 16)

                rows(pool, row)

                def expert(e, w, last):
                    if not last:
                        pool.wait_ge(e_high, e + 2)
                        pool.wait_ge(down_done, N0 + e)
                        low_parts(pool, e13[1][:, 1 - w], e2[1][:, 1 - w], e13[0][:, 1 - w], e2[0][:, 1 - w],
                                  e13_in[:, 1 - w], e2_in[:, 1 - w], e_low)

                experts(pool, expert)
                for w in range(2):
                    pool.wait_ge(eo_stored[w], AHEAD + 16 * E // 2)
                for t in range(TILES):
                    if t >= 4:
                        pool.wait_ge(combined, t - 3)
                    pool.indirect_dma_start(
                        got[:, t % 4, :], None, oe, bass.IndirectOffsetOnAxis(ap=from_slot[:, t:t + 1], axis=0),
                        bounds_check=E * C - 1, oob_is_err=False).then_inc(gathered[t % 4], 16)

            @block.scalar
            def _(act):
                act.wait_ge(s_loaded, 48)
                high_parts(act, s13[0][:, :, :, :], s2[0], s13_in[:, :, :, :], s2_in, s_high)
                act.wait_ge(g_loaded, 16)
                act.activation(wgs[0][:, :, :], wg_in[:, :, :], ACT.Copy).then_inc(s_high, 1)

                def transposed(b):
                    for k in range(KD):
                        act.wait_ge(t_filled, 2 * b + k + 1)
                        act.activation(xt_h[:, k, :], ps_t[:, k, :], ACT.Copy).then_inc(xt_high, 1)

                def stage_rows(b):
                    if not isinstance(b, int) or b > 0:
                        act.wait_ge(scattered, 64 * b)
                    act.activation(xs[:, :, :], xn[:, :, :], ACT.Copy).then_inc(xs_copied, 1)

                transposed(0)
                act.wait_ge(e_loaded[0], 48)
                high_parts(act, e13[0][:, 0], e2[0][:, 0], e13_in[:, 0], e2_in[:, 0], e_high)

                def row(b, last):
                    n = 2 * b
                    silu(act, n, 0)
                    silu(act, n, 1)
                    hidden_high(act, n, 0)
                    silu(act, n, 2)
                    hidden_high(act, n, 1)
                    hidden_high(act, n, 2)
                    act.wait_ge(route, AHEAD + ROUTE * b + 2)
                    act.activation(ex[:, :, :], lg[:, :, :], ACT.Exp).then_inc(ex_done, 1)
                    stage_rows(b)
                    n = 2 * b + 1
                    silu(act, n, 0)
                    silu(act, n, 1)
                    hidden_high(act, n, 0)
                    silu(act, n, 2)
                    hidden_high(act, n, 1)
                    hidden_high(act, n, 2)
                    if not last:
                        transposed(b + 1)

                rows(act, row)

                def expert_rows(e):
                    act.wait_ge(t_filled, 2 * B + e + 1)
                    act.activation(xet_h[:, :, :].rearrange("p k c -> p (k c)"), ps_t[:, 0, :],
                                   ACT.Copy).then_inc(xt_high, 1)

                expert_rows(0)

                def expert(e, w, last):
                    n = N0 + e
                    if not last:
                        act.wait_ge(e_loaded[1 - w], 24 * (e - w) + 48 * (1 + w))
                        act.wait_ge(down_done, N0 + e)
                        high_parts(act, e13[0][:, 1 - w], e2[0][:, 1 - w], e13_in[:, 1 - w], e2_in[:, 1 - w], e_high)
                    silu(act, n, 0)
                    silu(act, n, 1)
                    hidden_high(act, n, 0)
                    silu(act, n, 2)
                    hidden_high(act, n, 1)
                    hidden_high(act, n, 2)
                    if not last:
                        expert_rows(e + 1)

                experts(act, expert)

            @block.vector
            def _(dve):
                dve.memset(base[:, :], 0.0).then_inc(set_up, 1)
                dve.wait_ge(set_up, 2)

                def statistics(b):
                    dve.tensor_copy(xb[:, :, :], X[:, bass.ds(TB * b, TB), :]).then_inc(xb_copied, 1)
                    dve.wait_ge(xb_copied, b + 1)
                    ln.run(dve, b, lambda t: xb[:, t, :])

                def normalize(b):
                    dve.wait_ge(rstd_ready, b + 1)
                    dve.wait_ge(xs_copied, b)
                    for t in range(TB):
                        dve.tensor_scalar(xn[:, t, :], xb[:, t, :], ln.mean[:, t:t + 1], rstd[:, t:t + 1],
                                          ALU.subtract, ALU.mult).then_inc(xn_ready, 1)

                def transposed(b):
                    for k in range(KD):
                        dve.wait_ge(xt_high, KD * b + k + 1)
                        dve.tensor_tensor(xt_l[:, k, :], ps_t[:, k, :], xt_h[:, k, :].bitcast(F32),
                                          ALU.subtract).then_inc(xt_low, 1)

                statistics(0)
                normalize(0)
                dve.wait_ge(s_high, 1)
                low_parts(dve, s13[1][:, :, :, :], s2[1], s13[0][:, :, :, :], s2[0], s13_in[:, :, :, :], s2_in, s_low)
                dve.wait_ge(s_high, 2)
                dve.tensor_tensor(wgs[1][:, :, :], wg_in[:, :, :], wgs[0][:, :, :].bitcast(F32),
                                  ALU.subtract).then_inc(s_low, 1)
                transposed(0)

                def wide(a):
                    return a[:, :].unsqueeze(2).to_broadcast([P, TB, E])

                def row(b, last):
                    at = ROUTE * b
                    steps = [0]

                    def step(ins):
                        ins.then_inc(route, 1)
                        steps[0] += 1
                        dve.wait_ge(route, AHEAD + at + steps[0])

                    def add_down(n, half):
                        dve.wait_ge(down_done, n + 1)
                        dve.tensor_tensor(X[:, bass.ds(TB * b + U * half, U), :],
                                          ps_down[:, :, 0:D], X[:, bass.ds(TB * b + U * half, U), :],
                                          ALU.add).then_inc(added, 1)

                    bank = ps_r[:, 0:3 * TB * E].rearrange("p (a t e) -> p a t e", a=3, e=E)
                    hidden(dve, 2 * b, 0)
                    dve.wait_ge(logits_done, b + 1)
                    step(dve.tensor_reduce(mx[:, :], bank[:, 0], AX_X, ALU.max))
                    step(dve.tensor_tensor(lg[:, :, :], bank[:, 0], wide(mx), ALU.subtract))
                    hidden(dve, 2 * b, 1)
                    hidden(dve, 2 * b, 2)
                    if not last:
                        statistics(b + 1)
                    dve.wait_ge(ex_done, b + 1)
                    step(dve.tensor_reduce(em[:, :], ex[:, :, :], AX_X, ALU.max))
                    step(dve.tensor_tensor(eq[:, :, :], ex[:, :, :], wide(em), ALU.is_ge))
                    step(dve.tensor_tensor(sc[:, :, :], eq[:, :, :], rank, ALU.mult))
                    step(dve.tensor_reduce(ms[:, :], sc[:, :, :], AX_X, ALU.max))
                    step(dve.tensor_tensor(oh[:, :, :], sc[:, :, :], wide(ms), ALU.is_equal))
                    step(dve.tensor_reduce(sm[:, :], ex[:, :, :], AX_X, ALU.add))
                    step(dve.reciprocal(rsm[:, :], sm[:, :]))
                    add_down(2 * b, 0)
                    hidden(dve, 2 * b + 1, 0)
                    if not last:
                        normalize(b + 1)
                    hidden(dve, 2 * b + 1, 1)
                    hidden(dve, 2 * b + 1, 2)
                    if not last:
                        transposed(b + 1)
                    dve.wait_ge(counted, b + 1)
                    for t in range(TB):
                        dve.tensor_tensor(pos[:, t, :], bank[:, 1, t, :], base[:, :], ALU.add)
                        step(dve.tensor_tensor(base[:, :], bank[:, 2, t, :], base[:, :], ALU.add))
                    step(dve.tensor_tensor(val[:, :, :], pos[:, :, :], first_slot, ALU.add))
                    step(dve.tensor_tensor(pos[:, :, :], pos[:, :, :], oh[:, :, :], ALU.mult))
                    step(dve.tensor_tensor(val[:, :, :], val[:, :, :], oh[:, :, :], ALU.mult))
                    dve.tensor_reduce(px[:, :], pos[:, :, :], AX_X, ALU.add)
                    step(dve.tensor_reduce(slot[:, :], val[:, :, :], AX_X, ALU.add))
                    step(dve.tensor_scalar(keep[:, :], px[:, :], float(C), None, ALU.is_le))
                    step(dve.tensor_scalar(off[:, :], keep[:, :], -2.0 * E * C, 2.0 * E * C, ALU.mult, ALU.add))
                    step(dve.tensor_tensor(sls[:, :], slot[:, :], off[:, :], ALU.add))
                    step(dve.tensor_copy(to_slot[:, :], sls[:, :]))
                    step(dve.tensor_scalar(from_slot[:, bass.ds(TB * b, TB)], sls[:, :], float(E * C - 1), None,
                                           ALU.min))
                    add_down(2 * b + 1, 1)
                    dve.wait_ge(gate_ready, b + 1)
                    step(dve.tensor_tensor(weight[:, bass.ds(TB * b, TB)], gate[:, :], keep[:, :], ALU.mult))
                    assert steps[0] == ROUTE

                rows(dve, row)

                def expert_rows(e):
                    dve.wait_ge(xt_high, KD * B + e + 1)
                    dve.tensor_tensor(xet_l[:, :, :].rearrange("p k c -> p (k c)"), ps_t[:, 0, :],
                                      xet_h[:, :, :].bitcast(F32).rearrange("p k c -> p (k c)"),
                                      ALU.subtract).then_inc(xt_low, 1)

                expert_rows(0)

                def expert(e, w, last):
                    n = N0 + e
                    hidden(dve, n, 0)
                    hidden(dve, n, 1)
                    hidden_low(dve, n, 0)
                    hidden(dve, n, 2)
                    hidden_low(dve, n, 1)
                    hidden_low(dve, n, 2)
                    if not last:
                        expert_rows(e + 1)
                    dve.wait_ge(down_done, n + 1)
                    dve.wait_ge(eo_stored[w], AHEAD + 8 * (e - w))
                    dve.tensor_copy(eo[:, w, :, :], ps_down[:, :, 0:D]).then_inc(added, 1)

                experts(dve, expert)
                for t in range(TILES):
                    dve.wait_ge(gathered[t % 4], 16 * (t // 4 + 1))
                    dve.scalar_tensor_tensor(X[:, t, :], got[:, t % 4, :], weight[:, t:t + 1], X[:, t, :],
                                             ALU.mult, ALU.add).then_inc(combined, 1)

            @block.tensor
            def _(pe):
                shared_w13, shared_w2 = s13, s2
                xt = (xt_h, xt_l)

                def transposes(b):
                    pe.wait_ge(xn_ready, TB * (b + 1))
                    for k in range(KD):
                        for t in range(TB):
                            ins = pe.transpose(ps_t[:, k, P * t:P * (t + 1)], xn[:, t, P * k:P * (k + 1)], ident[:, :])
                        ins.then_inc(t_filled, 1)

                transposes(0)
                pe.wait_ge(s_low, 2)

                def row(b, last):
                    n = 2 * b
                    pe.wait_ge(xt_low, KD * (b + 1))
                    up(pe, n, 0, xt, shared_w13, 0)
                    pe.wait_ge(route, AHEAD + ROUTE * b)
                    for t in range(TB):
                        for k in range(KD):
                            at = P * t
                            ins = product(pe, ps_r[:, E * t:E * (t + 1)], (xt_h[:, k, at:at + P], xt_l[:, k, at:at + P]),
                                          (wgs[0][:, k, :], wgs[1][:, k, :]), k == 0, k == KD - 1)
                    ins.then_inc(logits_done, 1)
                    up(pe, n, 1, xt, shared_w13, 0)
                    up(pe, n, 2, xt, shared_w13, 0)
                    for i in range(3):
                        down(pe, n, i, shared_w2)
                    n = 2 * b + 1
                    for i in range(3):
                        up(pe, n, i, xt, shared_w13, C)
                    if not last:
                        transposes(b + 1)
                    pe.wait_ge(route, AHEAD + ROUTE * b + 7)
                    one_hot = oh[:, :, :].rearrange("p t e -> p (t e)")
                    pe.matmul(ps_r[:, TB * E:2 * TB * E], upper, one_hot, start=True, stop=True)
                    pe.matmul(ps_r[:, 2 * TB * E:3 * TB * E], ones, one_hot, start=True, stop=True).then_inc(counted, 1)
                    for i in range(3):
                        down(pe, n, i, shared_w2)

                rows(pe, row)

                def expert_rows(e, w):
                    pe.wait_ge(xe_loaded[w], 8 * (e - w) + 16)
                    for k in range(KD):
                        for t in range(U):
                            at = C * k + P * t
                            ins = pe.transpose(ps_t[:, 0, at:at + P], xe[:, w, t, P * k:P * (k + 1)], ident[:, :])
                    ins.then_inc(t_filled, 1)

                expert_rows(0, 0)

                def expert(e, w, last):
                    n = N0 + e
                    w13p = (e13[0][:, w], e13[1][:, w])
                    w2p = (e2[0][:, w], e2[1][:, w])
                    pe.wait_ge(e_low, e + 1)
                    pe.wait_ge(xt_low, KD * B + e + 1)
                    for i in range(3):
                        up(pe, n, i, (xet_h, xet_l), w13p, 0)
                    if not last:
                        expert_rows(e + 1, 1 - w)
                    for i in range(3):
                        down(pe, n, i, w2p)

                experts(pe, expert)
        m.close()


def state_space_stage(nc, a, X, ident, consts, banks, raw, raw_loaded):
    upper, ones = consts[0], consts[1]
    NF = 4
    with ExitStack() as ctx:
        m = Memory(nc, ctx, "ssm", banks)
        sb, sem = m.sb, m.sem
        win, wout = m.pair("win", [P, KD, PROJ]), m.pair("wout", [P, KD, D])
        w1, w3, w2 = m.pair("w1", [P, KD, INTER]), m.pair("w3", [P, KD, INTER]), m.pair("w2", [P, IT, D])
        w_of = {"win": win, "wout": wout, "w1": w1, "w3": w3, "w2": w2}
        norms = sb("norms", [P, 3, KD])
        conv_w = sb("conv_w", [P, NF, 4])
        conv_b = sb("conv_b", [P, NF])
        heads = sb("heads", [P, 3, 2])
        neg_a = sb("neg_a", [P, 2])
        cap = sb("cap", [P, P])
        nhalf = sb("nhalf", [P, TB])
        xb, xh, hn = sb("xb", [P, TB, D]), sb("xh", [P, TB, D]), sb("hn", [P, TB, D])
        ln = RowStats(m, "ln", TB)
        rstd, rstd2, var, v2, r1, rr = (sb(n, [P, TB]) for n in ("rstd", "rstd2", "var", "v2", "r1", "rr"))
        ht_h, ht_l = m.pair("ht", [P, KD, S])
        cv = sb("cv", [P, NF, S + 4])
        ca = sb("ca", [P, 2, S])
        xc = sb("xc", [P, NF, S])
        sz = sb("sz", [P, TB, D])
        small = [sb(f"dt{i}", [P, TB, 2]) for i in range(16)]
        (xdt, adt, udt, wdt, ddt, zdt, dden, rden, qdt, lnw, tdt, t2, mdt, sdt, dt, dA) = small
        ecs, etot, csum, dif, dec0, dec = (sb(n, [P, TB, 2]) for n in ("ecs", "etot", "csum", "dif", "dec0", "dec"))
        xtm, btm = sb("xtm", [P, TB, P]), sb("btm", [P, TB, P])
        dd, ee, mm = sb("dd", [P, 2, P]), sb("ee", [P, 2, P]), sb("mm", [P, 2, P])
        xd, t0 = sb("xd", [P, 2, P]), sb("t0", [P, 2, P])
        state = sb("state", [P, 2, 2, P])
        y1, y2 = sb("y1", [P, 2, P]), sb("y2", [P, 2, P])
        yg = sb("yg", [P, TB, D])
        sq = sb("sq", [P, D])
        ss, ms, rq = sb("ss", [P, TB]), sb("ms", [P, TB]), sb("rq", [P, TB])
        sil, hid = sb("sil", [P, 3, C]), sb("hid", [P, 3, C])
        h_h, h_l = m.pair("h", [P, IT, C])

        ps = m.psum([P, 8, S])
        bank_t = (5, 6)
        bank_small = 7

        loads = sem("loads")
        scaled, ffn_scaled, w_high, w_low, ffn_low, set_up, nhalf_set = sem("scaled"), sem("ffn_scaled"), sem("w_high"), sem("w_low"), sem("ffn_low"), sem("set_up"), sem("nhalf_set")
        nega = sem("nega")
        xb_copied, rstd_ready, r1_ready = sem("xb_copied"), sem("rstd_ready"), sem("r1_ready")
        pre, hn_ready = sem("pre"), sem("hn_ready")
        t_filled, t_high, t_low = sem("t_filled"), sem("t_high"), sem("t_low")
        feat, feat_out, z_filled, z_out = sem("feat"), sem("feat_out"), sem("z_filled"), sem("z_out")
        conv, conv_out, softplus = sem("conv"), sem("conv_out", ahead=True), sem("softplus")
        dts, dt_act, sums, dt_filled = sem("dts"), sem("dt_act"), sem("sums"), sem("dt_filled")
        tm_filled, tm_out = sem("tm_filled"), sem("tm_out")
        g_done, row_done, dd_done, ee_done, mm_done, xd_done = (
            sem("g_done"), sem("row_done"), sem("dd_done", ahead=True), sem("ee_done"), sem("mm_done"), sem("xd_done"))
        y_done, s_done, st_done, ys, yg_done, sq_done = (
            sem("y_done", ahead=True), sem("s_done"), sem("st_done"), sem("ys"), sem("yg_done"), sem("sq_done", ahead=True))
        norm_v, rq_ready = sem("norm_v"), sem("rq_ready")
        o_done, h2_done, r2_done = sem("o_done"), sem("h2_done"), sem("r2_done", ahead=True)
        up_done, sil_done, hid_done, h_high, h_low = (
            sem("up_done"), sem("sil_done"), sem("hid_done", ahead=True), sem("h_high"), sem("h_low"))
        down_done, added = sem("down_done"), sem("added", ahead=True)

        def square(act, b, c):
            act.wait_ge(yg_done, TB * b + c + 1)
            act.wait_ge(sq_done, AHEAD + 2 * TB * b + c)
            act.activation(sq[:, :], yg[:, c, :], ACT.Square, accum_out=ss[:, c:c + 1]).then_inc(sq_done, 1)

        def t_banks(k):
            return ps[:, bank_t[k], :]

        m.open()
        with nc.Block() as block:

            @block.sync
            def _(sp):
                def load(dst, src):
                    sp.dma_start(dst, src).then_inc(loads, 16)
                load(norms[:, :, :], a["norms"])
                load(conv_w[:, :, :], a["conv_w"])
                load(conv_b[:, :], a["conv_b"])
                load(heads[:, :, :].rearrange("p a h -> p (a h)"),
                     a["heads"].rearrange("(o n) -> o n", o=1).to_broadcast([P, 6]))
                load(cap[:, :], a["cap"])

            @block.gpsimd
            def _(pool):
                pool.memset(nhalf[:, :], -0.5).then_inc(nhalf_set, 1)
                pool.wait_ge(nhalf_set, 1)

                def row(b, first):
                    pool.wait_ge(ln.done, ln.steps * (b + 1))
                    pool.tensor_tensor(rstd[:, :], ln.ve[:, :], nhalf[:, :], ALU.pow).then_inc(rstd_ready, 1)
                    pool.wait_ge(pre, 6 * b + 4)
                    pool.tensor_tensor(r1[:, :], v2[:, :], nhalf[:, :], ALU.pow).then_inc(r1_ready, 1)
                    if first:
                        for i, n in enumerate(("w1", "w3", "w2")):
                            pool.wait_ge(w_high, 3 + i)
                            pool.tensor_tensor(w_of[n][1][:, :, :], raw[n], w_of[n][0][:, :, :].bitcast(F32),
                                               ALU.subtract).then_inc(ffn_low, 1)
                    for i in range(2):
                        pool.wait_ge(norm_v, 2 * b + i + 1)
                        pool.tensor_tensor(rq[:, :], ms[:, :], nhalf[:, :], ALU.pow).then_inc(rq_ready, 1)
                    pool.wait_ge(h2_done, 2 * (b + 1))
                    pool.tensor_tensor(xb[:, :, :], xb[:, :, :], xh[:, :, :], ALU.add).then_inc(r2_done, 1)

                row(0, True)
                with pool.Fori(1, B) as b:
                    row(b, False)

            @block.scalar
            def _(act):
                act.wait_ge(loads, 16 * 5)
                act.activation(neg_a[:, :], heads[:, 1, :], ACT.Exp).then_inc(nega, 1)
                for i, n in enumerate(("win", "wout", "w1", "w3", "w2")):
                    if n in ("win", "wout"):
                        act.wait_ge(scaled, i + 1)
                    elif n != "w2":
                        act.wait_ge(ffn_scaled, i - 1)
                    act.activation(w_of[n][0][:, :, :], raw[n], ACT.Copy).then_inc(w_high, 1)
                act.wait_ge(set_up, 2)
                with act.Fori(0, B) as b:

                    def high(n):
                        for k in range(KD):
                            act.wait_ge(t_filled, 6 * b + 2 * n + k + 1)
                            act.activation(ht_h[:, k, :], t_banks(k), ACT.Copy).then_inc(t_high, 1)

                    high(0)
                    for f in range(NF):
                        act.wait_ge(feat, NF * b + f + 1)
                        act.activation(cv[:, f, 3:3 + S], ps[:, f, :], ACT.Copy).then_inc(feat_out, 1)
                    act.wait_ge(dts, 11 * b + 2)
                    act.activation(udt[:, :, :], adt[:, :, :], ACT.Exp, scale=-1.0).then_inc(dt_act, 1)
                    act.wait_ge(dts, 11 * b + 3)
                    act.activation(lnw[:, :, :], wdt[:, :, :], ACT.Ln).then_inc(dt_act, 1)
                    act.wait_ge(sums, 2 * b + 2)
                    act.activation(ecs[:, :, :], ps[:, bank_small, 8:16].rearrange("p (t h) -> p t h", h=2), ACT.Exp)
                    act.activation(etot[:, :, :], ps[:, bank_small, 16:24].rearrange("p (t h) -> p t h", h=2),
                                   ACT.Exp).then_inc(dt_act, 1)
                    act.wait_ge(dts, 11 * b + 10)
                    act.activation(dec0[:, :, :], dif[:, :, :], ACT.Exp).then_inc(dt_act, 1)
                    for i in range(2):
                        act.wait_ge(z_filled, 2 * b + i + 1)
                        act.activation(sz[:, 2 * i:2 * i + 2, :].rearrange("p t d -> p (t d)"), t_banks(i),
                                       ACT.Silu).then_inc(z_out, 1)
                    for f in range(NF):
                        act.wait_ge(conv, 4 * (NF * b + f + 1))
                        act.activation(xc[:, f, :], ca[:, f % 2, :], ACT.Silu, bias=conv_b[:, f:f + 1]).then_inc(conv_out, 1)
                    for i, o in enumerate((xtm, btm)):
                        act.wait_ge(tm_filled, 2 * b + i + 1)
                        act.activation(o[:, :, :].rearrange("p t n -> p (t n)"), t_banks(i), ACT.Copy).then_inc(tm_out, 1)
                    for c in range(TB):
                        act.wait_ge(dd_done, AHEAD + 2 * (TB * b + c) + 2)
                        act.activation(ee[:, :, :], dd[:, :, :], ACT.Exp).then_inc(ee_done, 1)
                        if c > 0:
                            square(act, b, c - 1)
                    square(act, b, TB - 1)
                    high(1)
                    for t in range(TB):
                        act.wait_ge(h2_done, 2 * b + t // 2 + 1)
                        act.wait_ge(sq_done, AHEAD + 2 * TB * b + TB + t)
                        act.activation(sq[:, :], xh[:, t, :], ACT.Square, accum_out=ss[:, t:t + 1]).then_inc(sq_done, 1)
                    high(2)
                    for u in range(2):
                        n = IT * 2 * b + IT * u
                        for i in range(IT + 1):
                            if i < IT:
                                act.wait_ge(up_done, n + i + 1)
                                act.activation(sil[:, i % 3, :], ps[:, i % 3, 0:C], ACT.Silu).then_inc(sil_done, 1)
                            if i > 0:
                                act.wait_ge(hid_done, AHEAD + n + i)
                                act.activation(h_h[:, i - 1, :], hid[:, (i - 1) % 3, :], ACT.Copy).then_inc(h_high, 1)

            @block.vector
            def _(dve):
                dve.memset(cv[:, :, 0:3], 0.0).then_inc(set_up, 1)
                dve.wait_ge(nega, 1)
                dve.tensor_scalar(neg_a[:, :], neg_a[:, :], -1.0, None, ALU.mult).then_inc(set_up, 1)
                dve.wait_ge(set_up, 2)
                dve.wait_ge(raw_loaded, 16 * 5)
                norm_of = {"win": 0, "wout": 1, "w1": 2, "w3": 2}
                for n, i in norm_of.items():
                    for j in range(KD):
                        ins = dve.tensor_scalar(raw[n][:, j, :], raw[n][:, j, :], norms[:, i, j:j + 1], None, ALU.mult)
                    ins.then_inc(scaled if n in ("win", "wout") else ffn_scaled, 1)
                for i, n in enumerate(("win", "wout")):
                    dve.wait_ge(w_high, i + 1)
                    dve.tensor_tensor(w_of[n][1][:, :, :], raw[n], w_of[n][0][:, :, :].bitcast(F32),
                                      ALU.subtract).then_inc(w_low, 1)
                with dve.Fori(0, B) as b:
                    dve.wait_ge(r2_done, AHEAD + b)
                    dve.tensor_copy(xb[:, :, :], X[:, bass.ds(TB * b, TB), :]).then_inc(xb_copied, 1)
                    dve.wait_ge(xb_copied, b + 1)
                    ln.run(dve, b, lambda t: xb[:, t, :])
                    at = 6 * b
                    dve.wait_ge(rstd_ready, b + 1)
                    dve.wait_ge(ln.done, ln.steps * (b + 1))
                    dve.tensor_scalar(var[:, :], ln.ve[:, :], -EPS, None, ALU.add).then_inc(pre, 1)
                    dve.tensor_tensor(rstd2[:, :], rstd[:, :], rstd[:, :], ALU.mult).then_inc(pre, 1)
                    dve.wait_ge(pre, at + 2)
                    dve.tensor_tensor(v2[:, :], var[:, :], rstd2[:, :], ALU.mult).then_inc(pre, 1)
                    dve.wait_ge(pre, at + 3)
                    dve.tensor_scalar(v2[:, :], v2[:, :], EPS, None, ALU.add).then_inc(pre, 1)
                    for t in range(TB):
                        ins = dve.tensor_scalar(xh[:, t, :], xb[:, t, :], ln.mean[:, t:t + 1], rstd[:, t:t + 1],
                                                ALU.subtract, ALU.mult)
                    ins.then_inc(pre, 1)
                    dve.wait_ge(r1_ready, b + 1)
                    dve.tensor_tensor(rr[:, :], rstd[:, :], r1[:, :], ALU.mult).then_inc(pre, 1)
                    dve.wait_ge(pre, at + 6)
                    for t in range(TB):
                        ins = dve.tensor_scalar(hn[:, t, :], xb[:, t, :], ln.mean[:, t:t + 1], rr[:, t:t + 1],
                                                ALU.subtract, ALU.mult)
                    ins.then_inc(hn_ready, 1)

                    def low(n):
                        for k in range(KD):
                            dve.wait_ge(t_high, 6 * b + 2 * n + k + 1)
                            dve.tensor_tensor(ht_l[:, k, :], t_banks(k), ht_h[:, k, :].bitcast(F32),
                                              ALU.subtract).then_inc(t_low, 1)

                    low(0)
                    d0 = 11 * b
                    dve.wait_ge(dt_filled, b + 1)
                    raw_dt = ps[:, bank_small, 0:8].rearrange("p (t h) -> p t h", h=2)
                    wide = (lambda v: v.unsqueeze(1).to_broadcast([P, TB, 2]))
                    dve.tensor_tensor(xdt[:, :, :], raw_dt, wide(heads[:, 0, :]), ALU.add).then_inc(dts, 1)
                    dve.wait_ge(dts, d0 + 1)
                    dve.tensor_scalar(mdt[:, :, :], xdt[:, :, :], 0.0, None, ALU.max)
                    dve.scalar_tensor_tensor(adt[:, :, :], xdt[:, :, :], -1.0, xdt[:, :, :], ALU.mult, ALU.max
                                             ).then_inc(dts, 1)
                    dve.wait_ge(dt_act, 4 * b + 1)
                    dve.tensor_scalar(wdt[:, :, :], udt[:, :, :], 1.0, None, ALU.add).then_inc(dts, 1)
                    dve.wait_ge(dts, d0 + 3)
                    dve.tensor_scalar(ddt[:, :, :], wdt[:, :, :], -1.0, None, ALU.add).then_inc(dts, 1)
                    dve.wait_ge(dts, d0 + 4)
                    dve.tensor_scalar(zdt[:, :, :], ddt[:, :, :], 0.0, None, ALU.is_equal).then_inc(dts, 1)
                    dve.wait_ge(dts, d0 + 5)
                    dve.tensor_tensor(t2[:, :, :], zdt[:, :, :], udt[:, :, :], ALU.mult)
                    dve.tensor_tensor(dden[:, :, :], zdt[:, :, :], ddt[:, :, :], ALU.add).then_inc(dts, 1)
                    dve.wait_ge(dts, d0 + 6)
                    dve.reciprocal(rden[:, :, :], dden[:, :, :]).then_inc(dts, 1)
                    dve.wait_ge(dts, d0 + 7)
                    dve.tensor_tensor(qdt[:, :, :], udt[:, :, :], rden[:, :, :], ALU.mult).then_inc(softplus, 1)
                    dve.wait_ge(softplus, 4 * b + 1)
                    dve.wait_ge(dt_act, 4 * b + 2)
                    dve.tensor_tensor(tdt[:, :, :], qdt[:, :, :], lnw[:, :, :], ALU.mult).then_inc(softplus, 1)
                    dve.wait_ge(softplus, 4 * b + 2)
                    dve.tensor_tensor(sdt[:, :, :], tdt[:, :, :], t2[:, :, :], ALU.add).then_inc(softplus, 1)
                    dve.wait_ge(softplus, 4 * b + 3)
                    dve.tensor_tensor(dt[:, :, :], sdt[:, :, :], mdt[:, :, :], ALU.add).then_inc(softplus, 1)
                    dve.wait_ge(softplus, 4 * b + 4)
                    dve.tensor_tensor(dA[:, :, :], dt[:, :, :], wide(neg_a[:, :]), ALU.mult).then_inc(dts, 1)
                    for f in range(NF):
                        dve.wait_ge(feat_out, NF * b + f + 1)
                        n = 4 * (NF * b + f)
                        if f >= 2:
                            dve.wait_ge(conv_out, AHEAD + NF * b + f - 1)
                        else:
                            dve.wait_ge(conv_out, AHEAD + NF * b)
                        dve.tensor_scalar(ca[:, f % 2, :], cv[:, f, 0:S], conv_w[:, f, 0:1], None,
                                          ALU.mult).then_inc(conv, 1)
                        for j in range(1, 4):
                            dve.wait_ge(conv, n + j)
                            dve.scalar_tensor_tensor(ca[:, f % 2, :], cv[:, f, j:j + S], conv_w[:, f, j:j + 1],
                                                     ca[:, f % 2, :], ALU.mult, ALU.add).then_inc(conv, 1)
                        if f == 1:
                            dve.wait_ge(dt_act, 4 * b + 3)
                            dve.tensor_copy(csum[:, :, :], ps[:, bank_small, 8:16].rearrange("p (t h) -> p t h", h=2)
                                            ).then_inc(dts, 1)
                            dve.wait_ge(dts, d0 + 9)
                            dve.tensor_tensor(dif[:, :, :], ps[:, bank_small, 16:24].rearrange("p (t h) -> p t h", h=2),
                                              csum[:, :, :], ALU.subtract).then_inc(dts, 1)
                    dve.wait_ge(dt_act, 4 * b + 4)
                    dve.tensor_tensor(dec[:, :, :], dec0[:, :, :], dt[:, :, :], ALU.mult).then_inc(dts, 1)
                    dve.wait_ge(dts, d0 + 11)
                    dve.wait_ge(tm_out, 2 * b + 2)
                    for c in range(TB):
                        q = TB * b + c
                        dve.wait_ge(row_done, q + 1)
                        for h in range(2):
                            dve.scalar_tensor_tensor(dd[:, h, :], ps[:, bank_small, P * h:P * (h + 1)],
                                                     csum[:, c, h:h + 1], cap[:, :], ALU.subtract, ALU.min
                                                     ).then_inc(dd_done, 1)
                        dve.wait_ge(y_done, AHEAD + q)
                        for h in range(2):
                            dve.tensor_scalar(xd[:, h, :], xtm[:, c, :], dec[:, c, h:h + 1], None, ALU.mult)
                            ins = dve.tensor_scalar(t0[:, h, :], xtm[:, c, :], heads[:, 2, h:h + 1], None, ALU.mult)
                        ins.then_inc(xd_done, 1)
                        dve.wait_ge(ee_done, q + 1)
                        dve.wait_ge(g_done, q + 1)
                        for h in range(2):
                            ins = dve.scalar_tensor_tensor(mm[:, h, :], ps[:, c % 2, P * h:P * (h + 1)],
                                                           dt[:, c, h:h + 1], ee[:, h, :], ALU.mult, ALU.mult)
                        ins.then_inc(mm_done, 1)
                        if c < TB - 1:
                            dve.wait_ge(s_done, 3 * b + c + 1)
                            new, old = state[:, (c + 1) % 2], state[:, c % 2]
                            for h in range(2):
                                src = ps[:, 4, P * h:P * (h + 1)]
                                if c == 0:
                                    ins = dve.tensor_copy(new[:, h, :], src)
                                else:
                                    ins = dve.scalar_tensor_tensor(new[:, h, :], old[:, h, :], etot[:, c, h:h + 1], src,
                                                                   ALU.mult, ALU.add)
                            ins.then_inc(st_done, 1)
                        dve.wait_ge(y_done, AHEAD + q + 1)
                        dve.wait_ge(xd_done, q + 1)
                        yd = ps[:, 2 + c % 2, 0:2 * P]
                        flat = (lambda v: v[:, :, :].rearrange("p h n -> p (h n)"))
                        if c > 0:
                            for h in range(2):
                                ins = dve.scalar_tensor_tensor(y1[:, h, :], ps[:, 2 + c % 2, P * (2 + h):P * (3 + h)],
                                                               ecs[:, c, h:h + 1], t0[:, h, :], ALU.mult, ALU.add)
                            ins.then_inc(ys, 1)
                            dve.wait_ge(ys, 7 * b + 2 * c)
                            dve.tensor_tensor(flat(y2), yd, flat(y1), ALU.add).then_inc(ys, 1)
                            dve.wait_ge(ys, 7 * b + 2 * c + 1)
                        else:
                            dve.tensor_tensor(flat(y2), yd, flat(t0), ALU.add).then_inc(ys, 1)
                            dve.wait_ge(ys, 7 * b + 1)
                        dve.tensor_tensor(yg[:, c, :], flat(y2), sz[:, c, :], ALU.mult).then_inc(yg_done, 1)

                    def norm(i, src, dst):
                        dve.wait_ge(sq_done, AHEAD + 2 * TB * b + TB * (i + 1))
                        dve.tensor_scalar(ms[:, :], ss[:, :], 1.0 / D, EPS, ALU.mult, ALU.add).then_inc(norm_v, 1)
                        dve.wait_ge(rq_ready, 2 * b + i + 1)
                        for t in range(TB):
                            ins = dve.tensor_scalar(dst[:, t, :], src[:, t, :], rq[:, t:t + 1], None, ALU.mult)
                        ins.then_inc(hn_ready, 1)

                    norm(0, yg, hn)
                    low(1)
                    for i in range(2):
                        dve.wait_ge(o_done, 2 * b + i + 1)
                        v = xh[:, 2 * i:2 * i + 2, :].rearrange("p t d -> p (t d)")
                        dve.tensor_tensor(v, ps[:, i, :], v, ALU.add).then_inc(h2_done, 1)
                    norm(1, xh, hn)
                    low(2)
                    for u in range(2):
                        n = IT * 2 * b + IT * u
                        for i in range(IT + 1):
                            if i < IT:
                                dve.wait_ge(sil_done, n + i + 1)
                                if i >= 3:
                                    dve.wait_ge(h_low, n + i - 2)
                                dve.tensor_tensor(hid[:, i % 3, :], sil[:, i % 3, :], ps[:, i % 3, C:2 * C],
                                                  ALU.mult).then_inc(hid_done, 1)
                            if i > 0:
                                dve.wait_ge(h_high, n + i)
                                dve.tensor_tensor(h_l[:, i - 1, :], hid[:, (i - 1) % 3, :],
                                                  h_h[:, i - 1, :].bitcast(F32), ALU.subtract).then_inc(h_low, 1)
                        dve.wait_ge(down_done, 2 * b + u + 1)
                        dve.wait_ge(r2_done, AHEAD + b + 1)
                        dve.tensor_tensor(X[:, bass.ds(TB * b + U * u, U), :], ps[:, 3:5, 0:D], xb[:, U * u:U * u + U, :],
                                          ALU.add).then_inc(added, 1)
                    dve.wait_ge(added, AHEAD + 2 * (b + 1))

            @block.tensor
            def _(pe):
                pe.wait_ge(w_low, 2)
                pe.wait_ge(set_up, 2)
                with pe.Fori(0, B) as b:

                    def transposes(n, before):
                        pe.wait_ge(hn_ready, 3 * b + n + 1)
                        before()
                        for k in range(KD):
                            for t in range(TB):
                                ins = pe.transpose(t_banks(k)[:, P * t:P * (t + 1)], hn[:, t, P * k:P * (k + 1)],
                                                   ident[:, :])
                            ins.then_inc(t_filled, 1)
                        pe.wait_ge(t_low, 6 * b + 2 * (n + 1))

                    transposes(0, lambda: pe.wait_ge(added, AHEAD + 2 * b))
                    rows = (lambda k, at: (ht_h[:, k, at:at + P], ht_l[:, k, at:at + P]))
                    cols = (lambda w, k, lo, hi: (w[0][:, k, lo:hi], w[1][:, k, lo:hi]))
                    for t in range(TB):
                        for k in range(KD):
                            ins = product(pe, ps[:, bank_small, 2 * t:2 * t + 2], rows(k, P * t),
                                          cols(win, k, PROJ - 2, PROJ), k == 0, k == KD - 1)
                    ins.then_inc(dt_filled, 1)
                    for f in range(NF):
                        for k in range(KD):
                            at = D + P * f
                            ins = product(pe, ps[:, f, :], cols(win, k, at, at + P),
                                          (ht_h[:, k, :], ht_l[:, k, :]), k == 0, k == KD - 1)
                        ins.then_inc(feat, 1)
                    for i in range(2):
                        for t in range(2):
                            for k in range(KD):
                                ins = product(pe, t_banks(i)[:, D * t:D * (t + 1)], rows(k, P * (2 * i + t)),
                                              cols(win, k, 0, D), k == 0, k == KD - 1)
                        ins.then_inc(z_filled, 1)
                    pe.wait_ge(dts, 11 * b + 8)
                    flat = dA[:, :, :].rearrange("p t h -> p (t h)")
                    pe.matmul(ps[:, bank_small, 8:16], upper, flat, start=True, stop=True).then_inc(sums, 1)
                    pe.matmul(ps[:, bank_small, 16:24], ones, flat, start=True, stop=True).then_inc(sums, 1)
                    for i in range(2):
                        pe.wait_ge(z_out, 2 * b + i + 1)
                        pe.wait_ge(conv_out, AHEAD + NF * b + i + 1)
                        for t in range(TB):
                            ins = pe.transpose(t_banks(i)[:, P * t:P * (t + 1)], xc[:, i, P * t:P * (t + 1)], ident[:, :])
                        ins.then_inc(tm_filled, 1)
                    pe.wait_ge(conv_out, AHEAD + NF * (b + 1))
                    pe.wait_ge(feat_out, NF * (b + 1))
                    pe.wait_ge(dts, 11 * b + 10)
                    for c in range(TB):
                        q = TB * b + c
                        ch = slice(P * c, P * (c + 1))
                        pe.wait_ge(dd_done, AHEAD + 2 * q)
                        for h in range(2):
                            ins = pe.matmul(ps[:, bank_small, P * h:P * (h + 1)],
                                            dA[:, c, h:h + 1].to_broadcast([P, P]), upper, start=True, stop=True)
                        ins.then_inc(row_done, 1)
                        if c >= 2:
                            pe.wait_ge(mm_done, q - 1)
                        pe.matmul(ps[:, c % 2, 0:2 * P], xc[:, 1, ch], xc[:, 2:4, ch], start=True,
                                  stop=True).then_inc(g_done, 1)
                        if c >= 2:
                            pe.wait_ge(yg_done, q - 1)
                        if c > 0:
                            pe.wait_ge(st_done, 3 * b + c)
                            for h in range(2):
                                pe.matmul(ps[:, 2 + c % 2, P * (2 + h):P * (3 + h)], xc[:, 2 + h, ch],
                                          state[:, c % 2, h, :], start=True, stop=True)
                        if c < TB - 1:
                            pe.wait_ge(xd_done, q + 1)
                            pe.wait_ge(tm_out, 2 * (b + 1))
                            pe.matmul(ps[:, 4, 0:2 * P], btm[:, c, :], xd[:, :, :], start=True, stop=True).then_inc(s_done, 1)
                        pe.wait_ge(mm_done, q + 1)
                        for h in range(2):
                            ins = pe.matmul(ps[:, 2 + c % 2, P * h:P * (h + 1)], mm[:, h, :], xtm[:, c, :], start=True,
                                            stop=True)
                        ins.then_inc(y_done, 1)
                    transposes(1, lambda: None)
                    pe.wait_ge(mm_done, TB * (b + 1))
                    for i in range(2):
                        for t in range(2):
                            for k in range(KD):
                                ins = product(pe, ps[:, i, D * t:D * (t + 1)], rows(k, P * (2 * i + t)),
                                              cols(wout, k, 0, D), k == 0, k == KD - 1)
                        ins.then_inc(o_done, 1)
                    transposes(2, lambda: pe.wait_ge(ffn_low, 3))
                    for u in range(2):
                        n = IT * 2 * b + IT * u
                        for i in range(IT + 2):
                            if i < IT:
                                pe.wait_ge(hid_done, AHEAD + n + max(i - 2, 0))
                                for j, w in enumerate((w1, w3)):
                                    for k in range(KD):
                                        ins = product(pe, ps[:, i % 3, C * j:C * (j + 1)], cols(w, k, P * i, P * (i + 1)),
                                                      (ht_h[:, k, C * u:C * (u + 1)], ht_l[:, k, C * u:C * (u + 1)]),
                                                      k == 0, k == KD - 1)
                                ins.then_inc(up_done, 1)
                            if i >= 2:
                                d = i - 2
                                if d == 0:
                                    pe.wait_ge(added, AHEAD + 2 * b + u)
                                pe.wait_ge(h_low, n + d + 1)
                                for t in range(U):
                                    ins = product(pe, ps[:, 3 + t, 0:D],
                                                  (h_h[:, d, P * t:P * (t + 1)], h_l[:, d, P * t:P * (t + 1)]),
                                                  (w2[0][:, d, :], w2[1][:, d, :]), d == 0, d == IT - 1)
                        ins.then_inc(down_done, 1)
        m.close()


def build(nc, a, out, stages=4):
    with ExitStack() as ctx:
        m = Memory(nc, ctx, "all")
        X = m.sb("x", [P, TILES, D])
        banks = ctx.enter_context(nc.psum_tensor("banks", [P, 8, S], F32))
        ident = m.sb("ident", [P, P])
        upper, ones = m.sb("upper", [P, P]), m.sb("ones", [P, P])
        rank, first_slot = m.sb("rank", [P, TB, E]), m.sb("first_slot", [P, TB, E])
        zero_rows = m.sb("zero_rows", [P, D])
        loaded, stored, zeroed, zero_set = m.sem("loaded"), m.sem("stored"), m.sem("zeroed"), m.sem("zero_set")
        xd = [nc.dram_tensor(f"dispatched{i}", (E * C, D), F32, kind="Internal").ap() for i in range(2)]
        oe = [nc.dram_tensor(f"expert_rows{i}", (E * C, D), F32, kind="Internal").ap() for i in range(2)]
        consts = (upper[:, :], ones[:, :], rank[:, :, :], first_slot[:, :, :])
        with nc.Block() as block:

            @block.sync
            def _(sp):
                sp.dma_start(ident[:, :], a["ident"]).then_inc(loaded, 16)
                sp.dma_start(upper[:, :], a["upper"]).then_inc(loaded, 16)
                sp.dma_start(ones[:, :], a["ones"]).then_inc(loaded, 16)
                sp.dma_start(rank[:, :, :], a["rank"]).then_inc(loaded, 16)
                sp.dma_start(first_slot[:, :, :], a["first_slot"]).then_inc(loaded, 16)
                sp.wait_ge(zero_set, 1)
                sp.wait_ge(loaded, 16 * 5)

            @block.vector
            def _(dve):
                dve.memset(zero_rows[:, :], 0.0).then_inc(zero_set, 1)

        if stages >= 1:
            attention_stage(nc, a["x"], a["wqkv"], a["wo"], a["rope"], X, ident, banks, xd, zero_rows, zeroed)
        raw_loaded = m.sem("raw_loaded")
        with ExitStack() as held:
            raw = {}
            for n, chunks, width in (("win", KD, PROJ), ("wout", KD, D), ("w1", KD, INTER), ("w3", KD, INTER),
                                     ("w2", IT, D)):
                raw[n] = held.enter_context(nc.sbuf_tensor(f"raw_{n}", [P, chunks, width], F32))[:, :, :]
            if stages >= 2:
                experts_stage(nc, "moe1", a["w13"], a["w2a"], a["w2b"], a["wg"], X, ident, consts, xd[0], oe[0], banks,
                              zeroed, 1, [(raw[n], a[n]) for n in raw], raw_loaded)
            if stages >= 3:
                state_space_stage(nc, a, X, ident, consts, banks, raw, raw_loaded)
        if stages >= 4:
            experts_stage(nc, "moe2", a["w13"], a["w2a"], a["w2b"], a["wg"], X, ident, consts, xd[1], oe[1], banks,
                          zeroed, 2)
        with nc.Block() as block:

            @block.sync
            def _(sp):
                sp.dma_start(out.rearrange("b (t p) d -> p (b t) d", p=P), X[:, :, :]).then_inc(stored, 16)
                sp.wait_ge(stored, 16)


def layout(inputs):
    g = {k.removeprefix("L0_"): np.asarray(v) for k, v in inputs.items()}
    arrays = {"x": g["attn_a_x"]}
    heads = [2 * (2 * m + half) + r for m in range(NKV // 2) for r in range(2) for half in range(2)]
    halves = [d for p in range(2) for d in range(p, HD, 2)]
    qcols = [HD * h + d for h in heads for d in halves]
    kcols = [HD * j + d for j in range(NKV) for d in halves]
    arrays["wqkv"] = np.concatenate([g["attn_a_wq"][:, qcols], g["attn_a_wk"][:, kcols], g["attn_a_wv"]], axis=1)
    arrays["wo"] = g["attn_a_wo"]
    f = np.float32
    inv = f(1.0) / (f(10000.0) ** (np.arange(0, HD, 2, dtype=f) / f(HD)))
    ang = np.arange(S, dtype=f)[:, None] * inv[None, :]
    arrays["rope"] = np.stack([np.tile(np.cos(ang), 2), np.tile(np.sin(ang), 2)], axis=1).astype(f)
    arrays["ident"] = np.eye(P, dtype=f)
    arrays["upper"] = np.triu(np.ones((P, P), f))
    arrays["ones"] = np.ones((P, P), f)
    arrays["rank"] = np.broadcast_to(np.arange(E, 0, -1, dtype=f), (P, TB, E))
    arrays["first_slot"] = np.broadcast_to(np.arange(E, dtype=f) * C - 1, (P, TB, E))
    w1 = np.concatenate([g["ffn_W1"], g["ffn_sw1"][None]]).reshape(E + 1, KD, P, H)
    w3 = np.concatenate([g["ffn_W3"], g["ffn_sw3"][None]]).reshape(E + 1, KD, P, H)
    w2 = np.concatenate([g["ffn_W2"], g["ffn_sw2"][None]])
    arrays["w13"] = np.stack([w1, w3], axis=3).transpose(0, 2, 1, 3, 4).reshape(E + 1, P, 2 * KD * H)
    arrays["w2a"] = w2[:, :2 * P].reshape(E + 1, 2, P, D).transpose(0, 2, 1, 3).reshape(E + 1, P, 2 * D)
    arrays["w2b"] = w2[:, 2 * P:]
    arrays["wg"] = g["ffn_Wg"]
    arrays["win"], arrays["wout"] = g["attn_b_W_in"], g["attn_b_W_out"]
    arrays["w1"], arrays["w3"], arrays["w2"] = g["attn_b_w1"], g["attn_b_w3"], g["attn_b_w2"]
    arrays["norms"] = np.stack([g["attn_b_ln1_w"], g["attn_b_norm_w"], g["attn_b_ln2_w"]]
                               ).reshape(3, KD, P).transpose(2, 0, 1)
    arrays["conv_w"] = g["attn_b_conv_w"].reshape(4, 4, P).transpose(2, 1, 0)
    arrays["conv_b"] = g["attn_b_conv_b"].reshape(4, P).T
    arrays["heads"] = np.concatenate([g["attn_b_dt_bias"], g["attn_b_A_log"], g["attn_b_D"]])
    arrays["cap"] = np.tril(np.full((P, P), -1e30, f), -1)
    return {k: np.ascontiguousarray(v) for k, v in arrays.items()}


def kernel(**inputs):
    import concourse.bacc as bacc
    from concourse.bass_utils import run_bass_kernel_spmd

    nc = bacc.Bacc("TRN2", target_bir_lowering=False, num_devices=1)
    arrays = layout(inputs)
    aps = {k: nc.dram_tensor(f"in_{k}", v.shape, mybir.dt.from_np(v.dtype), kind="ExternalInput").ap()
           for k, v in arrays.items()}
    out = nc.dram_tensor("out_x", (B, S, D), F32, kind="ExternalOutput").ap()
    build(nc, aps, out)
    r = run_bass_kernel_spmd(nc, [{f"in_{k}": v for k, v in arrays.items()}], core_ids=[0])
    return r.results[0]["out_x"]
```

```python
from contextlib import ExitStack

import numpy as np

import concourse.bass as bass
from concourse import mybir

F32 = mybir.dt.float32
F32R = mybir.dt.float32r
U32 = mybir.dt.uint32
ALU = mybir.AluOpType
ACT = mybir.ActivationFunctionType
AX_X = mybir.AxisListType.X

P = 128
B, S, D = 4, 512, 256
KD = D // P
TB = S // P
TILES = B * TB
NH, NKV, HD = 16, 8, 16
QC, KC = NH * HD, NKV * HD
SLOTS = 4
PACKS = NH // 2
E, H, C = 8, 352, 256
HT = [P, P, H - 2 * P]
U = C // P
UNITS = TILES // U
XB, DI, INTER = 128, 256, 1024
PROJ = 2 * DI + 2 * XB + 2
IT = INTER // P
EPS = 1e-5
AHEAD = 1


class Ring:

    def __init__(self, size, first, body, last, owner, steps=None):
        self.size, self.uses, self.owner = size, {"first": first, "body": body, "last": last}, owner
        self.steps = steps or {}
        assert len(first) % size == 0 and len(body) % size == 0

    def increments(self, names, owner):
        return sum(self.steps.get(owner, 1) for n in names if self.owner(n) == owner)

    def before(self, phase, owner):
        kind, it = phase
        if kind == "first":
            return 0
        return self.increments(self.uses["first"], owner) + self.increments(self.uses["body"], owner) * it

    def index(self, phase, name):
        return self.uses[phase[0]].index(name)

    def slot(self, phase, name):
        return self.index(phase, name) % self.size

    def filled(self, phase, name):
        kind, it = phase
        n = self.index(phase, name) + 1
        return n if kind == "first" else len(self.uses["first"]) + len(self.uses["body"]) * it + n

    def emptied(self, phase, name, owner):
        i = self.index(phase, name)
        return AHEAD + self.before(phase, owner) + self.increments(self.uses[phase[0]][:i + 1], owner)

    def wait_free(self, eng, sems, phase, name):
        i = self.index(phase, name)
        if i >= self.size:
            last = self.uses[phase[0]][i - self.size]
            o = self.owner(last)
            eng.wait_ge(sems[o], self.emptied(phase, last, o))
        elif phase[0] != "first":
            tails = [self.uses[k][len(self.uses[k]) - self.size + i:] for k in ("first", "body")]
            o = self.owner(tails[0][0])
            if o == self.owner(tails[1][0]):
                late = [self.increments(t[1:], o) for t in tails]
                assert late[0] == late[1]
                eng.wait_ge(sems[o], AHEAD + self.before(phase, o) - late[0])
            else:
                for o in (o, self.owner(tails[1][0])):
                    eng.wait_ge(sems[o], AHEAD + self.before(phase, o))


def product(pe, out, a, b, first, last):
    pe.matmul(out, a[0], b[0], start=first, stop=False)
    pe.matmul(out, a[0], b[1], start=False, stop=False)
    return pe.matmul(out, a[1], b[0], start=False, stop=last)


class Memory:

    def __init__(self, nc, ctx, stage, banks=None):
        self.nc, self.ctx, self.stage, self.banks, self.used = nc, ctx, stage, banks, 0
        self.sems, self.ahead = [], []

    def sb(self, name, shape, dt=F32):
        return self.ctx.enter_context(self.nc.sbuf_tensor(f"{self.stage}_{name}", shape, dt))

    def pair(self, name, shape):
        return self.sb(name + "_hi", shape, F32R), self.sb(name + "_lo", shape, F32R)

    def psum(self, shape):
        n = int(np.prod(shape[1:])) // S
        v = self.banks[:, self.used:self.used + n, :]
        self.used += n
        assert self.used <= 8
        if len(shape) == 4:
            return v.rearrange("p b n -> p (b n)").rearrange("p (x y z) -> p x y z", x=shape[1], y=shape[2])
        return v if len(shape) == 3 else v[:, 0, :]

    def sem(self, name, keep=False, ahead=False):
        h = self.nc.alloc_semaphore(f"{self.stage}_{name}")
        if ahead:
            self.ahead.append(h)
        if not keep:
            self.sems.append(h)
        return h

    def open(self):
        for h in self.ahead:
            self.nc.gpsimd.sem_inc(h, AHEAD)
        self.nc.all_engine_barrier()

    def close(self):
        self.nc.clear_and_free_semaphores(self.sems)
        self.nc.all_engine_barrier()


class RowStats:

    def __init__(self, m, name, n):
        self.n = n
        self.stats = m.sb(name + "_stats", [P, n, 6])
        self.tmp = m.sb(name + "_tmp", [P, 5, n])
        self.mean = m.sb(name + "_mean", [P, n])
        self.ve = m.sb(name + "_ve", [P, n])
        self.done = m.sem(name + "_done")
        self.steps = n + 7

    def run(self, dve, it, rows):
        n, s, done, base = self.n, self.stats, self.done, self.steps * it
        tot, dif, m2, q, m2e = (self.tmp[:, i, :] for i in range(5))
        for t in range(n):
            dve.bn_stats(s[:, t, :], rows(t)).then_inc(done, 1)
        dve.wait_ge(done, base + n)
        dve.tensor_tensor(tot, s[:, :, 1], s[:, :, 4], ALU.add).then_inc(done, 1)
        dve.tensor_tensor(dif, s[:, :, 1], s[:, :, 4], ALU.subtract).then_inc(done, 1)
        dve.tensor_tensor(m2, s[:, :, 2], s[:, :, 5], ALU.add).then_inc(done, 1)
        dve.wait_ge(done, base + n + 3)
        dve.tensor_scalar(self.mean[:, :], tot, 0.5, None, ALU.mult).then_inc(done, 1)
        dve.scalar_tensor_tensor(q, dif, 0.25, dif, ALU.mult, ALU.mult).then_inc(done, 1)
        dve.tensor_scalar(m2e, m2, 1.0 / D, EPS, ALU.mult, ALU.add).then_inc(done, 1)
        dve.wait_ge(done, base + n + 6)
        dve.tensor_tensor(self.ve[:, :], q, m2e, ALU.add).then_inc(done, 1)


def attention_stage(nc, x_dram, wqkv, wo, rope, X, ident, banks, xd, zero_rows, zeroed, const_loaded, const_loads):
    with ExitStack() as ctx:
        m = Memory(nc, ctx, "attn", banks)
        sb, sem = m.sb, m.sem
        w_in = sb("w_in", [P, KD, 2 * D])
        w_h, w_l = m.pair("wqkv", [P, KD, 2 * D])
        wo_in = sb("wo_in", [P, KD, D])
        wo_h, wo_l = m.pair("wo", [P, KD, D])
        cs = sb("rope", [P, TB, 2, HD])
        xb = sb("xb", [P, TB, D])
        ln = RowStats(m, "ln", TB)
        rstd = sb("rstd", [P, TB])
        nhalf = sb("nhalf", [P, TB])
        xn = sb("xn", [P, TB, D])
        xt_h, xt_l = m.pair("xt", [P, KD, S])
        rc = sb("rc", [P, 2, 24, HD])
        rs = sb("rs", [P, 2, 24, HD])
        qk = sb("qk", [P, TB, 24, HD])
        st = sb("st", [P, TB, 24, SLOTS, HD])
        vn = sb("vn", [P, TB, NKV, HD])
        v = sb("v", [P, TB, NKV, 32])
        qp = sb("qp", [P, PACKS, S], F32R)
        kz = sb("kz", [P, NKV, S], F32R)
        nm = sb("nm", [P, TB, NH])
        pt = sb("pt", [P, 3, 4, S])
        ot = sb("ot", [P, 2, S])
        rec = sb("rec", [P, 2, TB, 4])
        ao = sb("ao", [P, TB, D])
        at_h, at_l = m.pair("at", [P, KD, S])

        ps_ring = m.psum([P, 2, 2, S])
        ps_sc = m.psum([P, 2, S])
        ps_pv = m.psum([P, S])
        ps_m = m.psum([P, S])

        w_loaded, wo_loaded, c_loaded, x_loaded = sem("w_loaded"), sem("wo_loaded"), sem("c_loaded"), sem("x_loaded")
        set_up, w_act, w_split = sem("set_up"), sem("w_act"), sem("w_split")
        kz_zeroed, nhalf_set = sem("kz_zeroed"), sem("nhalf_set")
        xb_copied, rstd_ready, xn_ready = sem("xb_copied"), sem("rstd_ready"), sem("xn_ready", ahead=True)
        filled = sem("filled")
        emptied = {"dve": sem("emptied_dve", ahead=True), "act": sem("emptied_act", ahead=True)}
        xt_hi = sem("xt_hi")
        v_copied, rotated, qk_ready = sem("v_copied"), sem("rotated", ahead=True), sem("qk_ready", ahead=True)
        v_moved = sem("v_moved")
        emptied["rot"] = rotated
        spare_zeroed = sem("spare_zeroed")
        k_hi, k_low, k_copied = sem("k_hi"), sem("k_low", ahead=True), sem("k_copied")
        q_hi, q_low, q_copied = sem("q_hi"), sem("q_low", ahead=True), sem("q_copied")
        aux0, aux1 = sem("aux0"), sem("aux1", ahead=True)
        m_filled = sem("m_filled")
        m_emptied = {"dve": sem("m_emptied_dve", ahead=True), "act": sem("m_emptied_act", ahead=True)}
        at_hi = sem("at_hi")
        sc_filled, exp_done, pv_done, ot_copied, rec_ready = (
            sem("sc_filled"), sem("exp_done", ahead=True), sem("pv_done", ahead=True), sem("ot_copied", ahead=True),
            sem("rec_ready"))

        STEPS, UNIT, LEAD = 16, 8, 10
        EARLY = {13: (0, 1), 14: (2, 3), 15: (4, 5, 6, 7)}
        LATE = ((), (8, 9))
        HEAD = 3
        END = {0: ("at0",), 1: ("at1",), 2: ("wo0", "wo1")}
        ENDS = [n for s in range(HEAD) for n in END[s]]
        units = [f"max{n}" for n in range(4 * UNIT)]
        NORM, SCALE, TURN, PROJECT, KEYS, PARTS = 3, 4, 5, (6, 8), (7, 9), 11
        PACKED = {10: ("k0",), 12: ("q0", "q1"), 15: ("q2",)}
        PACKED_LAST = ("k1", "q3")

        def step_units(s):
            return range(LEAD + 2 * s, min(LEAD + 2 * s + 2, 4 * UNIT))

        head = [units[n] for s in range(HEAD) for n in step_units(s)]
        first = ["xt0", "xt1", "qkv0", "qkv1", "k0", "q0", "k1", "q1", "q2", "q3"] + units[:LEAD] + head
        body, last = [], []
        for s in range(HEAD, STEPS):
            body += [units[n] for n in step_units(s)]
            last += [units[n] for n in step_units(s)]
            if s == TURN:
                body += ["xt0", "xt1"]
            if s in PROJECT:
                body += [f"qkv{PROJECT.index(s)}"]
            body += PACKED.get(s, ())
            body += [units[n] for n in EARLY.get(s, ())]
        body += list(PACKED_LAST) + [units[n] for ns in LATE for n in ns] + head
        OWNER = {"qkv0": "rot", "qkv1": "rot", "k0": "act", "q1": "act", "q3": "act", "q2": "act"}
        ring = Ring(2, first, body, last, lambda n: OWNER.get(n, "dve"), {"rot": 4})
        last = []
        for g in range(4):
            if g > 0:
                last += [f"ot{g - 1}"]
            if g < 3:
                last += [f"retr{g + 1}a", f"retr{g + 1}b"]
        last += ["ot3"]
        misc = Ring(1, ["retr0a", "retr0b"], last + ["retr0a", "retr0b"] + ENDS, last + ENDS,
                    lambda n: "act" if n.startswith("retr") else "dve")

        def rows(eng, body):
            with eng.Fori(0, B - 1) as b:
                body(("body", b), b, False)
            body(("last", B - 1), B - 1, True)

        FIRST = ("first", 0)

        m.open()
        with nc.Block() as block:

            @block.sync
            def _(sp):
                for b in range(B):
                    if b > 0:
                        sp.wait_ge(x_loaded, 16 * b)
                    sp.dma_start(X[:, TB * b:TB * (b + 1), :],
                                 x_dram[b].rearrange("(t p) d -> p t d", p=P)).then_inc(x_loaded, 16)
                    if b == 0:
                        sp.dma_start(w_in[:, :, :], wqkv.rearrange("(k p) n -> p k n", p=P)).then_inc(w_loaded, 16)
                        sp.dma_start(cs[:, :, :, :], rope.rearrange("(t p) a n -> p t a n", p=P)).then_inc(c_loaded, 16)
                        sp.dma_start(wo_in[:, :, :], wo.rearrange("(k p) n -> p k n", p=P)).then_inc(wo_loaded, 16)
                for dst in xd:
                    sp.dma_start(dst.rearrange("(r p) d -> p r d", p=P),
                                 zero_rows[:, :].unsqueeze(1).to_broadcast([P, E * C // P, D])).then_inc(zeroed, 16)
                sp.wait_ge(x_loaded, 16 * B)

            @block.gpsimd
            def _(pool):
                pool.memset(nhalf[:, :], -0.5).then_inc(nhalf_set, 1)
                pool.memset(v[:, :, :, HD:32], 0.0).then_inc(set_up, 1)
                pool.memset(st[:, :, :, 3, :], 0.0).then_inc(set_up, 1)
                pool.wait_ge(nhalf_set, 1)

                def power(r):
                    pool.wait_ge(ln.done, ln.steps * (r + 1))
                    pool.wait_ge(xn_ready, AHEAD + TB * r)
                    pool.tensor_tensor(rstd[:, :], ln.ve[:, :], nhalf[:, :], ALU.pow).then_inc(rstd_ready, 1)

                def rotation_sums(r, i):
                    for t in (2 * i, 2 * i + 1):
                        pool.wait_ge(rotated, AHEAD + 2 * (TB * r + t) + 2)
                        pool.wait_ge(q_low, AHEAD + TB * r)
                        pool.tensor_tensor(qk[:, t, :, 0:8], rc[:, t % 2, :, 0:8], rs[:, t % 2, :, 8:16],
                                           ALU.subtract).then_inc(qk_ready, 1)
                        pool.tensor_tensor(qk[:, t, :, 8:16], rs[:, t % 2, :, 0:8], rc[:, t % 2, :, 8:16],
                                           ALU.add).then_inc(qk_ready, 1)

                def key_low_parts(r, i):
                    for t in (2 * i, 2 * i + 1):
                        pool.wait_ge(k_hi, TB * r + t + 1)
                        pool.tensor_tensor(st[:, t, NH:24, 2, :], qk[:, t, NH:24, :], st[:, t, NH:24, 0, :],
                                           ALU.subtract).then_inc(k_low, 1)

                def prepare(r):
                    power(r)
                    for i in range(2):
                        rotation_sums(r, i)
                        key_low_parts(r, i)

                power(0)
                pool.memset(kz[:, :, :].bitcast(F32), 0.0).then_inc(kz_zeroed, 1)
                for i in range(2):
                    rotation_sums(0, i)
                    key_low_parts(0, i)
                with pool.Fori(0, B - 1) as b:
                    prepare(b + 1)

            @block.scalar
            def _(act):
                act.wait_ge(w_loaded, 16)
                act.activation(w_h[:, :, :], w_in[:, :, :], ACT.Copy).then_inc(w_act, 1)

                def turned(phase, r):
                    for k in range(KD):
                        act.wait_ge(filled, ring.filled(phase, f"xt{k}"))
                        act.activation(xt_h[:, k, :], ps_ring[:, ring.slot(phase, f"xt{k}"), 0, :],
                                       ACT.Copy).then_inc(xt_hi, 1)

                def values(phase, r, i):
                    act.wait_ge(filled, ring.filled(phase, f"qkv{i}"))
                    act.activation(vn[:, 2 * i:2 * i + 2, :, :],
                                   ps_ring[:, ring.slot(phase, f"qkv{i}"), :, QC + KC:].rearrange(
                                       "p t (j d) -> p t j d", d=HD), ACT.Copy).then_inc(v_copied, 1)

                def key_copies(r, i):
                    for t in (2 * i, 2 * i + 1):
                        act.wait_ge(k_hi, TB * r + t + 1)
                        act.activation(st[:, t, NH:24, 1, :], st[:, t, NH:24, 0, :], ACT.Copy).then_inc(k_copied, 1)

                def query_copies(r):
                    for t in range(TB):
                        act.wait_ge(q_hi, TB * r + t + 1)
                        act.activation(st[:, t, 0:NH, 2, :], st[:, t, 0:NH, 0, :], ACT.Copy).then_inc(q_copied, 1)

                def pack(phase, names):
                    for name in names:
                        if OWNER.get(name) == "act":
                            act.wait_ge(filled, ring.filled(phase, name))
                            src = ps_ring[:, ring.slot(phase, name), :, :]
                            if name == "k0":
                                act.activation(kz[0:64, 0:4:2, :], src[0:64], ACT.Copy)
                                act.activation(kz[64:P, 1:4:2, :], src[64:P], ACT.Copy).then_inc(emptied["act"], 1)
                            else:
                                n = 2 * int(name[1])
                                act.activation(qp[:, n:n + 2, :], src, ACT.Copy).then_inc(emptied["act"], 1)

                def move_values(r):
                    act.wait_ge(v_copied, 2 * (r + 1))
                    act.wait_ge(pv_done, AHEAD + STEPS * r)
                    act.activation(v[:, :, :, 0:HD], vn[:, :, :, :], ACT.Copy).then_inc(v_moved, 1)

                def requery(phase, g, j):
                    act.wait_ge(m_filled, misc.filled(phase, f"retr{g}{'ab'[j]}"))
                    act.activation(qp[:, 2 * g + j, :], ps_m[:, :], ACT.Copy).then_inc(m_emptied["act"], 1)

                def copy_out(phase, b, g):
                    act.wait_ge(pv_done, AHEAD + STEPS * b + 4 * g + 4)
                    if g >= 2:
                        act.wait_ge(m_filled, misc.filled(phase, f"ot{g - 2}"))
                    act.activation(ot[:, g % 2, :], ps_pv[:, :], ACT.Copy).then_inc(ot_copied, 1)

                def step(phase, b, s, prepare):
                    g, kt = s // 4, s % 4
                    for a in range(4):
                        act.wait_ge(sc_filled, 64 * b + 4 * s + a + 1)
                        if a == 0:
                            act.wait_ge(pv_done, AHEAD + STEPS * b + max(s - 2, 0))
                        act.activation(pt[:, s % 3, a, :], ps_sc[:, a % 2, :], ACT.Exp,
                                       scale=HD ** -0.5).then_inc(exp_done, 1)
                        if kt == 3 and g < 3 and a in (1, 2):
                            requery(phase, g + 1, a - 1)
                    if kt == 1 and g > 0:
                        copy_out(phase, b, g - 1)
                    if prepare:
                        if s == TURN:
                            turned(phase, b + 1)
                        if s in PROJECT:
                            values(phase, b + 1, PROJECT.index(s))
                        if s in KEYS:
                            key_copies(b + 1, KEYS.index(s))
                        if s == PARTS:
                            query_copies(b + 1)
                        pack(phase, PACKED.get(s, ()))

                def end(phase, b, name):
                    if name in ("at0", "at1"):
                        k = int(name[2])
                        act.wait_ge(m_filled, misc.filled(phase, name))
                        act.activation(at_h[:, k, :], ps_m[:, :], ACT.Copy).then_inc(at_hi, 1)

                turned(FIRST, 0)
                values(FIRST, 0, 0)
                values(FIRST, 0, 1)
                key_copies(0, 0)
                key_copies(0, 1)
                query_copies(0)
                act.wait_ge(kz_zeroed, 1)
                act.wait_ge(set_up, 4)
                pack(FIRST, ("k0", "q0", "k1", "q1", "q2", "q3"))
                move_values(0)
                requery(FIRST, 0, 0)
                requery(FIRST, 0, 1)
                for s in range(HEAD):
                    step(FIRST, 0, s, False)
                act.wait_ge(wo_loaded, 16)
                act.activation(wo_h[:, :, :], wo_in[:, :, :], ACT.Copy).then_inc(w_act, 1)

                def row(phase, b, last):
                    for s in range(HEAD, STEPS):
                        step(phase, b, s, not last)
                    if not last:
                        pack(phase, PACKED_LAST)
                    copy_out(phase, b, 3)
                    if not last:
                        move_values(b + 1)
                        requery(phase, 0, 0)
                        requery(phase, 0, 1)
                    for s in range(HEAD):
                        if not last:
                            step(phase, b + 1, s, False)
                        for name in END[s]:
                            end(phase, b, name)

                rows(act, row)

            @block.vector
            def _(dve):

                def statistics(r):
                    dve.wait_ge(x_loaded, 16 * (r + 1))
                    dve.tensor_copy(xb[:, :, :], X[:, bass.ds(TB * r, TB), :]).then_inc(xb_copied, 1)
                    dve.wait_ge(xb_copied, r + 1)
                    ln.run(dve, r, lambda t: xb[:, t, :])

                def scale_rows(r):
                    dve.wait_ge(rstd_ready, r + 1)
                    for t in range(TB):
                        dve.tensor_scalar(xn[:, t, :], xb[:, t, :], ln.mean[:, t:t + 1], rstd[:, t:t + 1],
                                          ALU.subtract, ALU.mult).then_inc(xn_ready, 1)

                def turned(phase, r):
                    for k in range(KD):
                        dve.wait_ge(xt_hi, KD * r + k + 1)
                        dve.tensor_tensor(xt_l[:, k, :], ps_ring[:, ring.slot(phase, f"xt{k}"), 0, :],
                                          xt_h[:, k, :].bitcast(F32), ALU.subtract).then_inc(emptied["dve"], 1)

                def rotate(phase, r, i):
                    name = f"qkv{i}"
                    dve.wait_ge(filled, ring.filled(phase, name))
                    dve.wait_ge(v_copied, 2 * r + i + 1)
                    for t in (2 * i, 2 * i + 1):
                        if t >= 2:
                            dve.wait_ge(qk_ready, AHEAD + 2 * (TB * r + t - 1))
                        else:
                            dve.wait_ge(qk_ready, AHEAD + 2 * TB * r)
                        src = ps_ring[:, ring.slot(phase, name), t % 2, 0:QC + KC].rearrange(
                            "p (h d) -> p h d", d=HD)
                        dve.tensor_tensor(rc[:, t % 2, :, :], src, cs[:, t, 0:1, :].to_broadcast([P, 24, HD]),
                                          ALU.mult).then_inc(rotated, 1)
                        dve.tensor_tensor(rs[:, t % 2, :, :], src, cs[:, t, 1:2, :].to_broadcast([P, 24, HD]),
                                          ALU.mult).then_inc(rotated, 1)

                def key_parts(r, i):
                    for t in (2 * i, 2 * i + 1):
                        dve.wait_ge(qk_ready, AHEAD + 2 * (TB * r + t) + 2)
                        dve.tensor_copy(st[:, t, NH:24, 0, :].bitcast(F32R), qk[:, t, NH:24, :]).then_inc(k_hi, 1)

                def query_parts(r):
                    dve.memset(st[:, :, 0:NH, 3, 0:2], 0.0).then_inc(spare_zeroed, 1)
                    for t in range(TB):
                        dve.tensor_copy(st[:, t, 0:NH, 0, :].bitcast(F32R), qk[:, t, 0:NH, :]).then_inc(q_hi, 1)
                    for t in range(TB):
                        dve.wait_ge(q_hi, TB * r + t + 1)
                        dve.tensor_tensor(st[:, t, 0:NH, 1, :], qk[:, t, 0:NH, :], st[:, t, 0:NH, 0, :],
                                          ALU.subtract).then_inc(q_low, 1)

                def pack(phase, names):
                    for name in names:
                        if name not in OWNER:
                            dve.wait_ge(filled, ring.filled(phase, name))
                            src = ps_ring[:, ring.slot(phase, name), :, :]
                            if name == "k1":
                                dve.tensor_copy(kz[0:64, 4:8:2, :], src[0:64])
                                dve.tensor_copy(kz[64:P, 5:8:2, :], src[64:P]).then_inc(emptied["dve"], 1)
                            else:
                                n = 2 * int(name[1])
                                dve.tensor_copy(qp[:, n:n + 2, :], src).then_inc(emptied["dve"], 1)

                def maxima(phase, r, ns):
                    for n in ns:
                        i, qt = n // 2, 2 * (n % 2)
                        dve.wait_ge(filled, ring.filled(phase, units[n]))
                        if n == 0:
                            dve.wait_ge(aux1, AHEAD + 4 * r)
                        dve.tensor_reduce(nm[:, qt:qt + 2, i], ps_ring[:, ring.slot(phase, units[n]), :, :],
                                          AX_X, ALU.max, negate=True).then_inc(emptied["dve"], 1)

                def spare_rows(phase, r, g):
                    h = slice(4 * g, 4 * g + 4)
                    dve.wait_ge(emptied["dve"], ring.emptied(phase, units[UNIT * g + UNIT - 1], "dve"))
                    dve.tensor_copy(st[:, :, h, 3, 0].bitcast(F32R), nm[:, :, h]).then_inc(aux0, 1)
                    dve.wait_ge(aux0, 4 * r + g + 1)
                    dve.tensor_tensor(st[:, :, h, 3, 1], nm[:, :, h], st[:, :, h, 3, 0],
                                      ALU.subtract).then_inc(aux1, 1)

                def first_maxima(phase, r, ns):
                    maxima(phase, r, ns)
                    if UNIT - 1 in ns:
                        spare_rows(phase, r, 0)

                statistics(0)
                scale_rows(0)
                dve.wait_ge(w_act, 1)
                dve.tensor_tensor(w_l[:, :, :], w_in[:, :, :], w_h[:, :, :].bitcast(F32),
                                  ALU.subtract).then_inc(w_split, 1)
                turned(FIRST, 0)
                dve.wait_ge(set_up, 2)
                dve.memset(v[:, :, :, HD:HD + 1], 1.0).then_inc(set_up, 1)
                dve.memset(st[:, :, NH:24, 3, 0:2], 1.0).then_inc(set_up, 1)
                dve.wait_ge(c_loaded, 16)
                rotate(FIRST, 0, 0)
                rotate(FIRST, 0, 1)
                key_parts(0, 0)
                key_parts(0, 1)
                dve.wait_ge(set_up, 4)
                query_parts(0)
                dve.wait_ge(kz_zeroed, 1)
                pack(FIRST, ("k0", "q0", "k1", "q1", "q2", "q3"))
                for n in range(LEAD):
                    first_maxima(FIRST, 0, (n,))

                def normalize(phase, b, g):
                    dve.wait_ge(m_filled, misc.filled(phase, f"ot{g}"))
                    o = ps_m[:, :].rearrange("p (t a c) -> p t a c", t=TB, c=32)
                    dve.reciprocal(rec[:, g % 2, :, :], o[:, :, :, HD]).then_inc(rec_ready, 1)
                    dve.wait_ge(rec_ready, 4 * b + g + 1)
                    for t in range(TB):
                        ins = dve.tensor_tensor(
                            ao[:, t, 64 * g:64 * g + 64].rearrange("p (a d) -> p a d", d=HD), o[:, t, :, 0:HD],
                            rec[:, g % 2, t, :].unsqueeze(2).to_broadcast([P, 4, HD]), ALU.mult)
                    ins.then_inc(m_emptied["dve"], 1)

                def step(phase, b, s, prepare):
                    g, kt = s // 4, s % 4
                    maxima(phase, b, step_units(s))
                    if kt == 2 and g < 3:
                        spare_rows(phase, b, g + 1)
                    if kt == 2 and g > 0:
                        normalize(phase, b, g - 1)
                    if prepare:
                        if s == NORM:
                            statistics(b + 1)
                        if s == SCALE:
                            scale_rows(b + 1)
                        if s == TURN:
                            turned(phase, b + 1)
                        if s in PROJECT:
                            rotate(phase, b + 1, PROJECT.index(s))
                        if s in KEYS:
                            key_parts(b + 1, KEYS.index(s))
                        if s == PARTS:
                            dve.wait_ge(m_filled, misc.filled(phase, "retr3b"))
                            query_parts(b + 1)
                        pack(phase, PACKED.get(s, ()))
                        first_maxima(phase, b + 1, EARLY.get(s, ()))

                def end(phase, b, name):
                    k = int(name[2])
                    if name in ("at0", "at1"):
                        dve.wait_ge(at_hi, KD * b + k + 1)
                        dve.tensor_tensor(at_l[:, k, :], ps_m[:, :], at_h[:, k, :].bitcast(F32),
                                          ALU.subtract).then_inc(m_emptied["dve"], 1)
                    else:
                        dve.wait_ge(m_filled, misc.filled(phase, name))
                        dve.tensor_tensor(X[:, bass.ds(TB * b + 2 * k, 2), :],
                                          ps_m[:, :].rearrange("p (t d) -> p t d", t=2),
                                          X[:, bass.ds(TB * b + 2 * k, 2), :], ALU.add).then_inc(m_emptied["dve"], 1)

                for s in range(HEAD):
                    step(FIRST, 0, s, False)
                dve.wait_ge(w_act, 2)
                dve.tensor_tensor(wo_l[:, :, :], wo_in[:, :, :], wo_h[:, :, :].bitcast(F32),
                                  ALU.subtract).then_inc(w_split, 1)

                def row(phase, b, last):
                    for s in range(HEAD, STEPS):
                        step(phase, b, s, not last)
                    if not last:
                        pack(phase, PACKED_LAST)
                        first_maxima(phase, b + 1, LATE[0])
                    normalize(phase, b, 3)
                    if not last:
                        first_maxima(phase, b + 1, LATE[1])
                    for s in range(HEAD):
                        if not last:
                            step(phase, b + 1, s, False)
                        for name in END[s]:
                            end(phase, b, name)

                rows(dve, row)

            @block.tensor
            def _(pe):

                def transposes(out, cols):
                    for t in range(TB):
                        ins = pe.transpose(out[:, P * t:P * (t + 1)], cols(t), ident[:, :])
                    return ins

                def begin(phase, name):
                    ring.wait_free(pe, emptied, phase, name)
                    return ps_ring[:, ring.slot(phase, name), :, :]

                def turn(phase, r):
                    pe.wait_ge(xn_ready, AHEAD + TB * (r + 1))
                    for k in range(KD):
                        o = begin(phase, f"xt{k}")
                        transposes(o[:, 0, :], lambda t: xn[:, t, P * k:P * (k + 1)]).then_inc(filled, 1)

                def project(phase, r, i):
                    o = begin(phase, f"qkv{i}")
                    if i == 0:
                        pe.wait_ge(xt_hi, KD * (r + 1))
                        pe.wait_ge(emptied["dve"], ring.emptied(phase, "xt1", "dve"))
                    for t in range(2):
                        at = P * (2 * i + t)
                        for k in range(KD):
                            ins = product(pe, o[:, t, :], (xt_h[:, k, at:at + P], xt_l[:, k, at:at + P]),
                                          (w_h[:, k, :], w_l[:, k, :]), k == 0, k == KD - 1)
                    ins.then_inc(filled, 1)

                def pack(phase, r, names):
                    for name in names:
                        o = begin(phase, name)
                        if name == "k0":
                            pe.wait_ge(k_low, AHEAD + TB * (r + 1))
                            pe.wait_ge(k_copied, TB * (r + 1))
                        if name == "q0":
                            pe.wait_ge(q_low, AHEAD + TB * (r + 1))
                            pe.wait_ge(q_copied, TB * (r + 1))
                            pe.wait_ge(spare_zeroed, r + 1)
                        for j in range(2):
                            h = (NH if name[0] == "k" else 0) + 4 * int(name[1]) + 2 * j
                            ins = transposes(o[:, j, :],
                                             lambda t: st[:, t, h:h + 2, :, :].rearrange("p h s d -> p (h s d)"))
                        ins.then_inc(filled, 1)

                def score_rows(phase, n):
                    if n == 0:
                        for o in ("act", "dve"):
                            pe.wait_ge(emptied[o], ring.emptied(phase, "q1", o))
                    i, qt = n // 2, 2 * (n % 2)
                    o = begin(phase, units[n])
                    for q in range(2):
                        at = P * (qt + q)
                        ins = pe.matmul(o[:, q, :], qp[:, i // 2, at:at + P], kz[:, 2 * (i // 4) + i % 2, :],
                                        start=True, stop=True)
                    ins.then_inc(filled, 1)

                def all_packed(phase):
                    for o in ("act", "dve"):
                        name = [n for n in ("k0", "q0", "q1", "q2", "k1", "q3") if OWNER.get(n, "dve") == o][-1]
                        pe.wait_ge(emptied[o], ring.emptied(phase, name, o))

                def requery(phase, r, g, j):
                    if j == 0:
                        pe.wait_ge(aux1, AHEAD + 4 * r + g + 1)
                    misc.wait_free(pe, m_emptied, phase, f"retr{g}{'ab'[j]}")
                    h = 4 * g + 2 * j
                    transposes(ps_m[:, :], lambda t: st[:, t, h:h + 2, :, :].rearrange(
                        "p h s d -> p (h s d)")).then_inc(m_filled, 1)

                pe.wait_ge(const_loaded, const_loads)
                turn(FIRST, 0)
                pe.wait_ge(w_split, 1)
                project(FIRST, 0, 0)
                project(FIRST, 0, 1)
                pe.wait_ge(set_up, 4)
                pack(FIRST, 0, ("k0", "q0", "k1", "q1", "q2", "q3"))
                for n in range(LEAD):
                    score_rows(FIRST, n)
                all_packed(FIRST)
                requery(FIRST, 0, 0, 0)
                requery(FIRST, 0, 0, 1)

                def scores(phase, b, s):
                    g, kt = s // 4, s % 4
                    ns = step_units(s)
                    for a in range(4):
                        if a in (1, 3) and a // 2 < len(ns):
                            score_rows(phase, ns[a // 2])
                        if a == 2 and s > 1:
                            values(b, s - 2)
                        if a > 1 and kt == 3 and g < 3:
                            requery(phase, b, g + 1, a - 2)
                        if kt == 0 and a == 0:
                            pe.wait_ge(m_emptied["act"], AHEAD + 8 * b + 2 * g + 2)
                        pe.wait_ge(exp_done, AHEAD + 64 * b + max(4 * s + a - 1, 0))
                        pe.matmul(ps_sc[:, a % 2, :], kz[:, 2 * g + a // 2, P * kt:P * (kt + 1)],
                                  qp[:, 2 * g + a % 2, :], start=True, stop=True).then_inc(sc_filled, 1)

                def values(b, s):
                    g, kt = s // 4, s % 4
                    if s == 0:
                        pe.wait_ge(v_moved, b + 1)
                    if kt == 0:
                        pe.wait_ge(ot_copied, AHEAD + 4 * b + g)
                    pe.wait_ge(exp_done, AHEAD + 64 * b + 4 * s + 4)
                    for a in range(4):
                        ins = pe.matmul(ps_pv[32 * a:32 * a + 32, :], v[:, kt, 2 * g + a // 2, :],
                                        pt[:, s % 3, a, :], start=(kt == 0), stop=(kt == 3))
                    ins.then_inc(pv_done, 1)

                def outputs(phase, b, g):
                    pe.wait_ge(ot_copied, AHEAD + 4 * b + g + 1)
                    misc.wait_free(pe, m_emptied, phase, f"ot{g}")
                    transposes(ps_m[:, :], lambda t: ot[:, g % 2, P * t:P * (t + 1)]).then_inc(m_filled, 1)

                def step(phase, b, s, prepare):
                    g, kt = s // 4, s % 4
                    scores(phase, b, s)
                    if kt == 2 and g > 0:
                        outputs(phase, b, g - 1)
                    if prepare:
                        if s == TURN:
                            turn(phase, b + 1)
                        if s in PROJECT:
                            project(phase, b + 1, PROJECT.index(s))
                        pack(phase, b + 1, PACKED.get(s, ()))
                        for n in EARLY.get(s, ()):
                            score_rows(phase, n)

                def end(phase, b, name):
                    k = int(name[2])
                    misc.wait_free(pe, m_emptied, phase, name)
                    if name in ("at0", "at1"):
                        if k == 0:
                            pe.wait_ge(m_emptied["dve"], AHEAD + 8 * b + 4)
                        transposes(ps_m[:, :], lambda t: ao[:, t, P * k:P * (k + 1)]).then_inc(m_filled, 1)
                    else:
                        pe.wait_ge(m_emptied["dve"], AHEAD + 8 * b + 6)
                        for t in range(2):
                            at = P * (2 * k + t)
                            for j in range(KD):
                                ins = product(pe, ps_m[:, D * t:D * (t + 1)],
                                              (at_h[:, j, at:at + P], at_l[:, j, at:at + P]),
                                              (wo_h[:, j, :], wo_l[:, j, :]), j == 0, j == KD - 1)
                        ins.then_inc(m_filled, 1)

                for s in range(HEAD):
                    step(FIRST, 0, s, False)
                pe.wait_ge(w_split, 2)

                def row(phase, b, last):
                    for s in range(HEAD, STEPS):
                        step(phase, b, s, not last)
                    values(b, STEPS - 2)
                    if not last:
                        pack(phase, b + 1, PACKED_LAST)
                    values(b, STEPS - 1)
                    if not last:
                        for n in LATE[0]:
                            score_rows(phase, n)
                    outputs(phase, b, 3)
                    if not last:
                        for n in LATE[1]:
                            score_rows(phase, n)
                        all_packed(phase)
                        requery(phase, b + 1, 0, 0)
                        requery(phase, b + 1, 0, 1)
                    for s in range(HEAD):
                        if not last:
                            step(phase, b + 1, s, False)
                        for name in END[s]:
                            end(phase, b, name)

                rows(pe, row)

        m.close()


def experts_stage(nc, stage, w13, w2a, w2b, wg, X, ident, consts, xd, oe, banks, zeroed, zeroings,
                  ahead=None, out=None, stored=None):
    upper, ones, rank, first_slot = consts
    NW = 2 * KD * H
    with ExitStack() as ctx:
        m = Memory(nc, ctx, stage, banks)
        sb, sem = m.sb, m.sem
        s13_in, s2_in = sb("s13_in", [P, KD, 2, H]), sb("s2_in", [P, 3, D])
        s13, s2 = m.pair("s13", [P, KD, 2, H]), m.pair("s2", [P, 3, D])
        e13_in, e2_in = sb("e13_in", [P, 2, KD, 2, H]), sb("e2_in", [P, 2, 3, D])
        e13, e2 = m.pair("e13", [P, 2, KD, 2, H]), m.pair("e2", [P, 2, 3, D])
        wg_in, wgs = sb("wg_in", [P, KD, E]), m.pair("wg", [P, KD, E])
        ln = RowStats(m, "ln", TB)
        nhalf, rstd = sb("nhalf", [P, TB]), sb("rstd", [P, TB])
        xb = sb("xb", [P, TB, D])
        xn = sb("xn", [P, TB, D])
        xs = sb("xs", [P, TB, D])
        xt_h, xt_l = m.pair("xt", [P, KD, S])
        sil, hid = sb("sil", [P, 3, C]), sb("hid", [P, 3, C])
        h_h, h_l = m.pair("h", [P, 3, C])
        lg, ex, eq, sc, oh = (sb(n, [P, TB, E]) for n in ("lg", "ex", "eq", "sc", "oh"))
        pos, val = sb("pos", [P, TB, E]), sb("val", [P, TB, E])
        mx, sm, em, ms, rsm, gate, px, slot, keep, off, sls, slg = (
            sb(n, [P, TB]) for n in ("mx", "sm", "em", "ms", "rsm", "gate", "px", "slot", "keep", "off", "sls", "slg"))
        lt = sb("lt", [E, S])
        base = sb("base", [P, E])
        to_slot = sb("to_slot", [P, TB], U32)
        from_slot = sb("from_slot", [P, TILES], U32)
        weight = sb("weight", [P, TILES])
        xe = sb("xe", [P, 2, U, D])
        xet_h, xet_l = m.pair("xet", [P, KD, C])
        eo = sb("eo", [P, 2, U, D])
        got = sb("got", [P, 4, D])

        ps_t = m.psum([P, 2, S])
        ps_up = m.psum([P, 3, 2, C])
        ps_down = m.psum([P, U, S])
        ps_r = m.psum([P, S])

        s_loaded, g_loaded = sem("s_loaded"), sem("g_loaded")
        e_loaded = [sem("e_loaded0"), sem("e_loaded1")]
        xe_loaded = [sem("xe_loaded0"), sem("xe_loaded1")]
        set_up, nhalf_set = sem("set_up"), sem("nhalf_set")
        s_high, s_low = sem("s_high"), sem("s_low")
        e_high, e_low = sem("e_high"), sem("e_low")
        xb_copied, rstd_ready, xn_ready, xs_copied = (
            sem("xb_copied"), sem("rstd_ready"), sem("xn_ready"), sem("xs_copied"))
        t_filled, xt_high, xt_low = sem("t_filled"), sem("xt_high"), sem("xt_low")
        up_done, sil_done, hid_done, h_high, h_low = (
            sem("up_done"), sem("sil_done"), sem("hid_done", ahead=True), sem("h_high"), sem("h_low"))
        down_done, added = sem("down_done"), sem("added", ahead=True)
        lt_done, lt_copied = sem("lt_done"), sem("lt_copied")
        logits_done, ex_done, counted = sem("logits_done"), sem("ex_done"), sem("counted")
        route = sem("route", ahead=True)
        scattered = sem("scattered", keep=True)
        eo_stored = [sem("eo_stored0", ahead=True), sem("eo_stored1", ahead=True)]
        gathered = [sem(f"gathered{i}", keep=True) for i in range(4)]
        combined, gate_ready = sem("combined"), sem("gate_ready")
        ROUTE = 23

        def load_weights(q, dst13, dst2, e, done):
            q.dma_start(dst13.rearrange("p k a h -> p (k a h)"), w13[e]).then_inc(done, 16)
            q.dma_start(dst2[:, 0:2, :].rearrange("p i d -> p (i d)"), w2a[e]).then_inc(done, 16)
            q.dma_start(dst2[0:HT[2], 2, :], w2b[e]).then_inc(done, 16)

        def high_parts(eng, hi13, hi2, in13, in2, done):
            copy = (lambda o, i: eng.activation(o, i, ACT.Copy))
            copy(hi13, in13)
            copy(hi2[:, 0:2, :], in2[:, 0:2, :])
            copy(hi2[0:HT[2], 2, :], in2[0:HT[2], 2, :]).then_inc(done, 1)

        def low_parts(eng, lo13, lo2, hi13, hi2, in13, in2, done):
            sub = (lambda o, i, h: eng.tensor_tensor(o, i, h.bitcast(F32), ALU.subtract))
            sub(lo13, in13, hi13)
            sub(lo2[:, 0:2, :], in2[:, 0:2, :], hi2[:, 0:2, :])
            sub(lo2[0:HT[2], 2, :], in2[0:HT[2], 2, :], hi2[0:HT[2], 2, :]).then_inc(done, 1)

        def up(pe, n, i, xt, w, off_t, halfway=lambda: None):
            rows = slice(P * i, P * i + HT[i])
            if i == 0:
                pe.wait_ge(hid_done, AHEAD + 3 * n)
            for a in range(2):
                if a == 1:
                    halfway()
                for k in range(KD):
                    ins = product(pe, ps_up[0:HT[i], i, a, :], (w[0][:, k, a, rows], w[1][:, k, a, rows]),
                                  (xt[0][:, k, off_t:off_t + C], xt[1][:, k, off_t:off_t + C]), k == 0, k == KD - 1)
            ins.then_inc(up_done, 1)

        def down(pe, n, i, w):
            if i == 0:
                pe.wait_ge(added, AHEAD + n)
            pe.wait_ge(h_low, 3 * n + i + 1)
            for t in range(U):
                ins = product(pe, ps_down[:, t, 0:D],
                              (h_h[0:HT[i], i, P * t:P * (t + 1)], h_l[0:HT[i], i, P * t:P * (t + 1)]),
                              (w[0][0:HT[i], i, :], w[1][0:HT[i], i, :]), i == 0, i == 2)
            if i == 2:
                ins.then_inc(down_done, 1)

        def silu(act, n, i):
            act.wait_ge(up_done, 3 * n + i + 1)
            act.activation(sil[0:HT[i], i, :], ps_up[0:HT[i], i, 0, :], ACT.Silu).then_inc(sil_done, 1)

        def hidden_high(act, n, i):
            act.wait_ge(hid_done, AHEAD + 3 * n + i + 1)
            act.activation(h_h[0:HT[i], i, :], hid[0:HT[i], i, :], ACT.Copy).then_inc(h_high, 1)

        def hidden(dve, n, i):
            dve.wait_ge(sil_done, 3 * n + i + 1)
            dve.tensor_tensor(hid[0:HT[i], i, :], sil[0:HT[i], i, :], ps_up[0:HT[i], i, 1, :],
                              ALU.mult).then_inc(hid_done, 1)

        def hidden_low(eng, n, i):
            eng.wait_ge(h_high, 3 * n + i + 1)
            eng.tensor_tensor(h_l[0:HT[i], i, :], hid[0:HT[i], i, :], h_h[0:HT[i], i, :].bitcast(F32),
                              ALU.subtract).then_inc(h_low, 1)

        def rows(eng, body):
            body(0, False)
            with eng.Fori(1, B - 1) as b:
                body(b, False)
            body(B - 1, True)

        def experts(eng, body):
            with eng.Fori(0, E // 2 - 1) as v:
                body(2 * v, 0, False)
                body(2 * v + 1, 1, False)
            body(E - 2, 0, False)
            body(E - 1, 1, True)

        N0 = UNITS

        m.open()
        with nc.Block() as block:

            @block.sync
            def _(sp):
                load_weights(sp, s13_in[:, :, :, :], s2_in, E, s_loaded)
                sp.dma_start(wg_in[:, :, :], wg.rearrange("(k p) e -> p k e", p=P)).then_inc(g_loaded, 16)
                load_weights(sp, e13_in[:, 0], e2_in[:, 0], 0, e_loaded[0])
                load_weights(sp, e13_in[:, 1], e2_in[:, 1], 1, e_loaded[1])

                if ahead is not None:
                    ahead.load(sp)

                def load_rows(e, w):
                    sp.dma_start(xe[:, w, :, :], xd[bass.ds(C * e, C), :].rearrange("(t p) d -> p t d", p=P)
                                 ).then_inc(xe_loaded[w], 16)

                sp.wait_ge(scattered, 64 * B)
                load_rows(0, 0)
                load_rows(1, 1)

                def body(e, w, last):
                    sp.wait_ge(added, AHEAD + N0 + e + 1)
                    sp.dma_start(oe[bass.ds(C * e, C), :].rearrange("(t p) d -> p t d", p=P),
                                 eo[:, w, :, :]).then_inc(eo_stored[w], 16)

                def loads(e, w):
                    sp.wait_ge(t_filled, 2 * B + e + 1)
                    load_rows(e + 2, w)
                    sp.wait_ge(e_low, e + 1)
                    load_weights(sp, e13_in[:, w], e2_in[:, w], e + 2, e_loaded[w])

                with sp.Fori(0, E // 2 - 1) as v:
                    for w in range(2):
                        loads(2 * v + w, w)
                        body(2 * v + w, w, False)
                body(E - 2, 0, False)
                body(E - 1, 1, True)
                for w in range(2):
                    sp.wait_ge(eo_stored[w], AHEAD + 16 * E // 2)
                if out is not None:
                    for b in range(B):
                        sp.wait_ge(combined, TB * (b + 1))
                        sp.dma_start(out[b].rearrange("(t p) d -> p t d", p=P),
                                     X[:, TB * b:TB * (b + 1), :]).then_inc(stored, 16)
                    sp.wait_ge(stored, 16 * B)

            @block.gpsimd
            def _(pool):
                pool.memset(nhalf[:, :], -0.5).then_inc(nhalf_set, 1)
                pool.wait_ge(nhalf_set, 1)

                def power(b):
                    pool.wait_ge(ln.done, ln.steps * (b + 1))
                    pool.tensor_tensor(rstd[:, :], ln.ve[:, :], nhalf[:, :], ALU.pow).then_inc(rstd_ready, 1)

                power(0)
                pool.wait_ge(zeroed, 16 * zeroings)
                pool.wait_ge(e_high, 1)
                low_parts(pool, e13[1][:, 0], e2[1][:, 0], e13[0][:, 0], e2[0][:, 0], e13_in[:, 0], e2_in[:, 0], e_low)

                def row(b, last):
                    for i in range(3):
                        hidden_low(pool, 2 * b, i)
                    if not last:
                        pool.wait_ge(xn_ready, TB * (b + 1))
                        power(b + 1)
                    if not last:
                        for i in range(3):
                            hidden_low(pool, 2 * b + 1, i)
                    pool.wait_ge(xs_copied, b + 1)
                    pool.wait_ge(route, AHEAD + ROUTE * b + 21)
                    pool.tensor_tensor(gate[:, :], em[:, :], rsm[:, :], ALU.mult).then_inc(gate_ready, 1)
                    for t in range(TB):
                        pool.indirect_dma_start(
                            xd, bass.IndirectOffsetOnAxis(ap=to_slot[:, t:t + 1], axis=0), xs[:, t, :], None,
                            bounds_check=E * C - 1, oob_is_err=False).then_inc(scattered, 16)

                rows(pool, row)

                def expert(e, w, last):
                    if not last:
                        pool.wait_ge(e_high, e + 2)
                        pool.wait_ge(down_done, N0 + e)
                        low_parts(pool, e13[1][:, 1 - w], e2[1][:, 1 - w], e13[0][:, 1 - w], e2[0][:, 1 - w],
                                  e13_in[:, 1 - w], e2_in[:, 1 - w], e_low)

                experts(pool, expert)
                for w in range(2):
                    pool.wait_ge(eo_stored[w], AHEAD + 16 * E // 2)
                for t in range(TILES):
                    if t >= 4:
                        pool.wait_ge(combined, t - 3)
                    pool.indirect_dma_start(
                        got[:, t % 4, :], None, oe, bass.IndirectOffsetOnAxis(ap=from_slot[:, t:t + 1], axis=0),
                        bounds_check=E * C - 1, oob_is_err=False).then_inc(gathered[t % 4], 16)

            @block.scalar
            def _(act):
                act.wait_ge(s_loaded, 48)
                high_parts(act, s13[0][:, :, :, :], s2[0], s13_in[:, :, :, :], s2_in, s_high)
                act.wait_ge(g_loaded, 16)
                act.activation(wgs[0][:, :, :], wg_in[:, :, :], ACT.Copy).then_inc(s_high, 1)

                def transposed(b):
                    for k in range(KD):
                        act.wait_ge(t_filled, 2 * b + k + 1)
                        act.activation(xt_h[:, k, :], ps_t[:, k, :], ACT.Copy).then_inc(xt_high, 1)

                def stage_rows(b):
                    if not isinstance(b, int) or b > 0:
                        act.wait_ge(scattered, 64 * b)
                    act.activation(xs[:, :, :], xn[:, :, :], ACT.Copy).then_inc(xs_copied, 1)

                transposed(0)
                act.wait_ge(e_loaded[0], 48)
                high_parts(act, e13[0][:, 0], e2[0][:, 0], e13_in[:, 0], e2_in[:, 0], e_high)

                def row(b, last):
                    n = 2 * b
                    silu(act, n, 0)
                    act.wait_ge(lt_done, b + 1)
                    act.activation(lt[:, :], ps_r[0:E, :], ACT.Copy).then_inc(lt_copied, 1)
                    silu(act, n, 1)
                    hidden_high(act, n, 0)
                    silu(act, n, 2)
                    hidden_high(act, n, 1)
                    hidden_high(act, n, 2)
                    act.wait_ge(route, AHEAD + ROUTE * b + 2)
                    act.activation(ex[:, :, :], lg[:, :, :], ACT.Exp).then_inc(ex_done, 1)
                    stage_rows(b)
                    n = 2 * b + 1
                    silu(act, n, 0)
                    silu(act, n, 1)
                    hidden_high(act, n, 0)
                    silu(act, n, 2)
                    hidden_high(act, n, 1)
                    hidden_high(act, n, 2)
                    if not last:
                        transposed(b + 1)

                rows(act, row)

                def expert_rows(e):
                    act.wait_ge(t_filled, 2 * B + e + 1)
                    act.activation(xet_h[:, :, :].rearrange("p k c -> p (k c)"), ps_t[:, 0, :],
                                   ACT.Copy).then_inc(xt_high, 1)

                expert_rows(0)

                def expert(e, w, last):
                    n = N0 + e
                    if not last:
                        act.wait_ge(e_loaded[1 - w], 24 * (e - w) + 48 * (1 + w))
                        act.wait_ge(down_done, N0 + e)
                        high_parts(act, e13[0][:, 1 - w], e2[0][:, 1 - w], e13_in[:, 1 - w], e2_in[:, 1 - w], e_high)
                    silu(act, n, 0)
                    silu(act, n, 1)
                    hidden_high(act, n, 0)
                    silu(act, n, 2)
                    hidden_high(act, n, 1)
                    hidden_high(act, n, 2)
                    if not last:
                        expert_rows(e + 1)

                experts(act, expert)
                if ahead is not None:
                    ahead.act(act)

            @block.vector
            def _(dve):
                dve.memset(base[:, :], 0.0).then_inc(set_up, 1)
                dve.wait_ge(set_up, 1)

                def statistics(b):
                    dve.tensor_copy(xb[:, :, :], X[:, bass.ds(TB * b, TB), :]).then_inc(xb_copied, 1)
                    dve.wait_ge(xb_copied, b + 1)
                    ln.run(dve, b, lambda t: xb[:, t, :])

                def normalize(b):
                    dve.wait_ge(rstd_ready, b + 1)
                    dve.wait_ge(xs_copied, b)
                    for t in range(TB):
                        dve.tensor_scalar(xn[:, t, :], xb[:, t, :], ln.mean[:, t:t + 1], rstd[:, t:t + 1],
                                          ALU.subtract, ALU.mult).then_inc(xn_ready, 1)

                def transposed(b):
                    for k in range(KD):
                        dve.wait_ge(xt_high, KD * b + k + 1)
                        dve.tensor_tensor(xt_l[:, k, :], ps_t[:, k, :], xt_h[:, k, :].bitcast(F32),
                                          ALU.subtract).then_inc(xt_low, 1)

                statistics(0)
                normalize(0)
                dve.wait_ge(s_high, 1)
                low_parts(dve, s13[1][:, :, :, :], s2[1], s13[0][:, :, :, :], s2[0], s13_in[:, :, :, :], s2_in, s_low)
                dve.wait_ge(s_high, 2)
                dve.tensor_tensor(wgs[1][:, :, :], wg_in[:, :, :], wgs[0][:, :, :].bitcast(F32),
                                  ALU.subtract).then_inc(s_low, 1)
                transposed(0)

                def wide(a):
                    return a[:, :].unsqueeze(2).to_broadcast([P, TB, E])

                def row(b, last):
                    at = ROUTE * b
                    steps = [0]

                    def step(ins):
                        ins.then_inc(route, 1)
                        steps[0] += 1
                        dve.wait_ge(route, AHEAD + at + steps[0])

                    def add_down(n, half):
                        dve.wait_ge(down_done, n + 1)
                        dve.tensor_tensor(X[:, bass.ds(TB * b + U * half, U), :],
                                          ps_down[:, :, 0:D], X[:, bass.ds(TB * b + U * half, U), :],
                                          ALU.add).then_inc(added, 1)

                    bank = ps_r[:, 0:3 * TB * E].rearrange("p (a t e) -> p a t e", a=3, e=E)
                    hidden(dve, 2 * b, 0)
                    hidden(dve, 2 * b, 1)
                    dve.wait_ge(logits_done, b + 1)
                    step(dve.tensor_reduce(mx[:, :], bank[:, 0], AX_X, ALU.max))
                    step(dve.tensor_tensor(lg[:, :, :], bank[:, 0], wide(mx), ALU.subtract))
                    hidden(dve, 2 * b, 2)
                    if not last:
                        statistics(b + 1)
                    dve.wait_ge(ex_done, b + 1)
                    step(dve.tensor_reduce(em[:, :], ex[:, :, :], AX_X, ALU.max))
                    step(dve.tensor_tensor(eq[:, :, :], ex[:, :, :], wide(em), ALU.is_ge))
                    step(dve.tensor_tensor(sc[:, :, :], eq[:, :, :], rank, ALU.mult))
                    step(dve.tensor_reduce(ms[:, :], sc[:, :, :], AX_X, ALU.max))
                    step(dve.tensor_tensor(oh[:, :, :], sc[:, :, :], wide(ms), ALU.is_equal))
                    step(dve.tensor_reduce(sm[:, :], ex[:, :, :], AX_X, ALU.add))
                    step(dve.reciprocal(rsm[:, :], sm[:, :]))

                    def positions():
                        dve.wait_ge(xs_copied, b + 1)
                        dve.wait_ge(counted, b + 1)
                        for t in range(TB):
                            dve.tensor_tensor(pos[:, t, :], bank[:, 1, t, :], base[:, :], ALU.add)
                            step(dve.tensor_tensor(base[:, :], bank[:, 2, t, :], base[:, :], ALU.add))
                        step(dve.tensor_tensor(val[:, :, :], pos[:, :, :], first_slot, ALU.add))
                        step(dve.tensor_tensor(pos[:, :, :], pos[:, :, :], oh[:, :, :], ALU.mult))
                        step(dve.tensor_tensor(val[:, :, :], val[:, :, :], oh[:, :, :], ALU.mult))
                        dve.tensor_reduce(px[:, :], pos[:, :, :], AX_X, ALU.add)
                        step(dve.tensor_reduce(slot[:, :], val[:, :, :], AX_X, ALU.add))
                        step(dve.tensor_scalar(keep[:, :], px[:, :], float(C), None, ALU.is_le))
                        step(dve.tensor_scalar(off[:, :], keep[:, :], -2.0 * E * C, 2.0 * E * C, ALU.mult, ALU.add))
                        step(dve.tensor_tensor(sls[:, :], slot[:, :], off[:, :], ALU.add))
                        step(dve.tensor_copy(to_slot[:, :], sls[:, :]))
                        step(dve.tensor_scalar(from_slot[:, bass.ds(TB * b, TB)], sls[:, :], float(E * C - 1), None,
                                               ALU.min))

                    if last:
                        positions()
                        add_down(2 * b, 0)
                        for i in range(3):
                            hidden(dve, 2 * b + 1, i)
                            if i > 0:
                                hidden_low(dve, 2 * b + 1, i - 1)
                        hidden_low(dve, 2 * b + 1, 2)
                    else:
                        add_down(2 * b, 0)
                        hidden(dve, 2 * b + 1, 0)
                        normalize(b + 1)
                        hidden(dve, 2 * b + 1, 1)
                        hidden(dve, 2 * b + 1, 2)
                        transposed(b + 1)
                        positions()
                    add_down(2 * b + 1, 1)
                    dve.wait_ge(gate_ready, b + 1)
                    step(dve.tensor_tensor(weight[:, bass.ds(TB * b, TB)], gate[:, :], keep[:, :], ALU.mult))
                    assert steps[0] == ROUTE

                rows(dve, row)

                def expert_rows(e):
                    dve.wait_ge(xt_high, KD * B + e + 1)
                    dve.tensor_tensor(xet_l[:, :, :].rearrange("p k c -> p (k c)"), ps_t[:, 0, :],
                                      xet_h[:, :, :].bitcast(F32).rearrange("p k c -> p (k c)"),
                                      ALU.subtract).then_inc(xt_low, 1)

                expert_rows(0)

                def expert(e, w, last):
                    n = N0 + e
                    hidden(dve, n, 0)
                    hidden(dve, n, 1)
                    hidden_low(dve, n, 0)
                    hidden(dve, n, 2)
                    hidden_low(dve, n, 1)
                    hidden_low(dve, n, 2)
                    if not last:
                        expert_rows(e + 1)
                    dve.wait_ge(down_done, n + 1)
                    dve.wait_ge(eo_stored[w], AHEAD + 8 * (e - w))
                    dve.tensor_copy(eo[:, w, :, :], ps_down[:, :, 0:D]).then_inc(added, 1)

                experts(dve, expert)
                for t in range(TILES):
                    if ahead is not None and t % 4 == 0:
                        ahead.dve(dve, t // 4)
                    dve.wait_ge(gathered[t % 4], 16 * (t // 4 + 1))
                    dve.scalar_tensor_tensor(X[:, t, :], got[:, t % 4, :], weight[:, t:t + 1], X[:, t, :],
                                             ALU.mult, ALU.add).then_inc(combined, 1)

            @block.tensor
            def _(pe):
                shared_w13, shared_w2 = s13, s2
                xt = (xt_h, xt_l)

                def transposes(b):
                    pe.wait_ge(xn_ready, TB * (b + 1))
                    for k in range(KD):
                        for t in range(TB):
                            ins = pe.transpose(ps_t[:, k, P * t:P * (t + 1)], xn[:, t, P * k:P * (k + 1)], ident[:, :])
                        ins.then_inc(t_filled, 1)

                transposes(0)
                pe.wait_ge(s_low, 2)

                def row(b, last):
                    n = 2 * b
                    pe.wait_ge(xt_low, KD * (b + 1))
                    up(pe, n, 0, xt, shared_w13, 0)
                    pe.wait_ge(route, AHEAD + ROUTE * b)
                    for k in range(KD):
                        ins = product(pe, ps_r[0:E, :], (wgs[0][:, k, :], wgs[1][:, k, :]),
                                      (xt_h[:, k, :], xt_l[:, k, :]), k == 0, k == KD - 1)
                    ins.then_inc(lt_done, 1)
                    up(pe, n, 1, xt, shared_w13, 0, lambda: pe.wait_ge(lt_copied, b + 1))
                    for t in range(TB):
                        ins = pe.transpose(ps_r[:, E * t:E * (t + 1)], lt[:, P * t:P * (t + 1)], ident[0:E, 0:E])
                    ins.then_inc(logits_done, 1)
                    up(pe, n, 2, xt, shared_w13, 0)
                    for i in range(3):
                        down(pe, n, i, shared_w2)
                    n = 2 * b + 1

                    def count():
                        pe.wait_ge(route, AHEAD + ROUTE * b + 7)
                        one_hot = oh[:, :, :].rearrange("p t e -> p (t e)")
                        pe.matmul(ps_r[:, TB * E:2 * TB * E], upper, one_hot, start=True, stop=True)
                        pe.matmul(ps_r[:, 2 * TB * E:3 * TB * E], ones, one_hot, start=True, stop=True
                                  ).then_inc(counted, 1)

                    if last:
                        count()
                    for i in range(3):
                        up(pe, n, i, xt, shared_w13, C)
                    if not last:
                        transposes(b + 1)
                        count()
                    for i in range(3):
                        down(pe, n, i, shared_w2)

                rows(pe, row)

                def expert_rows(e, w):
                    pe.wait_ge(xe_loaded[w], 8 * (e - w) + 16)
                    for k in range(KD):
                        for t in range(U):
                            at = C * k + P * t
                            ins = pe.transpose(ps_t[:, 0, at:at + P], xe[:, w, t, P * k:P * (k + 1)], ident[:, :])
                    ins.then_inc(t_filled, 1)

                expert_rows(0, 0)

                def expert(e, w, last):
                    n = N0 + e
                    w13p = (e13[0][:, w], e13[1][:, w])
                    w2p = (e2[0][:, w], e2[1][:, w])
                    pe.wait_ge(e_low, e + 1)
                    pe.wait_ge(xt_low, KD * B + e + 1)
                    for i in range(3):
                        up(pe, n, i, (xet_h, xet_l), w13p, 0)
                    if not last:
                        expert_rows(e + 1, 1 - w)
                    for i in range(3):
                        down(pe, n, i, w2p)

                experts(pe, expert)
        m.close()


class Projections:

    def __init__(self, nc, ctx, a):
        m = Memory(nc, ctx, "proj")
        self.norms = m.sb("norms", [P, 3, KD])
        self.conv_w, self.conv_b = m.sb("conv_w", [P, 4, 4]), m.sb("conv_b", [P, 4])
        self.heads, self.neg_a = m.sb("heads", [P, 3, 2]), m.sb("neg_a", [P, 2])
        self.cap = m.sb("cap", [P, P])
        raw = {n: m.sb(f"raw_{n}", [P, KD, w])[:, :, :] for n, w in (("win", PROJ), ("wout", D))}
        self.raw_ffn = m.sb("raw_ffn", [P, 3, KD * INTER])
        for i, n in enumerate(("w1", "w3", "w2")):
            raw[n] = self.raw_ffn[:, i, :].rearrange("p (k n) -> p k n", k=IT if n == "w2" else KD)
        self.raw = raw
        self.split = {"win": m.pair("win", [P, KD, PROJ]), "wout": m.pair("wout", [P, KD, D])}
        self.loaded, self.scaled, self.high = m.sem("loaded"), m.sem("scaled"), m.sem("high")
        self.low, self.decay = m.sem("low"), m.sem("decay")
        self.pairs = [(raw[n], a[n].rearrange("(k p) n -> p k n", p=P)) for n in raw]
        self.pairs += [(self.norms[:, :, :], a["norms"]), (self.conv_w[:, :, :], a["conv_w"]),
                       (self.conv_b[:, :], a["conv_b"]), (self.cap[:, :], a["cap"]),
                       (self.heads[:, :, :].rearrange("p a h -> p (a h)"),
                        a["heads"].rearrange("(o n) -> o n", o=1).to_broadcast([P, 6]))]

    def load(self, sp):
        for dst, src in self.pairs:
            sp.dma_start(dst, src).then_inc(self.loaded, 16)

    def wait_loaded(self, eng):
        eng.wait_ge(self.loaded, 16 * len(self.pairs))

    def act(self, act):
        self.wait_loaded(act)
        act.activation(self.neg_a[:, :], self.heads[:, 1, :], ACT.Exp).then_inc(self.decay, 1)
        for i, n in enumerate(("win", "wout")):
            act.wait_ge(self.scaled, i + 1)
            act.activation(self.split[n][0][:, :, :], self.raw[n], ACT.Copy).then_inc(self.high, 1)

    def scale(self, dve, n, norm):
        for j in range(KD):
            ins = dve.tensor_scalar(self.raw[n][:, j, :], self.raw[n][:, j, :], self.norms[:, norm, j:j + 1], None,
                                    ALU.mult)
        ins.then_inc(self.scaled, 1)

    def subtract(self, dve, n, i):
        dve.wait_ge(self.high, i + 1)
        dve.tensor_tensor(self.split[n][1][:, :, :], self.raw[n], self.split[n][0][:, :, :].bitcast(F32),
                          ALU.subtract).then_inc(self.low, 1)

    def dve(self, dve, part):
        if part == 0:
            self.wait_loaded(dve)
            self.scale(dve, "win", 0)
            self.scale(dve, "wout", 1)
        if part == 1:
            self.subtract(dve, "win", 0)
        if part == 2:
            self.subtract(dve, "wout", 1)
            self.scale(dve, "w1", 2)
        if part == 3:
            self.scale(dve, "w3", 2)
            dve.wait_ge(self.decay, 1)
            dve.tensor_scalar(self.neg_a[:, :], self.neg_a[:, :], -1.0, None, ALU.mult).then_inc(self.decay, 1)


def state_space_stage(nc, X, ident, consts, banks, proj):
    upper, ones = consts[0], consts[1]
    NF = 4
    with ExitStack() as ctx:
        m = Memory(nc, ctx, "ssm", banks)
        sb, sem = m.sb, m.sem
        raw, raw_ffn = proj.raw, proj.raw_ffn
        norms, conv_w, conv_b, heads, neg_a, cap = (
            proj.norms, proj.conv_w, proj.conv_b, proj.heads, proj.neg_a, proj.cap)
        win, wout = proj.split["win"], proj.split["wout"]
        w1, w3, w2 = m.pair("w1", [P, KD, INTER]), m.pair("w3", [P, KD, INTER]), m.pair("w2", [P, IT, D])
        raw_flat = raw_ffn[:, :, :].rearrange("p i n -> p (i n)")
        taken = [0]

        def reuse(*shape):
            n = int(np.prod(shape))
            v = raw_flat[:, taken[0]:taken[0] + n]
            taken[0] += n
            if len(shape) == 1:
                return v
            if len(shape) == 2:
                return v.rearrange("p (a b) -> p a b", a=shape[0])
            return v.rearrange("p (a b c) -> p a b c", a=shape[0], b=shape[1])

        res = reuse(TB, D)
        yg, sq = reuse(TB, D), reuse(D)
        sil, hid = reuse(3, C), reuse(3, C)
        xtm, btm = reuse(TB, P), reuse(TB, P)
        state, mm = reuse(2, 2, P), reuse(2, P)
        y1, y2 = reuse(2, P), reuse(2, P)
        w_of = {"win": win, "wout": wout, "w1": w1, "w3": w3, "w2": w2}
        nhalf = sb("nhalf", [P, TB])
        xb, xh, hn = sb("xb", [P, TB, D]), sb("xh", [P, TB, D]), sb("hn", [P, TB, D])
        ln = RowStats(m, "ln", TB)
        rstd, rstd2, var, v2, r1, rr = (sb(n, [P, TB]) for n in ("rstd", "rstd2", "var", "v2", "r1", "rr"))
        ht_h, ht_l = m.pair("ht", [P, KD, S])
        ft_h, ft_l = m.pair("ft", [P, KD, S])
        cv = sb("cv", [P, NF, S + 4])
        ca = sb("ca", [P, 2, S])
        xc = sb("xc", [P, NF, S])
        sz = sb("sz", [P, TB, D])
        small = [sb(f"dt{i}", [P, TB, 2]) for i in range(16)]
        (xdt, adt, udt, wdt, ddt, zdt, dden, rden, qdt, lnw, tdt, t2, mdt, sdt, dt, dA) = small
        ecs, etot, csum, dif, dec0, dec = (sb(n, [P, TB, 2]) for n in ("ecs", "etot", "csum", "dif", "dec0", "dec"))
        dd, ee = sb("dd", [P, TB, 2, P]), sb("ee", [P, TB, 2, P])
        xd, t0 = sb("xd", [P, 2, P]), sb("t0", [P, 2, P])
        ss, ms, rq = sb("ss", [P, TB]), sb("ms", [P, TB]), sb("rq", [P, TB])
        HR = 12
        h_h, h_l = m.pair("h", [P, HR, C])

        ps = m.psum([P, 8, S])
        UP, DOWN, bank_t, bank_f, bank_small = (0, 1), 2, (3, 4), (5, 6), 7

        w_high, ffn_low, set_up, nhalf_set = sem("w_high"), sem("ffn_low"), sem("set_up"), sem("nhalf_set")
        xb_copied, rstd_ready, r1_ready = sem("xb_copied"), sem("rstd_ready"), sem("r1_ready")
        pre, hn_ready = sem("pre"), sem("hn_ready")
        t_filled, t_high, t_low = sem("t_filled"), sem("t_high"), sem("t_low")
        feat, feat_out, z_filled, z_out = sem("feat"), sem("feat_out"), sem("z_filled"), sem("z_out")
        conv, conv_out, softplus = sem("conv"), sem("conv_out", ahead=True), sem("softplus")
        dts, dt_act, sums, dt_filled = sem("dts"), sem("dt_act"), sem("sums"), sem("dt_filled")
        tm_filled, tm_out = sem("tm_filled"), sem("tm_out")
        g_done, row_done, dd_done, ee_done, mm_done, xd_done = (
            sem("g_done"), sem("row_done"), sem("dd_done"), sem("ee_done"), sem("mm_done"), sem("xd_done"))
        y_done, s_done, st_done, ys, yg_done, sq_done = (
            sem("y_done", ahead=True), sem("s_done"), sem("st_done"), sem("ys"), sem("yg_done"), sem("sq_done", ahead=True))
        norm_v, rq_ready = sem("norm_v"), sem("rq_ready")
        o_done, h2_done, r2_done = sem("o_done"), sem("h2_done"), sem("r2_done", ahead=True)
        up_done, sil_done, hid_done, h_high, h_low = (
            sem("up_done"), sem("sil_done"), sem("hid_done", ahead=True), sem("h_high"), sem("h_low"))
        down_done, added = sem("down_done", ahead=True), sem("added", ahead=True)

        def square(act, b, c):
            act.wait_ge(yg_done, TB * b + c + 1)
            act.wait_ge(sq_done, AHEAD + 2 * TB * b + c)
            act.activation(sq[:, :], yg[:, c, :], ACT.Square, accum_out=ss[:, c:c + 1]).then_inc(sq_done, 1)

        def t_banks(k):
            return ps[:, bank_t[k], :]

        TILES_UP = 2 * IT
        FFN_STEPS = TILES_UP + 4
        DOWN_AT = {IT + 3: 0, TILES_UP + 2: 1}
        ADD_AT = {IT + 5: 0, TILES_UP + 3: 1}
        FILL = {"start": (0, 1), "scaled": (2, 3), "turned": (4, 5), "dt": (), "z": (), "tm": (6, 7),
                0: (8, 9), 1: (10,), 2: (), 3: (11, 12, 13), "norm": (14, 15), "out": (16, 17), "norm2": (18, 19)}

        def ffn_act(act, r, p):
            n = TILES_UP * r
            t = p - 1
            if 0 <= t < TILES_UP:
                act.wait_ge(up_done, n + t + 1)
                act.activation(sil[:, t % 3, :], ps[:, UP[t % 2], 0:C], ACT.Silu).then_inc(sil_done, 1)
            t = p - 2
            if 0 <= t < TILES_UP:
                act.wait_ge(hid_done, AHEAD + n + t + 1)
                act.wait_ge(down_done, AHEAD + 2 * r + (1 if t >= HR else 0))
                act.activation(h_h[:, t % HR, :], hid[:, t % 3, :], ACT.Copy).then_inc(h_high, 1)

        def ffn_dve(dve, r, p):
            n = TILES_UP * r
            t = p - 1
            if 0 <= t < TILES_UP:
                dve.wait_ge(sil_done, n + t + 1)
                if t >= 3:
                    dve.wait_ge(h_low, n + t - 2)
                dve.tensor_tensor(hid[:, t % 3, :], sil[:, t % 3, :], ps[:, UP[t % 2], C:2 * C],
                                  ALU.mult).then_inc(hid_done, 1)
            t = p - 2
            if 0 <= t < TILES_UP:
                dve.wait_ge(h_high, n + t + 1)
                dve.tensor_tensor(h_l[:, t % HR, :], hid[:, t % 3, :], h_h[:, t % HR, :].bitcast(F32),
                                  ALU.subtract).then_inc(h_low, 1)
            if p in ADD_AT:
                u = ADD_AT[p]
                dve.wait_ge(r2_done, AHEAD + r + 1)
                dve.wait_ge(down_done, AHEAD + 2 * r + u + 1)
                dve.tensor_tensor(X[:, bass.ds(TB * r + U * u, U), :],
                                  ps[:, DOWN, :].rearrange("p (t d) -> p t d", t=U),
                                  res[:, U * u:U * u + U, :], ALU.add).then_inc(added, 1)

        def ffn_pe(pe, r, p):
            n = TILES_UP * r
            if p < TILES_UP:
                u, i = p // IT, p % IT
                if p == 0:
                    pe.wait_ge(ffn_low, 3)
                    pe.wait_ge(t_low, 6 * (r + 1))
                pe.wait_ge(hid_done, AHEAD + n + max(p - 1, 0))
                for j, w in enumerate((w1, w3)):
                    for k in range(KD):
                        ins = product(pe, ps[:, UP[p % 2], C * j:C * (j + 1)],
                                      (w[0][:, k, P * i:P * (i + 1)], w[1][:, k, P * i:P * (i + 1)]),
                                      (ft_h[:, k, C * u:C * (u + 1)], ft_l[:, k, C * u:C * (u + 1)]),
                                      k == 0, k == KD - 1)
                ins.then_inc(up_done, 1)
            if p in DOWN_AT:
                u = DOWN_AT[p]
                pe.wait_ge(added, AHEAD + 2 * r + u)
                pe.wait_ge(h_low, n + IT * (u + 1))
                for t in range(U):
                    for i in range(IT):
                        slot, at = (IT * u + i) % HR, P * t
                        ins = product(pe, ps[:, DOWN, D * t:D * (t + 1)],
                                      (h_h[:, slot, at:at + P], h_l[:, slot, at:at + P]),
                                      (w2[0][:, i, :], w2[1][:, i, :]), i == 0, i == IT - 1)
                ins.then_inc(down_done, 1)

        def rows(eng, body, step):
            body(0, lambda place: None)

            def filler(b):
                def fill(place):
                    for p in FILL[place]:
                        step(eng, b - 1, p)
                return fill

            with eng.Fori(1, B) as b:
                body(b, filler(b))
            for p in range(FFN_STEPS):
                step(eng, B - 1, p)

        m.open()
        with nc.Block() as block:

            @block.gpsimd
            def _(pool):
                pool.memset(nhalf[:, :], -0.5).then_inc(nhalf_set, 1)
                pool.wait_ge(nhalf_set, 1)

                def row(b, first):
                    pool.wait_ge(ln.done, ln.steps * (b + 1))
                    pool.tensor_tensor(rstd[:, :], ln.ve[:, :], nhalf[:, :], ALU.pow).then_inc(rstd_ready, 1)
                    pool.wait_ge(pre, 6 * b + 4)
                    pool.tensor_tensor(r1[:, :], v2[:, :], nhalf[:, :], ALU.pow).then_inc(r1_ready, 1)
                    if first:
                        for i, n in enumerate(("w1", "w3", "w2")):
                            pool.wait_ge(w_high, i + 1)
                            pool.tensor_tensor(w_of[n][1][:, :, :], raw[n], w_of[n][0][:, :, :].bitcast(F32),
                                               ALU.subtract).then_inc(ffn_low, 1)
                    for i in range(2):
                        pool.wait_ge(norm_v, 2 * b + i + 1)
                        pool.tensor_tensor(rq[:, :], ms[:, :], nhalf[:, :], ALU.pow).then_inc(rq_ready, 1)
                    pool.wait_ge(h2_done, 2 * (b + 1))
                    pool.wait_ge(added, AHEAD + 2 * b)
                    pool.tensor_tensor(res[:, :, :], xb[:, :, :], xh[:, :, :], ALU.add).then_inc(r2_done, 1)

                row(0, True)
                with pool.Fori(1, B) as b:
                    row(b, False)

            @block.scalar
            def _(act):
                for i, n in enumerate(("w1", "w3", "w2")):
                    if n != "w2":
                        act.wait_ge(proj.scaled, i + 3)
                    act.activation(w_of[n][0][:, :, :], raw[n], ACT.Copy).then_inc(w_high, 1)
                act.wait_ge(set_up, 1)

                def row(b, fill):

                    def high(n, dst):
                        for k in range(KD):
                            act.wait_ge(t_filled, 6 * b + 2 * n + k + 1)
                            act.activation(dst[:, k, :], t_banks(k), ACT.Copy).then_inc(t_high, 1)

                    def features(f):
                        act.wait_ge(feat, NF * b + f + 1)
                        act.activation(cv[:, f, 3:3 + S], ps[:, bank_f[f % 2], :], ACT.Copy).then_inc(feat_out, 1)

                    fill("start")
                    fill("scaled")
                    high(0, ht_h)
                    fill("turned")
                    fill("dt")
                    act.wait_ge(dts, 11 * b + 2)
                    act.activation(udt[:, :, :], adt[:, :, :], ACT.Exp, scale=-1.0).then_inc(dt_act, 1)
                    features(0)
                    act.wait_ge(dts, 11 * b + 3)
                    act.activation(lnw[:, :, :], wdt[:, :, :], ACT.Ln).then_inc(dt_act, 1)
                    for f in range(1, NF):
                        features(f)
                    act.wait_ge(sums, 2 * b + 2)
                    act.activation(ecs[:, :, :], ps[:, bank_small, 8:16].rearrange("p (t h) -> p t h", h=2), ACT.Exp)
                    act.activation(etot[:, :, :], ps[:, bank_small, 16:24].rearrange("p (t h) -> p t h", h=2),
                                   ACT.Exp).then_inc(dt_act, 1)
                    act.wait_ge(dts, 11 * b + 10)
                    act.activation(dec0[:, :, :], dif[:, :, :], ACT.Exp).then_inc(dt_act, 1)
                    act.wait_ge(dd_done, 2 * TB * (b + 1))
                    act.activation(ee[:, :, :, :], dd[:, :, :, :], ACT.Exp).then_inc(ee_done, 1)
                    for i in range(2):
                        act.wait_ge(z_filled, 2 * b + i + 1)
                        act.activation(sz[:, 2 * i:2 * i + 2, :].rearrange("p t d -> p (t d)"), t_banks(i),
                                       ACT.Silu).then_inc(z_out, 1)
                    for f in range(NF):
                        if f == 2:
                            fill("z")
                        act.wait_ge(conv, 4 * (NF * b + f + 1))
                        act.activation(xc[:, f, :], ca[:, f % 2, :], ACT.Silu, bias=conv_b[:, f:f + 1]).then_inc(conv_out, 1)
                    act.wait_ge(ffn_low, 3)
                    for i, o in enumerate((xtm, btm)):
                        act.wait_ge(tm_filled, 2 * b + i + 1)
                        act.activation(o[:, :, :].rearrange("p t n -> p (t n)"), t_banks(i), ACT.Copy).then_inc(tm_out, 1)
                    fill("tm")
                    for c in range(TB):
                        if c > 0:
                            square(act, b, c - 1)
                        fill(c)
                    square(act, b, TB - 1)
                    fill("norm")
                    high(1, ht_h)
                    fill("out")
                    for t in range(TB):
                        act.wait_ge(h2_done, 2 * b + t // 2 + 1)
                        act.wait_ge(sq_done, AHEAD + 2 * TB * b + TB + t)
                        act.activation(sq[:, :], xh[:, t, :], ACT.Square, accum_out=ss[:, t:t + 1]).then_inc(sq_done, 1)
                    fill("norm2")
                    high(2, ft_h)

                rows(act, row, ffn_act)

            @block.vector
            def _(dve):
                dve.memset(cv[:, :, 0:3], 0.0).then_inc(set_up, 1)
                dve.wait_ge(set_up, 1)
                dve.wait_ge(proj.decay, 2)

                def row(b, fill):
                    dve.wait_ge(r2_done, AHEAD + b)
                    dve.tensor_copy(xb[:, :, :], X[:, bass.ds(TB * b, TB), :]).then_inc(xb_copied, 1)
                    dve.wait_ge(xb_copied, b + 1)
                    ln.run(dve, b, lambda t: xb[:, t, :])
                    fill("start")
                    at = 6 * b
                    dve.wait_ge(rstd_ready, b + 1)
                    dve.wait_ge(ln.done, ln.steps * (b + 1))
                    dve.tensor_scalar(var[:, :], ln.ve[:, :], -EPS, None, ALU.add).then_inc(pre, 1)
                    dve.tensor_tensor(rstd2[:, :], rstd[:, :], rstd[:, :], ALU.mult).then_inc(pre, 1)
                    dve.wait_ge(pre, at + 2)
                    dve.tensor_tensor(v2[:, :], var[:, :], rstd2[:, :], ALU.mult).then_inc(pre, 1)
                    dve.wait_ge(pre, at + 3)
                    dve.tensor_scalar(v2[:, :], v2[:, :], EPS, None, ALU.add).then_inc(pre, 1)
                    for t in range(TB):
                        ins = dve.tensor_scalar(xh[:, t, :], xb[:, t, :], ln.mean[:, t:t + 1], rstd[:, t:t + 1],
                                                ALU.subtract, ALU.mult)
                    ins.then_inc(pre, 1)
                    fill("scaled")
                    dve.wait_ge(r1_ready, b + 1)
                    dve.tensor_tensor(rr[:, :], rstd[:, :], r1[:, :], ALU.mult).then_inc(pre, 1)
                    dve.wait_ge(pre, at + 6)
                    for t in range(TB):
                        ins = dve.tensor_scalar(hn[:, t, :], xb[:, t, :], ln.mean[:, t:t + 1], rr[:, t:t + 1],
                                                ALU.subtract, ALU.mult)
                    ins.then_inc(hn_ready, 1)

                    def low(n, dst, high):
                        for k in range(KD):
                            dve.wait_ge(t_high, 6 * b + 2 * n + k + 1)
                            dve.tensor_tensor(dst[:, k, :], t_banks(k), high[:, k, :].bitcast(F32),
                                              ALU.subtract).then_inc(t_low, 1)

                    low(0, ht_l, ht_h)
                    fill("turned")
                    fill("dt")
                    d0 = 11 * b
                    dve.wait_ge(dt_filled, b + 1)
                    raw_dt = ps[:, bank_small, 0:8].rearrange("p (t h) -> p t h", h=2)
                    wide = (lambda v: v.unsqueeze(1).to_broadcast([P, TB, 2]))
                    dve.tensor_tensor(xdt[:, :, :], raw_dt, wide(heads[:, 0, :]), ALU.add).then_inc(dts, 1)
                    dve.wait_ge(dts, d0 + 1)
                    dve.tensor_scalar(mdt[:, :, :], xdt[:, :, :], 0.0, None, ALU.max)
                    dve.scalar_tensor_tensor(adt[:, :, :], xdt[:, :, :], -1.0, xdt[:, :, :], ALU.mult, ALU.max
                                             ).then_inc(dts, 1)
                    dve.wait_ge(dt_act, 4 * b + 1)
                    dve.tensor_scalar(wdt[:, :, :], udt[:, :, :], 1.0, None, ALU.add).then_inc(dts, 1)
                    dve.wait_ge(dts, d0 + 3)
                    dve.tensor_scalar(ddt[:, :, :], wdt[:, :, :], -1.0, None, ALU.add).then_inc(dts, 1)
                    dve.wait_ge(dts, d0 + 4)
                    dve.tensor_scalar(zdt[:, :, :], ddt[:, :, :], 0.0, None, ALU.is_equal).then_inc(dts, 1)
                    dve.wait_ge(dts, d0 + 5)
                    dve.tensor_tensor(t2[:, :, :], zdt[:, :, :], udt[:, :, :], ALU.mult)
                    dve.tensor_tensor(dden[:, :, :], zdt[:, :, :], ddt[:, :, :], ALU.add).then_inc(dts, 1)
                    dve.wait_ge(dts, d0 + 6)
                    dve.reciprocal(rden[:, :, :], dden[:, :, :]).then_inc(dts, 1)
                    dve.wait_ge(dts, d0 + 7)
                    dve.tensor_tensor(qdt[:, :, :], udt[:, :, :], rden[:, :, :], ALU.mult).then_inc(softplus, 1)
                    dve.wait_ge(softplus, 4 * b + 1)
                    dve.wait_ge(dt_act, 4 * b + 2)
                    dve.tensor_tensor(tdt[:, :, :], qdt[:, :, :], lnw[:, :, :], ALU.mult).then_inc(softplus, 1)
                    dve.wait_ge(softplus, 4 * b + 2)
                    dve.tensor_tensor(sdt[:, :, :], tdt[:, :, :], t2[:, :, :], ALU.add).then_inc(softplus, 1)
                    dve.wait_ge(softplus, 4 * b + 3)
                    dve.tensor_tensor(dt[:, :, :], sdt[:, :, :], mdt[:, :, :], ALU.add).then_inc(softplus, 1)
                    dve.wait_ge(softplus, 4 * b + 4)
                    dve.tensor_tensor(dA[:, :, :], dt[:, :, :], wide(neg_a[:, :]), ALU.mult).then_inc(dts, 1)
                    for f in range(NF):
                        dve.wait_ge(feat_out, NF * b + f + 1)
                        n = 4 * (NF * b + f)
                        if f >= 2:
                            dve.wait_ge(conv_out, AHEAD + NF * b + f - 1)
                        else:
                            dve.wait_ge(conv_out, AHEAD + NF * b)
                        dve.tensor_scalar(ca[:, f % 2, :], cv[:, f, 0:S], conv_w[:, f, 0:1], None,
                                          ALU.mult).then_inc(conv, 1)
                        for j in range(1, 4):
                            dve.wait_ge(conv, n + j)
                            dve.scalar_tensor_tensor(ca[:, f % 2, :], cv[:, f, j:j + S], conv_w[:, f, j:j + 1],
                                                     ca[:, f % 2, :], ALU.mult, ALU.add).then_inc(conv, 1)
                        if f == 0:
                            dve.wait_ge(dt_act, 4 * b + 3)
                            dve.tensor_copy(csum[:, :, :], ps[:, bank_small, 8:16].rearrange("p (t h) -> p t h", h=2)
                                            ).then_inc(dts, 1)
                            dve.wait_ge(dts, d0 + 9)
                            dve.tensor_tensor(dif[:, :, :], ps[:, bank_small, 16:24].rearrange("p (t h) -> p t h", h=2),
                                              csum[:, :, :], ALU.subtract).then_inc(dts, 1)
                            dve.wait_ge(row_done, b + 1)
                            for c in range(TB):
                                for h in range(2):
                                    at = P * (2 * (c % 2) + h)
                                    dve.scalar_tensor_tensor(dd[:, c, h, :], ps[:, bank_f[c // 2], at:at + P],
                                                             csum[:, c, h:h + 1], cap[:, :], ALU.subtract, ALU.min
                                                             ).then_inc(dd_done, 1)
                        if f == 1:
                            fill("z")
                    dve.wait_ge(dt_act, 4 * b + 4)
                    dve.tensor_tensor(dec[:, :, :], dec0[:, :, :], dt[:, :, :], ALU.mult).then_inc(dts, 1)
                    dve.wait_ge(dts, d0 + 11)
                    dve.wait_ge(tm_out, 2 * b + 2)
                    fill("tm")
                    dve.wait_ge(ee_done, b + 1)
                    for c in range(TB):
                        q = TB * b + c
                        dve.wait_ge(y_done, AHEAD + q)
                        for h in range(2):
                            dve.tensor_scalar(xd[:, h, :], xtm[:, c, :], dec[:, c, h:h + 1], None, ALU.mult)
                            ins = dve.tensor_scalar(t0[:, h, :], xtm[:, c, :], heads[:, 2, h:h + 1], None, ALU.mult)
                        ins.then_inc(xd_done, 1)
                        dve.wait_ge(g_done, q + 1)
                        for h in range(2):
                            ins = dve.scalar_tensor_tensor(mm[:, h, :], ps[:, bank_f[0], P * h:P * (h + 1)],
                                                           dt[:, c, h:h + 1], ee[:, c, h, :], ALU.mult, ALU.mult)
                        ins.then_inc(mm_done, 1)
                        if c < TB - 1:
                            dve.wait_ge(s_done, 3 * b + c + 1)
                            new, old = state[:, (c + 1) % 2], state[:, c % 2]
                            for h in range(2):
                                src = ps[:, bank_f[1], P * h:P * (h + 1)]
                                if c == 0:
                                    ins = dve.tensor_copy(new[:, h, :], src)
                                else:
                                    ins = dve.scalar_tensor_tensor(new[:, h, :], old[:, h, :], etot[:, c, h:h + 1], src,
                                                                   ALU.mult, ALU.add)
                            ins.then_inc(st_done, 1)
                        fill(c)
                        dve.wait_ge(y_done, AHEAD + q + 1)
                        dve.wait_ge(xd_done, q + 1)
                        yd = t_banks(c % 2)[:, 0:2 * P]
                        flat = (lambda v: v[:, :, :].rearrange("p h n -> p (h n)"))
                        if c > 0:
                            for h in range(2):
                                ins = dve.scalar_tensor_tensor(y1[:, h, :], t_banks(c % 2)[:, P * (2 + h):P * (3 + h)],
                                                               ecs[:, c, h:h + 1], t0[:, h, :], ALU.mult, ALU.add)
                            ins.then_inc(ys, 1)
                            dve.wait_ge(ys, 7 * b + 2 * c)
                            dve.tensor_tensor(flat(y2), yd, flat(y1), ALU.add).then_inc(ys, 1)
                            dve.wait_ge(ys, 7 * b + 2 * c + 1)
                        else:
                            dve.tensor_tensor(flat(y2), yd, flat(t0), ALU.add).then_inc(ys, 1)
                            dve.wait_ge(ys, 7 * b + 1)
                        dve.tensor_tensor(yg[:, c, :], flat(y2), sz[:, c, :], ALU.mult).then_inc(yg_done, 1)

                    def norm(i, src, dst):
                        dve.wait_ge(sq_done, AHEAD + 2 * TB * b + TB * (i + 1))
                        dve.tensor_scalar(ms[:, :], ss[:, :], 1.0 / D, EPS, ALU.mult, ALU.add).then_inc(norm_v, 1)
                        fill(("norm", "norm2")[i])
                        dve.wait_ge(rq_ready, 2 * b + i + 1)
                        for t in range(TB):
                            ins = dve.tensor_scalar(dst[:, t, :], src[:, t, :], rq[:, t:t + 1], None, ALU.mult)
                        ins.then_inc(hn_ready, 1)

                    norm(0, yg, hn)
                    low(1, ht_l, ht_h)
                    fill("out")
                    for i in range(2):
                        dve.wait_ge(o_done, 2 * b + i + 1)
                        v = xh[:, 2 * i:2 * i + 2, :].rearrange("p t d -> p (t d)")
                        dve.tensor_tensor(v, ps[:, bank_f[i], :], v, ALU.add).then_inc(h2_done, 1)
                    norm(1, xh, hn)
                    low(2, ft_l, ft_h)

                rows(dve, row, ffn_dve)

            @block.tensor
            def _(pe):
                pe.wait_ge(proj.low, 2)
                pe.wait_ge(set_up, 1)

                def row(b, fill):

                    def transposes(n):
                        pe.wait_ge(hn_ready, 3 * b + n + 1)
                        for k in range(KD):
                            for t in range(TB):
                                ins = pe.transpose(t_banks(k)[:, P * t:P * (t + 1)], hn[:, t, P * k:P * (k + 1)],
                                                   ident[:, :])
                            ins.then_inc(t_filled, 1)

                    rows_of = (lambda k, at: (ht_h[:, k, at:at + P], ht_l[:, k, at:at + P]))
                    cols = (lambda w, k, lo, hi: (w[0][:, k, lo:hi], w[1][:, k, lo:hi]))
                    fill("start")
                    fill("scaled")
                    transposes(0)
                    fill("turned")
                    pe.wait_ge(t_low, 6 * b + 2)
                    for t in range(TB):
                        for k in range(KD):
                            ins = product(pe, ps[:, bank_small, 2 * t:2 * t + 2], rows_of(k, P * t),
                                          cols(win, k, PROJ - 2, PROJ), k == 0, k == KD - 1)
                    ins.then_inc(dt_filled, 1)
                    fill("dt")
                    for f in range(NF):
                        if f >= 2:
                            pe.wait_ge(feat_out, NF * b + f - 1)
                        for k in range(KD):
                            at = D + P * f
                            ins = product(pe, ps[:, bank_f[f % 2], :], cols(win, k, at, at + P),
                                          (ht_h[:, k, :], ht_l[:, k, :]), k == 0, k == KD - 1)
                        ins.then_inc(feat, 1)
                    pe.wait_ge(dts, 11 * b + 8)
                    flat = dA[:, :, :].rearrange("p t h -> p (t h)")
                    pe.matmul(ps[:, bank_small, 8:16], upper, flat, start=True, stop=True).then_inc(sums, 1)
                    pe.matmul(ps[:, bank_small, 16:24], ones, flat, start=True, stop=True).then_inc(sums, 1)
                    pe.wait_ge(feat_out, NF * (b + 1))
                    for c in range(TB):
                        for h in range(2):
                            at = P * (2 * (c % 2) + h)
                            ins = pe.matmul(ps[:, bank_f[c // 2], at:at + P], dA[:, c, h:h + 1].to_broadcast([P, P]),
                                            upper, start=True, stop=True)
                    ins.then_inc(row_done, 1)
                    for i in range(2):
                        for t in range(2):
                            for k in range(KD):
                                ins = product(pe, t_banks(i)[:, D * t:D * (t + 1)], rows_of(k, P * (2 * i + t)),
                                              cols(win, k, 0, D), k == 0, k == KD - 1)
                        ins.then_inc(z_filled, 1)
                    fill("z")
                    for i in range(2):
                        pe.wait_ge(z_out, 2 * b + i + 1)
                        pe.wait_ge(conv_out, AHEAD + NF * b + i + 1)
                        for t in range(TB):
                            ins = pe.transpose(t_banks(i)[:, P * t:P * (t + 1)], xc[:, i, P * t:P * (t + 1)], ident[:, :])
                        ins.then_inc(tm_filled, 1)
                    fill("tm")
                    pe.wait_ge(conv_out, AHEAD + NF * (b + 1))
                    pe.wait_ge(dd_done, 2 * TB * (b + 1))
                    pe.wait_ge(tm_out, 2 * (b + 1))
                    for c in range(TB):
                        q = TB * b + c
                        ch = slice(P * c, P * (c + 1))
                        if c > 0:
                            pe.wait_ge(mm_done, q)
                        pe.matmul(ps[:, bank_f[0], 0:2 * P], xc[:, 1, ch], xc[:, 2:4, ch], start=True,
                                  stop=True).then_inc(g_done, 1)
                        if c >= 2:
                            pe.wait_ge(yg_done, q - 1)
                        if c > 0:
                            pe.wait_ge(st_done, 3 * b + c)
                            for h in range(2):
                                pe.matmul(t_banks(c % 2)[:, P * (2 + h):P * (3 + h)], xc[:, 2 + h, ch],
                                          state[:, c % 2, h, :], start=True, stop=True)
                        if c < TB - 1:
                            pe.wait_ge(xd_done, q + 1)
                            pe.matmul(ps[:, bank_f[1], 0:2 * P], btm[:, c, :], xd[:, :, :], start=True,
                                      stop=True).then_inc(s_done, 1)
                        fill(c)
                        pe.wait_ge(mm_done, q + 1)
                        for h in range(2):
                            ins = pe.matmul(t_banks(c % 2)[:, P * h:P * (h + 1)], mm[:, h, :], xtm[:, c, :], start=True,
                                            stop=True)
                        ins.then_inc(y_done, 1)
                    fill("norm")
                    transposes(1)
                    pe.wait_ge(t_low, 6 * b + 4)
                    pe.wait_ge(mm_done, TB * (b + 1))
                    for i in range(2):
                        for t in range(2):
                            for k in range(KD):
                                ins = product(pe, ps[:, bank_f[i], D * t:D * (t + 1)], rows_of(k, P * (2 * i + t)),
                                              cols(wout, k, 0, D), k == 0, k == KD - 1)
                        ins.then_inc(o_done, 1)
                    fill("out")
                    fill("norm2")
                    transposes(2)

                rows(pe, row, ffn_pe)

        m.close()


def build(nc, a, out):
    with ExitStack() as ctx:
        m = Memory(nc, ctx, "all")
        X = m.sb("x", [P, TILES, D])
        banks = ctx.enter_context(nc.psum_tensor("banks", [P, 8, S], F32))
        ident = m.sb("ident", [P, P])
        upper, ones = m.sb("upper", [P, P]), m.sb("ones", [P, P])
        rank, first_slot = m.sb("rank", [P, TB, E]), m.sb("first_slot", [P, TB, E])
        zero_rows = m.sb("zero_rows", [P, D])
        loaded, stored, zeroed, zero_set = m.sem("loaded"), m.sem("stored"), m.sem("zeroed"), m.sem("zero_set")
        xd = [nc.dram_tensor(f"dispatched{i}", (E * C, D), F32, kind="Internal").ap() for i in range(2)]
        oe = [nc.dram_tensor(f"expert_rows{i}", (E * C, D), F32, kind="Internal").ap() for i in range(2)]
        consts = (upper[:, :], ones[:, :], rank[:, :, :], first_slot[:, :, :])
        with nc.Block() as block:

            @block.sync
            def _(sp):
                sp.dma_start(ident[:, :], a["ident"]).then_inc(loaded, 16)
                sp.dma_start(upper[:, :], a["upper"]).then_inc(loaded, 16)
                sp.dma_start(ones[:, :], a["ones"]).then_inc(loaded, 16)
                sp.dma_start(rank[:, :, :], a["rank"]).then_inc(loaded, 16)
                sp.dma_start(first_slot[:, :, :], a["first_slot"]).then_inc(loaded, 16)
                sp.wait_ge(zero_set, 1)

            @block.vector
            def _(dve):
                dve.memset(zero_rows[:, :], 0.0).then_inc(zero_set, 1)

        attention_stage(nc, a["x"], a["wqkv"], a["wo"], a["rope"], X, ident, banks, xd, zero_rows, zeroed,
                        loaded, 16 * 5)
        expert_weights = (a["w13"], a["w2a"], a["w2b"], a["wg"])
        with ExitStack() as held:
            proj = Projections(nc, held, a)
            experts_stage(nc, "moe1", *expert_weights, X, ident, consts, xd[0], oe[0], banks, zeroed, 1, ahead=proj)
            state_space_stage(nc, X, ident, consts, banks, proj)
        experts_stage(nc, "moe2", *expert_weights, X, ident, consts, xd[1], oe[1], banks, zeroed, 2, out=out,
                      stored=stored)


def layout(inputs):
    g = {k.removeprefix("L0_"): np.asarray(v) for k, v in inputs.items()}
    arrays = {"x": g["attn_a_x"]}
    heads = [2 * (2 * m + half) + r for m in range(NKV // 2) for r in range(2) for half in range(2)]
    halves = [d for p in range(2) for d in range(p, HD, 2)]
    qcols = [HD * h + d for h in heads for d in halves]
    kcols = [HD * j + d for j in range(NKV) for d in halves]
    arrays["wqkv"] = np.concatenate([g["attn_a_wq"][:, qcols], g["attn_a_wk"][:, kcols], g["attn_a_wv"]], axis=1)
    arrays["wo"] = g["attn_a_wo"]
    f = np.float32
    inv = f(1.0) / (f(10000.0) ** (np.arange(0, HD, 2, dtype=f) / f(HD)))
    ang = np.arange(S, dtype=f)[:, None] * inv[None, :]
    arrays["rope"] = np.stack([np.tile(np.cos(ang), 2), np.tile(np.sin(ang), 2)], axis=1).astype(f)
    arrays["ident"] = np.eye(P, dtype=f)
    arrays["upper"] = np.triu(np.ones((P, P), f))
    arrays["ones"] = np.ones((P, P), f)
    arrays["rank"] = np.broadcast_to(np.arange(E, 0, -1, dtype=f), (P, TB, E))
    arrays["first_slot"] = np.broadcast_to(np.arange(E, dtype=f) * C - 1, (P, TB, E))
    w1 = np.concatenate([g["ffn_W1"], g["ffn_sw1"][None]]).reshape(E + 1, KD, P, H)
    w3 = np.concatenate([g["ffn_W3"], g["ffn_sw3"][None]]).reshape(E + 1, KD, P, H)
    w2 = np.concatenate([g["ffn_W2"], g["ffn_sw2"][None]])
    arrays["w13"] = np.stack([w1, w3], axis=3).transpose(0, 2, 1, 3, 4).reshape(E + 1, P, 2 * KD * H)
    arrays["w2a"] = w2[:, :2 * P].reshape(E + 1, 2, P, D).transpose(0, 2, 1, 3).reshape(E + 1, P, 2 * D)
    arrays["w2b"] = w2[:, 2 * P:]
    arrays["wg"] = g["ffn_Wg"]
    arrays["win"], arrays["wout"] = g["attn_b_W_in"], g["attn_b_W_out"]
    arrays["w1"], arrays["w3"], arrays["w2"] = g["attn_b_w1"], g["attn_b_w3"], g["attn_b_w2"]
    arrays["norms"] = np.stack([g["attn_b_ln1_w"], g["attn_b_norm_w"], g["attn_b_ln2_w"]]
                               ).reshape(3, KD, P).transpose(2, 0, 1)
    arrays["conv_w"] = g["attn_b_conv_w"].reshape(4, 4, P).transpose(2, 1, 0)
    arrays["conv_b"] = g["attn_b_conv_b"].reshape(4, P).T
    arrays["heads"] = np.concatenate([g["attn_b_dt_bias"], g["attn_b_A_log"], g["attn_b_D"]])
    arrays["cap"] = np.tril(np.full((P, P), -1e30, f), -1)
    return {k: np.ascontiguousarray(v) for k, v in arrays.items()}


def kernel(**inputs):
    import concourse.bacc as bacc
    from concourse.bass_utils import run_bass_kernel_spmd

    nc = bacc.Bacc("TRN2", target_bir_lowering=False, num_devices=1)
    arrays = layout(inputs)
    aps = {k: nc.dram_tensor(f"in_{k}", v.shape, mybir.dt.from_np(v.dtype), kind="ExternalInput").ap()
           for k, v in arrays.items()}
    out = nc.dram_tensor("out_x", (B, S, D), F32, kind="ExternalOutput").ap()
    build(nc, aps, out)
    r = run_bass_kernel_spmd(nc, [{f"in_{k}": v for k, v in arrays.items()}], core_ids=[0])
    return r.results[0]["out_x"]
```
